# Optimizing a Trainium2 kernel written in Bass

```python
import numpy as np
import jax
import jax.numpy as jnp

def _softmax(x, axis=-1):
    return jax.nn.softmax(x, axis=axis)

def _gelu(x):
    return jax.nn.gelu(x, approximate=True)

def _silu(x):
    return jax.nn.silu(x)

def _sigmoid(x):
    return jax.nn.sigmoid(x)

def _layernorm(x, axis=-1, eps=1e-05):
    m = jnp.mean(x, axis=axis, keepdims=True)
    v = jnp.var(x, axis=axis, keepdims=True)
    return (x - m) / jnp.sqrt(v + eps)

def _scatter_add(tgt, idx, src, axis=0):
    return tgt.at[idx].add(src)

def _segment_sum(src, seg, n):
    return jax.ops.segment_sum(src, seg, n)
kernel_name = 'mk_sandwich_d1_jaxref_r8_cdfd6c'

def setup_inputs(seed: int=0):
    np.random.seed(seed)
    _w = jnp.asarray

    def _L0_attn_setup():
        import jax, jax.numpy as jnp
        import numpy as np
        B, S, H = (2, 512, 256)
        HK = HV = 16
        DK = DV = 128
        KC = 4
        CH = 64

        def l2norm(x, eps=1e-06):
            return x * jax.lax.rsqrt(jnp.sum(x * x, axis=-1, keepdims=True) + eps)

        def gated_rmsnorm(x, gate, weight, eps=1e-06):
            xf = x.astype(jnp.float32)
            var = jnp.mean(xf * xf, axis=-1, keepdims=True)
            xn = weight * (xf * jax.lax.rsqrt(var + eps))
            return xn * jax.nn.silu(gate.astype(jnp.float32))

        def chunk_gated_delta_rule(q, k, v, g, beta):
            q = l2norm(q)
            k = l2norm(k)
            tr = lambda x: jnp.transpose(x, (0, 2, 1, 3)).astype(jnp.float32)
            q, k, v = (tr(q), tr(k), tr(v))
            g = jnp.transpose(g, (0, 2, 1)).astype(jnp.float32)
            beta = jnp.transpose(beta, (0, 2, 1)).astype(jnp.float32)
            b, h, s, dk = k.shape
            dv = v.shape[-1]
            n = s // CH
            q = q * dk ** (-0.5)
            v_beta = v * beta[..., None]
            k_beta = k * beta[..., None]
            cs = lambda x: x.reshape(b, h, n, CH, x.shape[-1])
            q, k, v_beta, k_beta = (cs(q), cs(k), cs(v_beta), cs(k_beta))
            gc = jnp.cumsum(g.reshape(b, h, n, CH), axis=-1)
            idx = jnp.arange(CH)
            lower_incl = idx[:, None] >= idx[None, :]
            strict_lower = idx[:, None] > idx[None, :]
            decay = jnp.where(lower_incl, jnp.exp(gc[..., :, None] - gc[..., None, :]), 0.0)
            Tm = -jnp.einsum('bhnik,bhnjk->bhnij', k_beta, k) * decay
            Tm = jnp.where(strict_lower, Tm, 0.0)
            eye = jnp.eye(CH, dtype=jnp.float32)
            inv = jax.scipy.linalg.solve_triangular(eye - Tm, jnp.broadcast_to(eye, Tm.shape), lower=True, unit_diagonal=True)
            u = jnp.einsum('bhnij,bhnjd->bhnid', inv, v_beta)
            w = jnp.einsum('bhnij,bhnjd->bhnid', inv, k_beta * jnp.exp(gc)[..., None])

            def step(S0, xs):
                q_i, k_i, u_i, w_i, gc_i = xs
                dec = jnp.where(lower_incl, jnp.exp(gc_i[..., :, None] - gc_i[..., None, :]), 0.0)
                attn = jnp.where(lower_incl, jnp.einsum('bhik,bhjk->bhij', q_i, k_i) * dec, 0.0)
                v_new = u_i - jnp.einsum('bhik,bhkd->bhid', w_i, S0)
                inter = jnp.einsum('bhik,bhkd->bhid', q_i * jnp.exp(gc_i)[..., None], S0)
                out_i = inter + jnp.einsum('bhij,bhjd->bhid', attn, v_new)
                g_last = gc_i[..., -1]
                k_dec = k_i * jnp.exp(g_last[..., None] - gc_i)[..., None]
                S1 = S0 * jnp.exp(g_last)[..., None, None] + jnp.einsum('bhik,bhid->bhkd', k_dec, v_new)
                return (S1, out_i)
            S0 = jnp.zeros((b, h, dk, dv), jnp.float32)
            xs = tuple((jnp.moveaxis(x, 2, 0) for x in (q, k, u, w, gc)))
            _, out = jax.lax.scan(step, S0, xs)
            out = jnp.moveaxis(out, 0, 2).reshape(b, h, s, dv)
            return jnp.transpose(out, (0, 2, 1, 3))
        key = jax.random.key(seed)
        ks = jax.random.split(key, 8)
        qkvz_dim = HK * 2 * DK + HV * 2 * DV
        conv_dim = 2 * HK * DK + HV * DV
        return {'hidden_states': jax.random.normal(ks[0], (B, S, H), jnp.float32), 'W_qkvz': jax.random.normal(ks[1], (H, qkvz_dim), jnp.float32) / np.sqrt(H), 'W_ba': jax.random.normal(ks[2], (H, HV * 2), jnp.float32) / np.sqrt(H), 'conv_weight': jax.random.normal(ks[3], (conv_dim, KC), jnp.float32) * 0.1, 'dt_bias': jax.random.normal(ks[4], (HV,), jnp.float32) * 0.1, 'A_log': jnp.log(jax.random.uniform(ks[5], (HV,), jnp.float32, 1.0, 8.0)), 'norm_weight': jnp.ones((DV,), jnp.float32), 'W_out': jax.random.normal(ks[6], (HV * DV, H), jnp.float32) / np.sqrt(HV * DV)}
    _L0_attn_in = _L0_attn_setup()

    def _L0_ffn_setup():
        import jax, jax.numpy as jnp
        import numpy as np
        D_MODEL = 256
        D_EXPERT = 1024
        EPS = 1e-08

        def ternary_quant(w):
            scale = jnp.mean(jnp.abs(w)) + EPS
            q = jnp.clip(jnp.round(w / scale), -1.0, 1.0) * scale
            return w + jax.lax.stop_gradient(q - w)
        key = jax.random.key(seed)
        k_x, k_up, k_gate, k_down = jax.random.split(key, 4)
        std_in = 1.0 / np.sqrt(D_MODEL)
        std_exp = 1.0 / np.sqrt(D_EXPERT)
        return {'x': jax.random.normal(k_x, (4, 256, D_MODEL), dtype=jnp.float32), 'W_up': jax.random.normal(k_up, (D_EXPERT, D_MODEL), dtype=jnp.float32) * std_in, 'W_gate': jax.random.normal(k_gate, (D_EXPERT, D_MODEL), dtype=jnp.float32) * std_in, 'W_down': jax.random.normal(k_down, (D_MODEL, D_EXPERT), dtype=jnp.float32) * std_exp}
    _L0_ffn_in = _L0_ffn_setup()
    _d = {'L0_attn_hidden_states': _L0_attn_in['hidden_states'], 'L0_attn_W_qkvz': _L0_attn_in['W_qkvz'], 'L0_attn_W_ba': _L0_attn_in['W_ba'], 'L0_attn_conv_weight': _L0_attn_in['conv_weight'], 'L0_attn_dt_bias': _L0_attn_in['dt_bias'], 'L0_attn_A_log': _L0_attn_in['A_log'], 'L0_attn_norm_weight': _L0_attn_in['norm_weight'], 'L0_attn_W_out': _L0_attn_in['W_out'], 'L0_ffn_W_up': _L0_ffn_in['W_up'], 'L0_ffn_W_gate': _L0_ffn_in['W_gate'], 'L0_ffn_W_down': _L0_ffn_in['W_down']}
    _x0 = _d['L0_attn_hidden_states']
    _d['L0_attn_hidden_states'] = jax.random.normal(jax.random.fold_in(jax.random.key(seed), 1), (4, 256, 256), dtype=_x0.dtype)
    del _x0
    return _d

def reference(L0_attn_hidden_states, L0_attn_W_qkvz, L0_attn_W_ba, L0_attn_conv_weight, L0_attn_dt_bias, L0_attn_A_log, L0_attn_norm_weight, L0_attn_W_out, L0_ffn_W_up, L0_ffn_W_gate, L0_ffn_W_down):

    def _L0_attn_ref(hidden_states, W_qkvz, W_ba, conv_weight, dt_bias, A_log, norm_weight, W_out):
        import jax, jax.numpy as jnp
        import numpy as np
        B, S, H = (2, 512, 256)
        HK = HV = 16
        DK = DV = 128
        KC = 4
        CH = 64

        def l2norm(x, eps=1e-06):
            return x * jax.lax.rsqrt(jnp.sum(x * x, axis=-1, keepdims=True) + eps)

        def gated_rmsnorm(x, gate, weight, eps=1e-06):
            xf = x.astype(jnp.float32)
            var = jnp.mean(xf * xf, axis=-1, keepdims=True)
            xn = weight * (xf * jax.lax.rsqrt(var + eps))
            return xn * jax.nn.silu(gate.astype(jnp.float32))

        def chunk_gated_delta_rule(q, k, v, g, beta):
            q = l2norm(q)
            k = l2norm(k)
            tr = lambda x: jnp.transpose(x, (0, 2, 1, 3)).astype(jnp.float32)
            q, k, v = (tr(q), tr(k), tr(v))
            g = jnp.transpose(g, (0, 2, 1)).astype(jnp.float32)
            beta = jnp.transpose(beta, (0, 2, 1)).astype(jnp.float32)
            b, h, s, dk = k.shape
            dv = v.shape[-1]
            n = s // CH
            q = q * dk ** (-0.5)
            v_beta = v * beta[..., None]
            k_beta = k * beta[..., None]
            cs = lambda x: x.reshape(b, h, n, CH, x.shape[-1])
            q, k, v_beta, k_beta = (cs(q), cs(k), cs(v_beta), cs(k_beta))
            gc = jnp.cumsum(g.reshape(b, h, n, CH), axis=-1)
            idx = jnp.arange(CH)
            lower_incl = idx[:, None] >= idx[None, :]
            strict_lower = idx[:, None] > idx[None, :]
            decay = jnp.where(lower_incl, jnp.exp(gc[..., :, None] - gc[..., None, :]), 0.0)
            Tm = -jnp.einsum('bhnik,bhnjk->bhnij', k_beta, k) * decay
            Tm = jnp.where(strict_lower, Tm, 0.0)
            eye = jnp.eye(CH, dtype=jnp.float32)
            inv = jax.scipy.linalg.solve_triangular(eye - Tm, jnp.broadcast_to(eye, Tm.shape), lower=True, unit_diagonal=True)
            u = jnp.einsum('bhnij,bhnjd->bhnid', inv, v_beta)
            w = jnp.einsum('bhnij,bhnjd->bhnid', inv, k_beta * jnp.exp(gc)[..., None])

            def step(S0, xs):
                q_i, k_i, u_i, w_i, gc_i = xs
                dec = jnp.where(lower_incl, jnp.exp(gc_i[..., :, None] - gc_i[..., None, :]), 0.0)
                attn = jnp.where(lower_incl, jnp.einsum('bhik,bhjk->bhij', q_i, k_i) * dec, 0.0)
                v_new = u_i - jnp.einsum('bhik,bhkd->bhid', w_i, S0)
                inter = jnp.einsum('bhik,bhkd->bhid', q_i * jnp.exp(gc_i)[..., None], S0)
                out_i = inter + jnp.einsum('bhij,bhjd->bhid', attn, v_new)
                g_last = gc_i[..., -1]
                k_dec = k_i * jnp.exp(g_last[..., None] - gc_i)[..., None]
                S1 = S0 * jnp.exp(g_last)[..., None, None] + jnp.einsum('bhik,bhid->bhkd', k_dec, v_new)
                return (S1, out_i)
            S0 = jnp.zeros((b, h, dk, dv), jnp.float32)
            xs = tuple((jnp.moveaxis(x, 2, 0) for x in (q, k, u, w, gc)))
            _, out = jax.lax.scan(step, S0, xs)
            out = jnp.moveaxis(out, 0, 2).reshape(b, h, s, dv)
            return jnp.transpose(out, (0, 2, 1, 3))
        b, s, _ = hidden_states.shape
        qkvz = (hidden_states @ W_qkvz).reshape(b, s, HK, 2 * DK + 2 * DV)
        q, k, v, z = jnp.split(qkvz, [DK, 2 * DK, 2 * DK + DV], axis=-1)
        ba = (hidden_states @ W_ba).reshape(b, s, HK, 2)
        b_gate, a = (ba[..., 0], ba[..., 1])
        mixed = jnp.concatenate([q.reshape(b, s, -1), k.reshape(b, s, -1), v.reshape(b, s, -1)], axis=-1)
        x = jnp.transpose(mixed, (0, 2, 1))
        x = jnp.pad(x, ((0, 0), (0, 0), (KC - 1, 0)))
        y = jax.lax.conv_general_dilated(x, conv_weight[:, None, :], (1,), 'VALID', dimension_numbers=('NCH', 'OIH', 'NCH'), feature_group_count=conv_weight.shape[0])
        y = jnp.transpose(jax.nn.silu(y), (0, 2, 1))
        qd = HK * DK
        qh = y[..., :qd].reshape(b, s, HK, DK)
        kh = y[..., qd:2 * qd].reshape(b, s, HK, DK)
        vh = y[..., 2 * qd:].reshape(b, s, HV, DV)
        beta = jax.nn.sigmoid(b_gate)
        g = -jnp.exp(A_log) * jax.nn.softplus(a + dt_bias)
        core = chunk_gated_delta_rule(qh, kh, vh, g, beta)
        core = gated_rmsnorm(core, z, norm_weight)
        return core.reshape(b, s, HV * DV) @ W_out

    def _L0_ffn_ref(x, W_up, W_gate, W_down):
        import jax, jax.numpy as jnp
        import numpy as np
        D_MODEL = 256
        D_EXPERT = 1024
        EPS = 1e-08

        def ternary_quant(w):
            scale = jnp.mean(jnp.abs(w)) + EPS
            q = jnp.clip(jnp.round(w / scale), -1.0, 1.0) * scale
            return w + jax.lax.stop_gradient(q - w)
        wu = ternary_quant(W_up)
        wg = ternary_quant(W_gate)
        wd = ternary_quant(W_down)
        up = jnp.einsum('bsd,ed->bse', x, wu)
        gate = jnp.einsum('bsd,ed->bse', x, wg)
        hidden = jax.nn.silu(up) * gate
        return jnp.einsum('bse,de->bsd', hidden, wd)
    x = L0_attn_hidden_states
    x = x + _layernorm(_L0_attn_ref(_layernorm(x, axis=-1), L0_attn_W_qkvz, L0_attn_W_ba, L0_attn_conv_weight, L0_attn_dt_bias, L0_attn_A_log, L0_attn_norm_weight, L0_attn_W_out), axis=-1)
    x = x + _layernorm(_L0_ffn_ref(_layernorm(x, axis=-1), L0_ffn_W_up, L0_ffn_W_gate, L0_ffn_W_down), axis=-1)
    return x

_drawn_inputs = setup_inputs


def setup_inputs(seed=0):
    import zlib

    import numpy as np

    out = dict(_drawn_inputs(seed))
    spreads = {'L0_attn_norm_weight': (1.0, 0.2)}
    factors = {'L0_attn_dt_bias': 3.222}
    for name, (base, spread) in spreads.items():
        noise = np.random.default_rng([zlib.crc32(name.encode()), seed]).standard_normal(out[name].shape)
        drawn = base * np.exp(spread * noise) if base else spread * noise
        out[name] = jnp.asarray(drawn.astype(out[name].dtype))
    for name, factor in factors.items():
        out[name] = (out[name] * factor).astype(out[name].dtype)
    return out
```

```python
from contextlib import ExitStack

import concourse.bass as bass
from concourse import mybir

F32 = mybir.dt.float32
ALU = mybir.AluOpType
ACT = mybir.ActivationFunctionType
AX = mybir.AxisListType

P = 128
T, D = 1024, 256
KT = D // P
NH, DH = 16, 128
NU = T // P
SEG = 256
NP = NH // 2
NB16 = P // 16
E = 1024
ET = E // P
LN_EPS, L2_EPS, RMS_EPS, Q_EPS = 1e-5, 1e-6, 1e-6, 1e-8

K_, Q_, V_ = 0, 1, 2
W_COL = {K_: DH, Q_: 0, V_: 2 * DH}
CONV_S = {K_: 1, Q_: 0, V_: 2}

PREP = {}
for g in range(4):
    PREP["kT", g] = 2 * g
    PREP["qT", g] = 2 * g + 1
    PREP["gram", g, 0] = 8 + 2 * g
    PREP["gram", g, 1] = 9 + 2 * g
    PREP["vT", g] = 16 + g
    PREP["z", g] = 20 + g
SOLVE = {}
for g in range(4):
    for lv in range(2):
        SOLVE["LM", lv, g] = 12 * lv + g
        SOLVE["MY", lv, g] = 12 * lv + 4 + 2 * g
        SOLVE["YX", lv, g] = 12 * lv + 5 + 2 * g
    SOLVE["LM", 2, g] = 24 + g
    SOLVE["MY", 2, g] = 28 + g
for h in range(2):
    for at, name in ((32, "y_even"), (34, "state"), (36, "kS"), (38, "o_even"), (40, "y_odd"),
                     (42, "o_odd"), (44, "oT_even"), (46, "out_even"), (48, "oT_odd"), (50, "out_odd")):
        SOLVE[name, h] = at + h
N_PREP, N_SOLVE = len(PREP), len(SOLVE)
N_TURNS = N_PREP + N_SOLVE
assert N_PREP % 4 == 0 and N_SOLVE % 4 == 0


def turn_of(phase, key):
    return (PREP if phase == "prep" else SOLVE)[key]


def bank_of(phase, key):
    return turn_of(phase, key) % 4


def filled_at(phase, n, key):
    return n * N_TURNS + ((0 if phase == "prep" else N_PREP) + turn_of(phase, key) + 1)


def before(phase, n, key):
    t = turn_of(phase, key) - 4
    if t < 0 and phase == "prep":
        phase, n, t = "solve", n - 1, t + N_SOLVE
        if isinstance(n, int) and n < 0:
            return None
    elif t < 0:
        phase, t = "prep", t + N_PREP
    table = PREP if phase == "prep" else SOLVE
    return phase, n, next(k for k, v in table.items() if v == t)


def tap_at(n, turn, tap):
    return n * 36 + (6 * (turn // 2) + 2 * tap + turn % 2 + 1)


def wait(eng, sem, value):
    if isinstance(value, int) and value <= 0:
        return
    eng.wait_ge(sem, value)


def m_blocks(lv):
    s = 16 << lv
    return [(a, a + s, a + s, a + 2 * s) for a in range(0, P, 2 * s)]


def x_blocks(lv):
    s = 16 << lv
    if s == 16:
        return [(a, a + 32, a, a + 16) for a in range(0, P, 32)]
    return [(a + s, a + 2 * s, a, a + s) for a in range(0, P, 2 * s)]


N_INV = 31
N_PREP_STEP = 4 * 2


def sandwich(nc, x, W_qkvz, W_ba, conv_w, dt_bias, A_log, norm_w, W_out, W_up, W_gate, W_down, out):
    x_t = x.rearrange("b s d -> (b s) d").rearrange("(u p) d -> p u d", p=P)
    out_t = out.rearrange("b s d -> (b s) d").rearrange("(u p) d -> p u d", p=P)
    wq_d = W_qkvz.rearrange("(k p) (n h c) -> n p k h c", p=P, n=NP, h=2)
    wout_d = W_out.rearrange("(n h p) d -> n p h d", n=NP, h=2)
    conv_d = conv_w.rearrange("(s n h p) t -> n p s h t", s=3, n=NP, h=2)
    gc_d = nc.dram_tensor("gc_rows", (NH, T), F32, kind="Internal").ap()
    blk_out_d = nc.dram_tensor("l_blocks", (2 * NU, NB16, 16, 16), F32, kind="Internal").ap()
    blk_in_d = nc.dram_tensor("x_blocks", (2 * NU, NB16, 2, 16, 16), F32, kind="Internal").ap()

    with ExitStack() as ctx:
        def sb(name, shape):
            return ctx.enter_context(nc.sbuf_tensor(name, shape, F32))

        def sem(name):
            return ctx.enter_context(nc.semaphore(name))

        x_sb = sb("x_sb", [P, NU, D])
        xnT = sb("xnT", [P, KT, T])
        attn_out = sb("attn_out", [P, NU, D])
        ident = sb("ident", [P, P])
        strict = sb("strict", [P, P])
        upper = sb("upper", [P, P])
        ones = sb("ones", [P, P])
        w_qkv = sb("w_qkv", [P, KT, 2, 3 * DH])
        w_z = sb("w_z", [P, KT, 2, DH])
        w_conv = sb("w_conv", [P, 3, 2, 4])
        w_o = sb("w_o", [P, 2, D])
        nw = sb("nw", [P, 1])
        wba = sb("wba", [P, KT, 2 * NH])
        alog = sb("alog", [NH, 1])
        dtb = sb("dtb", [NH, 1])
        conv = sb("conv", [P, 4, 512])
        chan = sb("chan", [P, 2, 3, T])
        decays = sb("decays", [P, 3, 2 * T])
        gcb = decays[:, 0, :].rearrange("p (h t) -> p h t", h=2)
        Wd = decays[:, 1, :].rearrange("p (u t) -> p u t", t=P)
        Wi = decays[:, 2, :].rearrange("p (u t) -> p u t", t=P)
        cols_all = sb("cols_all", [P, NH, 3, NU])
        cols = sb("cols", [P, 2, 3, NU])
        eg = sb("eg", [P, 2, 4, P])
        sq = sb("sq", [P, 4, 512])
        ss = sb("ss", [P, 16])
        sst = sb("sst", [P, 16])
        rt = sb("rt", [P, 16])
        rs = sb("rs", [P, 16])
        negc = sb("negc", [P, 16])
        fk = sb("fk", [P, 16])
        ssq = sb("ssq", [P, 16])
        qe = sb("qe", [P, 16])
        zs = sb("zs", [P, 16, P])
        kd = sb("kd", [P, 2, 4, P])
        kp = sb("kp", [P, 2, 4, P])
        qp = sb("qp", [P, 2, 4, P])
        vt = sb("vt", [P, 16, P])
        Lneg = sb("Lneg", [P, 16, P])
        attnT = sb("attnT", [P, 16, P])
        lb = sb("lb", [P, 16, 16])
        xm = sb("xm", [P, 2, 16, 16])
        prod = sb("prod", [P, 256])
        M = sb("M", [P, 16, P])
        X = sb("X", [P, 16, P])
        Y = sb("Y", [P, 16, P])
        ye = sb("ye", [P, 2, 4, P])
        yo = sb("yo", [P, 2, 4, P])
        S = sb("S", [P, 2, 4, P])
        og = sb("og", [P, 4, 4, P])
        oT = [t[:, h].rearrange("p a b -> p (a b)") for t in (ye, yo) for h in range(2)]
        sso = sb("sso", [P, 4, 4])
        rms = sb("rms", [P, 4, 4])
        fac = sb("fac", [P, 4, 4])
        stats = sb("stats", [P, NU, 6])
        mv = sb("mv", [P, NU, 2])
        rstd = sb("rstd", [P, NU])
        spare = sb("spare", [P, 1])
        lnk = sb("lnk", [P, 16])
        lno = sb("lno", [P, 4, 4])
        lnv = sb("lnv", [P, NU])
        raw = decays
        asum = sb("asum", [P, 3])
        scale = sb("scale", [P, 3])
        half = sb("half", [P, 3])
        nhalf = sb("nhalf", [P, 3])
        xn = og
        xn_v = og[:].rearrange("p a b c -> p (a b c)").rearrange("p (u d) -> p u d", d=D)
        wT = chan
        beta_r = Wd[0:NH, 0:8, :].rearrange("p a b -> p (a b)")
        t1_r = Wd[0:NH, 8:16, :].rearrange("p a b -> p (a b)")
        sp_r = Wi[0:NH, 0:8, :].rearrange("p a b -> p (a b)")
        g_r = Wi[0:NH, 8:16, :].rearrange("p a b -> p (a b)")
        gc_r = vt[0:NH, 0:8, :].rearrange("p a b -> p (a b)")
        ngc_r = vt[0:NH, 8:16, :].rearrange("p a b -> p (a b)")
        egl_r = zs[0:NH, 0:8, :].rearrange("p a b -> p (a b)")
        dif_r = zs[0:NH, 8:16, :].rearrange("p a b -> p (a b)")
        expA = sb("expA", [NH, 1])

        proj = [ctx.enter_context(nc.psum_tensor(f"proj{i}", [P, 512], F32)) for i in range(4)]
        work = [ctx.enter_context(nc.psum_tensor(f"work{i}", [P, 512], F32)) for i in range(4)]

        x_loaded, small_loaded, ffn_loaded = sem("x_loaded"), sem("small_loaded"), sem("ffn_loaded")
        wqkv_loaded, conv_loaded, wz_loaded, wo_loaded = (sem("wqkv_loaded"), sem("conv_loaded"),
                                                          sem("wz_loaded"), sem("wo_loaded"))
        gcb_loaded, cols_loaded = sem("gcb_loaded"), sem("cols_loaded")
        gc_stored, l_stored, l_loaded = sem("gc_stored"), sem("l_stored"), sem("l_loaded")
        x_stored, mx_loaded, out_stored = sem("x_stored"), sem("mx_loaded"), sem("out_stored")
        consts_step, consts_ready = sem("consts_step"), sem("consts_ready")
        ln_step, xn_ready, xnT_filled, xnT_ready = (sem("ln_step"), sem("xn_ready"), sem("xnT_filled"),
                                                    sem("xnT_ready"))
        ba_filled, rows_act, rows_dve, rows_ready = (sem("ba_filled"), sem("rows_act"), sem("rows_dve"),
                                                     sem("rows_ready"))
        colsT_filled, colsT_ready = sem("colsT_filled"), sem("colsT_ready")
        proj_filled, tap3_done, taps_done, silu_done = (sem("proj_filled"), sem("tap3_done"),
                                                        sem("taps_done"), sem("silu_done"))
        work_filled = sem("work_filled")
        z_ready, eg_ready, abs_done, w_ready, sq_ready, sq_read = (
            sem("z_ready"), sem("eg_ready"), sem("abs_done"), sem("w_ready"), sem("sq_ready"), sem("sq_read"))
        prep_step, negc_ready, kd_ready, masked, kq_ready, mx_zeroed = (
            sem("prep_step"), sem("negc_ready"), sem("kd_ready"), sem("masked"), sem("kq_ready"),
            sem("mx_zeroed"))
        l_ready, vt_ready, inv_step = sem("l_ready"), sem("vt_ready"), sem("inv_step")
        y_ready, m_ready, xj_ready = sem("y_ready"), sem("m_ready"), sem("xj_ready")
        ye_ready, s_ready, r_ready, yo_ready = sem("ye_ready"), sem("s_ready"), sem("r_ready"), sem("yo_ready")
        sqo_ready, sqo_read, rms_ready, og_ready, oT_ready, acc_done = (
            sem("sqo_ready"), sem("sqo_read"), sem("rms_ready"), sem("og_ready"), sem("oT_ready"),
            sem("acc_done"))
        fk_ready, spared = sem("fk_ready"), sem("spared")
        lnk_done, rs_ready, lno_done, fac_ready = (sem("lnk_done"), sem("rs_ready"), sem("lno_done"),
                                                   sem("fac_ready"))
        var_ready, lnv_done, rstd_ready = sem("var_ready"), sem("lnv_done"), sem("rstd_ready")
        asum_ready, total_filled, quant_step, digits_ready = (
            sem("asum_ready"), sem("total_filled"), sem("quant_step"), sem("digits_ready"))
        wT_filled, wT_ready = sem("wT_filled"), sem("wT_ready")
        x1_step, xn2_ready, xn2T_filled, xn2T_ready = (sem("x1_step"), sem("xn2_ready"),
                                                       sem("xn2T_filled"), sem("xn2T_ready"))
        up_filled, silu_up, hid_ready, down_filled = (sem("up_filled"), sem("silu_up"), sem("hid_ready"),
                                                      sem("down_filled"))
        fin_step, fin_ready = sem("fin_step"), sem("fin_ready")

        def four(ap):
            return ap[:].rearrange("p (a b) -> p a b", a=4)

        def units(g):
            return slice(4 * g, 4 * g + 4)

        def odd_units(t, h):
            return t[:, 8 * h + 1:8 * h + 8:2, :]

        block = ctx.enter_context(nc.Block())

        @block.sync
        def _(sp):
            sp.dma_start(x_sb[:], x_t).then_inc(x_loaded, 16)
            sp.dma_start(wba[:], W_ba.rearrange("(k p) c -> p k c", p=P)).then_inc(small_loaded, 16)
            sp.dma_start(alog[:], A_log.rearrange("(h a) -> h a", a=1)).then_inc(small_loaded, 16)
            sp.dma_start(dtb[:], dt_bias.rearrange("(h a) -> h a", a=1)).then_inc(small_loaded, 16)
            sp.dma_start(nw[:], norm_w.rearrange("(h a) -> h a", a=1)).then_inc(small_loaded, 16)

            def pick(view, n):
                if isinstance(n, int):
                    return view[n]
                v = view[bass.ds(n, 1)]
                names = " ".join("abcdef"[:len(view.shape) - 1])
                return v.rearrange(f"n {names} -> (n a) {names[2:]}")

            def constant_wait():
                sp.wait_ge(x_loaded, 16)

            def load_qkv(n):
                constant_wait()
                wait(sp, proj_filled, n * 12)
                for k in range(KT):
                    sp.dma_start(w_qkv[:, k], pick(wq_d[:, :, k, :, 0:3 * DH], n)).then_inc(wqkv_loaded, 16)
                constant_wait()
                wait(sp, taps_done, n * 36)
                for s in range(3):
                    sp.dma_start(w_conv[:, s], pick(conv_d[:, :, s], n)).then_inc(conv_loaded, 16)

            def load_prep(n):
                constant_wait()
                wait(sp, z_ready, n * 4)
                for k in range(KT):
                    sp.dma_start(w_z[:, k], pick(wq_d[:, :, k, :, 3 * DH:4 * DH], n)).then_inc(wz_loaded, 16)
                constant_wait()
                wait(sp, w_ready, n * 4)
                wait(sp, eg_ready, n * 2)
                if isinstance(n, int):
                    rows = gc_d[2 * n:2 * n + 2, :]
                    pair = cols_all[:, 2 * n:2 * n + 2]
                else:
                    rows = gc_d[bass.ds(n * 2, 2), :]
                    pair = cols_all[:, bass.ds(n * 2, 2)]
                sp.dma_start(gcb, rows.partition_broadcast(P)).then_inc(gcb_loaded, 16)
                constant_wait()
                wait(sp, vt_ready, n * 4)
                sp.dma_start(cols[:], pair).then_inc(cols_loaded, 16)

            def blocks(m, n):
                sp.wait_ge(l_ready, n * 8)
                for b in range(NB16):
                    sp.dma_start(blk_out_d[:, b].rearrange("u r c -> r u c"),
                                 Lneg[16 * b:16 * b + 16, :, 16 * b:16 * b + 16]).then_inc(l_stored, 16)
                sp.wait_ge(l_stored, n * (16 * NB16))
                sp.dma_start(lb[:], blk_out_d.rearrange("u b r c -> (u b) r c")).then_inc(l_loaded, 16)
                sp.wait_ge(inv_step, n * N_INV)
                sp.dma_start(blk_in_d.rearrange("u b x r c -> (u b) x r c"), xm[:]).then_inc(x_stored, 16)
                sp.wait_ge(x_stored, n * 16)
                sp.wait_ge(mx_zeroed, n * 2)
                for i, t in enumerate((X, M)):
                    for b in range(NB16):
                        sp.dma_start(t[16 * b:16 * b + 16, :, 16 * b:16 * b + 16],
                                     blk_in_d[:, b, i].rearrange("u r c -> r u c")).then_inc(mx_loaded, 16)

            def load_wo(m, n):
                constant_wait()
                wait(sp, acc_done, m * 4)
                sp.dma_start(w_o[:], pick(wout_d, m)).then_inc(wo_loaded, 16)

            load_qkv(0)
            sp.wait_ge(rows_dve, 12)
            sp.dma_start(gc_d, gc_r).then_inc(gc_stored, 16)
            sp.wait_ge(gc_stored, 16)
            sp.wait_ge(colsT_ready, 1)
            load_prep(0)
            load_qkv(1)

            def body(n, more):
                load_prep(n)
                load_wo(n - 1, n)
                blocks(n - 1, n)
                if more:
                    load_qkv(n + 1)

            with sp.Fori(1, NP - 1) as n:
                body(n, True)
            body(NP - 1, False)
            load_wo(NP - 1, NP)
            blocks(NP - 1, NP)
            sp.wait_ge(l_ready, 8 * NP)
            sp.wait_ge(w_ready, 4 * NP)
            for i, w in enumerate((W_up, W_gate)):
                sp.dma_start(raw[:, i].rearrange("p (t d) -> p t d", d=D),
                             w.rearrange("(t p) d -> p t d", p=P)).then_inc(ffn_loaded, 16)
            sp.dma_start(raw[:, 2].rearrange("p (a e) -> p a e", e=E),
                         W_down.rearrange("(a p) e -> p a e", p=P)).then_inc(ffn_loaded, 16)
            for u in range(NU):
                sp.wait_ge(fin_ready, u + 1)
                sp.dma_start(out_t[:, u, :], x_sb[:, u, :]).then_inc(out_stored, 16)
            sp.wait_ge(out_stored, 16 * NU)

        @block.gpsimd
        def _(pool):
            def select(t, ap, base, pattern, mult, op, fill):
                pool.affine_select(out=ap, in_=ap, compare_op=op, fill=fill, base=base, pattern=pattern,
                                   channel_multiplier=mult).then_inc(consts_ready, 1)

            pool.memset(ident[:], 0.0).then_inc(consts_step, 1)
            pool.memset(ones[:], 1.0).then_inc(consts_ready, 1)
            pool.memset(strict[:], 1.0).then_inc(consts_step, 1)
            pool.memset(upper[:], 1.0).then_inc(consts_step, 1)
            pool.memset(Y[:], 0.0).then_inc(consts_step, 1)
            pool.memset(M[:], 0.0).then_inc(consts_step, 1)
            pool.memset(X[:], 0.0).then_inc(consts_step, 1)
            pool.memset(xm[:], 0.0).then_inc(consts_step, 1)
            pool.memset(attn_out[:], 0.0).then_inc(consts_ready, 1)
            pool.wait_ge(consts_step, 7)
            select(ident, ident[:], 0, [[-1, P]], 1, ALU.not_equal, 1.0)
            select(strict, strict[:], 0, [[-1, P]], 1, ALU.is_gt, 0.0)
            select(upper, upper[:], 0, [[1, P]], -1, ALU.is_ge, 0.0)
            select(Y, Y[:], 0, [[0, 16], [-1, P]], 1, ALU.not_equal, 1.0)
            select(xm, xm[:], 0, [[0, 2], [-1, 16], [1, 16]], 0, ALU.not_equal, 1.0)

            def prepare(n, first):
                if first:
                    pool.wait_ge(consts_ready, 7)
                    pool.tensor_tensor(spare[:], ones[:, 0:1], ones[:, 0:1], ALU.mult).then_inc(spared, 1)
                    pool.memset(M[:], 0.0).then_inc(mx_zeroed, 1)
                    pool.memset(X[:], 0.0).then_inc(mx_zeroed, 1)
                else:
                    pool.wait_ge(work_filled, filled_at("solve", n - 1, ("o_odd", 1)))
                    pool.wait_ge(spared, n)
                    pool.tensor_tensor(spare[:], ones[:, 0:1], ones[:, 0:1], ALU.mult).then_inc(spared, 1)
                    pool.memset(M[:], 0.0).then_inc(mx_zeroed, 1)
                    pool.memset(X[:], 0.0).then_inc(mx_zeroed, 1)
                for g in range(4):
                    h = g // 2
                    pool.wait_ge(w_ready, n * 4 + (g + 1))
                    wait(pool, l_ready, n * 8)
                    w4 = Wd[:, units(g), :]
                    pool.tensor_tensor(Wi[:, units(g), :], w4, upper[:].unsqueeze(1).broadcast_to([P, 4, P]),
                                       ALU.mult).then_inc(masked, 1)
                    pool.wait_ge(masked, n * 12 + (3 * g + 1))
                    pool.tensor_tensor(w4, w4, strict[:].unsqueeze(1).broadcast_to([P, 4, P]),
                                       ALU.mult).then_inc(masked, 1)
                    pool.wait_ge(negc_ready, n * 4 + (g + 1))
                    pool.wait_ge(masked, n * 12 + (3 * g + 2))
                    pool.tensor_tensor(w4, w4, negc[:, units(g)].unsqueeze(2).broadcast_to([P, 4, P]),
                                       ALU.mult).then_inc(masked, 1)
                    if g % 2 == 0:
                        pool.wait_ge(eg_ready, n * 2 + (h + 1))
                        pool.wait_ge(silu_done, n * 12 + 12)
                        for s, t in ((K_, kp), (Q_, qp)):
                            src = chan[:, h, s, :].rearrange("p (u t) -> p u t", t=P)[:, 1::2, :]
                            ins = pool.tensor_tensor(t[:, h], src, eg[:, h], ALU.mult)
                        ins.then_inc(kq_ready, 1)

            prepare(0, True)
            with pool.Fori(1, NP) as n:
                prepare(n, False)

        @block.tensor
        def _(pe):
            read_by = {}
            for g in range(4):
                read_by["z", g] = [(z_ready, 4, g + 1)]
                read_by["kT", g] = [(sq_ready, 8, 2 * g + 1), (kd_ready, 5, g + 1)]
                read_by["qT", g] = [(sq_ready, 8, 2 * g + 2)]
                read_by["vT", g] = [(vt_ready, 4, g + 1)]
                for t in range(2):
                    read_by["gram", g, t] = [(l_ready, 8, 2 * g + t + 1)]
                for lv in range(3):
                    read_by["LM", lv, g] = [(y_ready, 12, 4 * lv + g + 1)]
                    read_by["MY", lv, g] = [(m_ready, 12, 4 * lv + g + 1)]
                    read_by["YX", lv, g] = [(xj_ready, 8, 4 * lv + g + 1)]
            for h in range(2):
                read_by["y_even", h] = [(ye_ready, 2, h + 1)]
                read_by["state", h] = [(s_ready, 2, h + 1)]
                read_by["kS", h] = [(r_ready, 2, h + 1)]
                read_by["y_odd", h] = [(yo_ready, 2, h + 1)]
                for par, name in enumerate(("even", "odd")):
                    read_by["o_" + name, h] = [(sqo_ready, 4, 2 * par + h + 1), (og_ready, 4, 2 * par + h + 1)]
                    read_by["oT_" + name, h] = [(oT_ready, 4, 2 * par + h + 1)]
                    read_by["out_" + name, h] = [(acc_done, 4, 2 * par + h + 1)]

            def bank(phase, n, key):
                earlier = before(phase, n, key)
                if earlier is not None:
                    for done, per, count in read_by[earlier[2]]:
                        pe.wait_ge(done, earlier[1] * per + count)
                return work[bank_of(phase, key)]

            def project(n):
                pe.wait_ge(wqkv_loaded, n * (16 * KT) + 16 * KT)
                for h in range(2):
                    for s in range(3):
                        for t in range(2):
                            turn = 6 * h + 2 * s + t
                            if turn >= 4:
                                pe.wait_ge(taps_done, tap_at(n, turn - 4, 2))
                            elif not (isinstance(n, int) and n == 0):
                                pe.wait_ge(taps_done, tap_at(n, turn + 8, 2) - 36)
                            c = W_COL[s]
                            for k in range(KT):
                                ins = pe.matmul(proj[turn % 4][:], w_qkv[:, k, h, c:c + DH],
                                                xnT[:, k, 512 * t:512 * t + 512],
                                                start=(k == 0), stop=(k == KT - 1))
                            ins.then_inc(proj_filled, 1)

            def prepare(n):
                pe.wait_ge(silu_done, n * 12 + 12)

                def turned(name, s, g):
                    ps = bank("prep", n, (name, g))
                    for j in range(4):
                        u = 4 * (g % 2) + j
                        ins = pe.transpose(ps[:, j * P:(j + 1) * P], chan[:, g // 2, s, u * P:(u + 1) * P],
                                           ident[:])
                    ins.then_inc(work_filled, 1)

                for g in range(4):
                    turned("kT", K_, g)
                    turned("qT", Q_, g)
                for g in range(4):
                    for t in range(2):
                        ps = bank("prep", n, ("gram", g, t))
                        for j in range(2):
                            u = 4 * (g % 2) + 2 * t + j
                            ins = pe.matmul(ps[:, j * 2 * P:(j + 1) * 2 * P],
                                            chan[:, g // 2, K_, u * P:(u + 1) * P],
                                            chan[:, g // 2, K_:V_, u * P:(u + 1) * P], start=True, stop=True)
                        ins.then_inc(work_filled, 1)
                for g in range(4):
                    turned("vT", V_, g)
                pe.wait_ge(wz_loaded, n * (16 * KT) + 16 * KT)
                for g in range(4):
                    ps = bank("prep", n, ("z", g))
                    for j in range(4):
                        u = 4 * (g % 2) + j
                        for k in range(KT):
                            ins = pe.matmul(ps[:, j * P:(j + 1) * P], xnT[:, k, u * P:(u + 1) * P],
                                            w_z[:, k, g // 2, :], start=(k == 0), stop=(k == KT - 1))
                    ins.then_inc(work_filled, 1)

            def product(n, key, terms):
                ps = bank("solve", n, key)
                for j in range(4):
                    ts = terms(j)
                    for i, (a, b) in enumerate(ts):
                        ins = pe.matmul(ps[:, j * P:(j + 1) * P], a, b, start=(i == 0), stop=(i == len(ts) - 1))
                ins.then_inc(work_filled, 1)

            def solve(m):
                pe.wait_ge(mx_loaded, m * (32 * NB16) + 32 * NB16)
                for lv in range(3):
                    for g in range(4):
                        if lv:
                            pe.wait_ge(m_ready, m * 12 + (4 * (lv - 1) + g + 1))
                        product(m, ("LM", lv, g), lambda j: [(Lneg[:, 4 * g + j, :], M[:, 4 * g + j, :])])
                    for g in range(4):
                        pe.wait_ge(y_ready, m * 12 + (4 * lv + g + 1))
                        if lv:
                            pe.wait_ge(xj_ready, m * 8 + (4 * (lv - 1) + g + 1))
                        product(m, ("MY", lv, g), lambda j: [(X[:, 4 * g + j, :], Y[:, 4 * g + j, :])])
                        if lv < 2:
                            product(m, ("YX", lv, g), lambda j: [(Y[:, 4 * g + j, :], X[:, 4 * g + j, :])])
                pe.wait_ge(m_ready, m * 12 + 12)
                for h in range(2):
                    product(m, ("y_even", h), lambda j: [(M[:, 8 * h + 2 * j, :], vt[:, 8 * h + 2 * j, :])])
                for h in range(2):
                    pe.wait_ge(ye_ready, m * 2 + (h + 1))
                    product(m, ("state", h), lambda j: [(kd[:, h, j, :], ye[:, h, j, :])])
                for h in range(2):
                    pe.wait_ge(s_ready, m * 2 + (h + 1))
                    product(m, ("kS", h), lambda j: [(kp[:, h, j, :], S[:, h, j, :])])
                for h in range(2):
                    product(m, ("o_even", h), lambda j: [(attnT[:, 8 * h + 2 * j, :], ye[:, h, j, :])])
                for h in range(2):
                    pe.wait_ge(r_ready, m * 2 + (h + 1))
                    product(m, ("y_odd", h), lambda j: [(M[:, 8 * h + 2 * j + 1, :], vt[:, 8 * h + 2 * j + 1, :])])
                for h in range(2):
                    pe.wait_ge(yo_ready, m * 2 + (h + 1))
                    product(m, ("o_odd", h), lambda j: [(qp[:, h, j, :], S[:, h, j, :]),
                                                        (attnT[:, 8 * h + 2 * j + 1, :], yo[:, h, j, :])])
                pe.wait_ge(wo_loaded, m * 16 + 16)
                for par, name in enumerate(("even", "odd")):
                    for h in range(2):
                        pe.wait_ge(og_ready, m * 4 + (2 * par + h + 1))
                        ps = bank("solve", m, (f"oT_{name}", h))
                        for j in range(4):
                            ins = pe.transpose(ps[:, j * P:(j + 1) * P], og[:, 2 * par + h, j, :], ident[:])
                        ins.then_inc(work_filled, 1)
                    pe.wait_ge(oT_ready, m * 4 + (2 * par + 2))
                    for t in range(2):
                        ps = bank("solve", m, (f"out_{name}", t))
                        for j in range(2):
                            for h in range(2):
                                at = (2 * t + j) * P
                                ins = pe.matmul(ps[:, j * D:(j + 1) * D], oT[2 * par + h][:, at:at + P],
                                                w_o[:, h, :], start=(h == 0), stop=(h == 1))
                        ins.then_inc(work_filled, 1)

            pe.wait_ge(consts_ready, 7)
            pe.wait_ge(xn_ready, NU)
            for k in range(KT):
                for t in range(2):
                    for j in range(4):
                        u = 4 * t + j
                        ins = pe.transpose(proj[2 * k + t][:, j * P:(j + 1) * P], xn_v[:, u, k * P:(k + 1) * P],
                                           ident[:])
                    ins.then_inc(xnT_filled, 1)
            pe.wait_ge(small_loaded, 64)
            pe.wait_ge(xnT_ready, 4)
            for i in range(2):
                for t in range(2):
                    for k in range(KT):
                        ins = pe.matmul(work[2 * i + t][0:NH, :], wba[:, k, i::2],
                                        xnT[:, k, 512 * t:512 * t + 512], start=(k == 0), stop=(k == KT - 1))
                    ins.then_inc(ba_filled, 1)
            project(0)
            pe.wait_ge(rows_dve, 14)
            pe.wait_ge(rows_ready, 1)
            for i, rows in enumerate((ngc_r, beta_r, egl_r)):
                for u in range(NU):
                    at = (i * NU + u) * NH
                    ins = pe.transpose(work[0][:, at:at + NH], rows[:, u * P:(u + 1) * P], ident[0:NH, 0:NH])
            ins.then_inc(colsT_filled, 1)
            pe.wait_ge(colsT_ready, 1)
            prepare(0)
            with pe.Fori(1, NP) as n:
                project(n)
                solve(n - 1)
                prepare(n)
            solve(NP - 1)

            pe.wait_ge(asum_ready, 3)
            pe.wait_ge(taps_done, 36 * NP)
            pe.matmul(proj[0][:, 0:3], ones[:], asum[:], start=True, stop=True).then_inc(total_filled, 1)
            pe.wait_ge(digits_ready, 3)
            for i in range(3):
                for q in range(4):
                    turn = 4 * i + q
                    if turn >= 4:
                        pe.wait_ge(wT_ready, turn - 3)
                    for j in range(4):
                        if i < 2:
                            src = raw[:, i, (4 * (q % 2) + j) * D + (q // 2) * P:][:, 0:P]
                        else:
                            src = raw[:, i, (j % 2) * E + (2 * q + j // 2) * P:][:, 0:P]
                        ins = pe.transpose(proj[q][:, j * P:(j + 1) * P], src, ident[:])
                    ins.then_inc(wT_filled, 1)
            pe.wait_ge(xn2_ready, NU)
            pe.wait_ge(wT_ready, 12)
            for k in range(KT):
                for t in range(2):
                    for j in range(4):
                        u = 4 * t + j
                        ins = pe.transpose(proj[2 * k + t][:, j * P:(j + 1) * P], xn_v[:, u, k * P:(k + 1) * P],
                                           ident[:])
                    ins.then_inc(xn2T_filled, 1)
            pe.wait_ge(xn2T_ready, 4)
            def down(t, e):
                i = t * ET + e
                pe.wait_ge(hid_ready, i + 1)
                for j in range(4):
                    ins = pe.matmul(work[2 * t + j // 2][:, (j % 2) * D:(j % 2 + 1) * D],
                                    og[:, i % 2, j, :], wT_flat[:, 2, e * D:(e + 1) * D],
                                    start=(e == 0 and j % 2 == 0), stop=(e == ET - 1), skip_group_check=True)
                ins.then_inc(down_filled, 1)

            wT_flat = chan[:].rearrange("p h s t -> p (h s t)").rearrange("p (i e) -> p i e", i=3)
            for t in range(2):
                for e in range(ET):
                    i = t * ET + e
                    if i >= 2:
                        pe.wait_ge(hid_ready, i - 1)
                    for w in range(2):
                        for k in range(KT):
                            ins = pe.matmul(proj[2 * (i % 2) + w][:],
                                            wT_flat[:, w, k * E + e * P:k * E + (e + 1) * P],
                                            xnT[:, k, 512 * t:512 * t + 512], start=(k == 0), stop=(k == KT - 1))
                    ins.then_inc(up_filled, 1)
                    if i >= 1:
                        down((i - 1) // ET, (i - 1) % ET)
            down(1, ET - 1)

        @block.scalar
        def _(act):
            def filled(phase, n, key):
                act.wait_ge(work_filled, filled_at(phase, n, key))
                return four(work[bank_of(phase, key)])

            def project(n):
                act.wait_ge(conv_loaded, n * 48 + 48)
                for p in range(8):
                    if p < 6:
                        for i in range(2):
                            turn = 2 * p + i
                            h, s = turn // 6, (turn // 2) % 3
                            act.wait_ge(proj_filled, n * 12 + (turn + 1))
                            wait(act, silu_done, n * 12 + (turn - 3))
                            act.activation(conv[:, turn % 4, :], proj[turn % 4][:], ACT.Copy,
                                           scale=w_conv[:, CONV_S[s], h, 3:4]).then_inc(tap3_done, 1)
                    if p >= 1 and p < 7:
                        for i in range(2):
                            turn = 2 * (p - 1) + i
                            h, s = turn // 6, (turn // 2) % 3
                            act.wait_ge(taps_done, tap_at(n, turn, 2))
                            act.activation(chan[:, h, s, 512 * i:512 * i + 512], conv[:, turn % 4, :],
                                           ACT.Silu).then_inc(silu_done, 1)

            def prepare(n):
                act.wait_ge(gcb_loaded, n * 16 + 16)
                act.wait_ge(cols_loaded, n * 16 + 16)
                wait(act, kq_ready, n * 2)
                wait(act, l_ready, n * 8)
                for g in range(4):
                    h = g // 2
                    if g % 2 == 0:
                        src = gcb[:, h, :].rearrange("p (u t) -> p u t", t=P)[:, 1::2, :]
                        act.activation(eg[:, h], src, ACT.Exp).then_inc(eg_ready, 1)
                    for j in range(4):
                        u = 4 * (g % 2) + j
                        ins = act.activation(Wd[:, 4 * g + j, :], gcb[:, h, u * P:(u + 1) * P], ACT.Abs,
                                             bias=cols[:, h, 0, u:u + 1])
                    ins.then_inc(abs_done, 1)
                    act.wait_ge(abs_done, n * 4 + (g + 1))
                    act.activation(Wd[:, units(g), :], Wd[:, units(g), :], ACT.Exp,
                                   scale=-1.0).then_inc(w_ready, 1)
                    for i, name in enumerate(("kT", "qT")):
                        ps = filled("prep", n, (name, g))
                        turn = 2 * g + i
                        if turn >= 4:
                            act.wait_ge(sq_read, n * 8 + (turn - 3))
                        ins = act.activation(sq[:, turn % 4, :].rearrange("p (a b) -> p a b", a=4), ps,
                                             ACT.Square)
                        ins.then_inc(sq_ready, 1)
                act.wait_ge(prep_step, n * N_PREP_STEP + N_PREP_STEP)
                act.activation(lnk[:], sst[:], ACT.Ln).then_inc(lnk_done, 1)
                act.wait_ge(lnk_done, n + 1)
                act.activation(rs[:], lnk[:], ACT.Exp, scale=-0.5).then_inc(rs_ready, 1)
                wait(act, og_ready, n * 4)
                for g in range(4):
                    ps = filled("prep", n, ("z", g))
                    ins = act.activation(zs[:, units(g), :], ps, ACT.Silu)
                    ins.then_inc(z_ready, 1)

            def solve(m):
                def evict(key, dst, done):
                    ps = filled("solve", m, key)
                    ins = act.activation(dst, ps, ACT.Copy)
                    ins.then_inc(done, 1)

                for lv in range(3):
                    for name, dst, done in (("LM", Y, y_ready), ("MY", M, m_ready)):
                        for g in range(4):
                            ps = filled("solve", m, (name, lv, g))
                            for p0, p1, c0, c1 in m_blocks(lv):
                                ins = act.activation(dst[p0:p1, units(g), c0:c1], ps[p0:p1, :, c0:c1], ACT.Copy)
                            ins.then_inc(done, 1)
                for h in range(2):
                    evict(("y_even", h), ye[:, h], ye_ready)
                for h in range(2):
                    evict(("state", h), S[:, h], s_ready)

                def square(par, h):
                    name = ("o_even", "o_odd")[par]
                    x = 2 * par + h
                    ps = filled("solve", m, (name, h))
                    if par == 0 and h == 0:
                        act.wait_ge(sq_read, m * 8 + 8)
                    wait(act, sqo_read, m * 4)
                    ins = act.activation(sq[:, x, :].rearrange("p (a b) -> p a b", a=4), ps, ACT.Square)
                    ins.then_inc(sqo_ready, 1)

                def factor(par):
                    act.wait_ge(rms_ready, m * 4 + (2 * par + 2))
                    act.activation(lno[:, 2 * par:2 * par + 2, :], rms[:, 2 * par:2 * par + 2, :],
                                   ACT.Ln).then_inc(lno_done, 1)
                    act.wait_ge(lno_done, m * 2 + (par + 1))
                    act.activation(fac[:, 2 * par:2 * par + 2, :], lno[:, 2 * par:2 * par + 2, :], ACT.Exp,
                                   scale=-0.5).then_inc(fac_ready, 1)

                for h in range(2):
                    square(0, h)
                factor(0)
                for h in range(2):
                    evict(("y_odd", h), yo[:, h], yo_ready)
                for h in range(2):
                    square(1, h)
                factor(1)
                for par, name in enumerate(("oT_even", "oT_odd")):
                    for h in range(2):
                        x = 2 * par + h
                        ps = filled("solve", m, (name, h))
                        ins = act.activation(oT[x].rearrange("p (a b) -> p a b", a=4), ps, ACT.Copy,
                                             scale=nw[:, 0:1])
                        ins.then_inc(oT_ready, 1)

            def inverse_root(u0, u1, norm):
                act.wait_ge(var_ready, norm)
                act.activation(lnv[:, u0:u1], rstd[:, u0:u1], ACT.Ln).then_inc(lnv_done, 1)
                act.wait_ge(lnv_done, norm)
                act.activation(rstd[:, u0:u1], lnv[:, u0:u1], ACT.Exp, scale=-0.5).then_inc(rstd_ready, 1)

            inverse_root(0, NU, 1)
            for i in range(4):
                act.wait_ge(xnT_filled, i + 1)
                act.activation(xnT[:, i // 2, 512 * (i % 2):512 * (i % 2) + 512], proj[i][:],
                               ACT.Copy).then_inc(xnT_ready, 1)
            act.wait_ge(ba_filled, 4)
            for t in range(2):
                act.activation(beta_r[:, 512 * t:512 * t + 512], work[t][0:NH, :],
                               ACT.Sigmoid).then_inc(rows_act, 1)
            for t in range(2):
                act.activation(t1_r[:, 512 * t:512 * t + 512], work[2 + t][0:NH, :], ACT.Abs,
                               bias=dtb[:, 0:1]).then_inc(rows_act, 1)
            act.activation(expA[:], alog[:], ACT.Exp).then_inc(rows_act, 1)
            act.wait_ge(rows_act, 4)
            act.activation(t1_r, t1_r, ACT.Exp, scale=-1.0).then_inc(rows_act, 1)
            act.wait_ge(rows_act, 6)
            act.activation(t1_r, t1_r, ACT.Ln, bias=1.0).then_inc(rows_act, 1)
            act.wait_ge(rows_dve, 13)
            act.activation(egl_r, dif_r, ACT.Exp).then_inc(rows_ready, 1)
            project(0)
            act.wait_ge(colsT_ready, 1)
            prepare(0)
            with act.Fori(1, NP) as n:
                project(n)
                solve(n - 1)
                prepare(n)
            solve(NP - 1)

            act.wait_ge(ffn_loaded, 48)
            act.wait_ge(silu_done, 12 * NP)
            for i in range(3):
                act.activation(conv[:].rearrange("p a b -> p (a b)"), raw[:, i, :], ACT.Abs,
                               accum_out=asum[:, i:i + 1]).then_inc(asum_ready, 1)
                act.wait_ge(asum_ready, i + 1)
            wT_flat = chan[:].rearrange("p h s t -> p (h s t)").rearrange("p (i e) -> p i e", i=3)
            for turn in range(12):
                act.wait_ge(wT_filled, turn + 1)
                i, q = turn // 4, turn % 4
                act.activation(wT_flat[:, i, 512 * q:512 * q + 512], proj[q][:], ACT.Copy).then_inc(wT_ready, 1)
            inverse_root(0, NU, 2)
            inverse_root(0, NU, 3)
            for i in range(4):
                act.wait_ge(xn2T_filled, i + 1)
                act.activation(xnT[:, i // 2, 512 * (i % 2):512 * (i % 2) + 512], proj[i][:],
                               ACT.Copy).then_inc(xn2T_ready, 1)
            for i in range(2 * ET):
                act.wait_ge(up_filled, i + 1)
                if i >= 2:
                    act.wait_ge(hid_ready, i - 1)
                act.activation(conv[:, i % 2, :], proj[2 * (i % 2)][:], ACT.Silu,
                               scale=scale[:, 0:1]).then_inc(silu_up, 1)
            inverse_root(0, 4, 4)
            inverse_root(4, 8, 5)

        @block.vector
        def _(dve):
            def filled(phase, n, key):
                dve.wait_ge(work_filled, filled_at(phase, n, key))
                return work[bank_of(phase, key)]

            def taps(n, pair):
                h, s = pair // 3, pair % 3
                for tap in range(3):
                    for i in range(2):
                        turn = 2 * pair + i
                        d = tap + 1
                        if tap == 0:
                            dve.wait_ge(tap3_done, n * 12 + (turn + 1))
                        else:
                            dve.wait_ge(taps_done, tap_at(n, turn, tap - 1))
                        acc = conv[:, turn % 4, :].rearrange("p (b t) -> p b t", t=SEG)[:, :, d:]
                        src = proj[turn % 4][:].rearrange("p (b t) -> p b t", t=SEG)[:, :, 0:SEG - d]
                        dve.scalar_tensor_tensor(out=acc, in0=src,
                                                 scalar=w_conv[:, CONV_S[s], h, 2 - tap:3 - tap],
                                                 in1=acc, op0=ALU.mult, op1=ALU.add).then_inc(taps_done, 1)

            def substitute(m):
                dve.wait_ge(l_loaded, m * 16 + 16)
                wait(dve, x_stored, m * 16)
                k = 0
                for i in range(1, 16):
                    pv = prod[:, 0:i * i].rearrange("p (c j) -> p c j", j=i)
                    if k:
                        dve.wait_ge(inv_step, m * N_INV + k)
                    dve.tensor_tensor(pv, lb[:, i, 0:i].unsqueeze(1).broadcast_to([P, i, i]),
                                      xm[:, 0, 0:i, 0:i].rearrange("p j c -> p c j"),
                                      ALU.mult).then_inc(inv_step, 1)
                    k += 1
                    dve.wait_ge(inv_step, m * N_INV + k)
                    dve.tensor_reduce(xm[:, 0, i, 0:i], pv, AX.X, ALU.add).then_inc(inv_step, 1)
                    k += 1
                dve.wait_ge(inv_step, m * N_INV + k)
                dve.tensor_copy(xm[:, 1], xm[:, 0].rearrange("p r c -> p c r")).then_inc(inv_step, 1)
                assert k + 1 == N_INV

            def prepare(n):
                dve.wait_ge(cols_loaded, n * 16 + 16)
                for g in range(4):
                    h, c0 = g // 2, 4 * (g % 2)
                    us = units(g)
                    beta = cols[:, h, 1, c0:c0 + 4]
                    b0 = n * N_PREP_STEP + 2 * g
                    dve.wait_ge(sq_ready, n * 8 + (2 * g + 1))
                    ins = dve.tensor_reduce(ss[:, us], sq[:, (2 * g) % 4, :].rearrange("p (a b) -> p a b", a=4),
                                            AX.X, ALU.add)
                    ins.then_inc(sq_read, 1)
                    dve.wait_ge(sq_read, n * 8 + (2 * g + 1))
                    dve.tensor_scalar(sst[:, us], ss[:, us], L2_EPS, None, ALU.add).then_inc(prep_step, 1)
                    dve.wait_ge(prep_step, b0 + 1)
                    dve.reciprocal(rt[:, us], sst[:, us]).then_inc(prep_step, 1)
                    dve.wait_ge(prep_step, b0 + 2)
                    dve.scalar_tensor_tensor(out=negc[:, us], in0=rt[:, us], scalar=-1.0, in1=beta,
                                             op0=ALU.mult, op1=ALU.mult).then_inc(negc_ready, 1)
                    ps = four(filled("prep", n, ("kT", g)))
                    ins = dve.tensor_tensor(kd[:, h, c0 // 2:c0 // 2 + 2, :], ps[:, 0::2, :],
                                            cols[:, h, 2, c0:c0 + 4:2].unsqueeze(2).broadcast_to([P, 2, P]),
                                            ALU.mult)
                    ins.then_inc(kd_ready, 1)
                    dve.wait_ge(sq_ready, n * 8 + (2 * g + 2))
                    dve.tensor_reduce(ssq[:, us], sq[:, (2 * g + 1) % 4, :].rearrange("p (a b) -> p a b", a=4),
                                      AX.X, ALU.add).then_inc(sq_read, 1)
                dve.wait_ge(sq_read, n * 8 + 8)
                dve.tensor_scalar(qe[:], ssq[:], L2_EPS, DH * RMS_EPS, ALU.add, ALU.mult).then_inc(kd_ready, 1)
                for g in range(4):
                    dve.wait_ge(masked, n * 12 + (3 * g + 3))
                    for t in range(2):
                        ps = filled("prep", n, ("gram", g, t))[:].rearrange("p (a b) -> p a b", a=2)
                        us = slice(4 * g + 2 * t, 4 * g + 2 * t + 2)
                        dve.tensor_tensor(Lneg[:, us, :], ps[:, :, 0:P], Wd[:, us, :], ALU.mult)
                        ins = dve.tensor_tensor(attnT[:, us, :], ps[:, :, P:2 * P], Wi[:, us, :], ALU.mult)
                        ins.then_inc(l_ready, 1)
                dve.wait_ge(rs_ready, n + 1)
                dve.tensor_tensor(fk[:].rearrange("p (h u) -> p h u", h=2),
                                  rs[:].rearrange("p (h u) -> p h u", h=2), cols[:, :, 1, :],
                                  ALU.mult).then_inc(fk_ready, 1)
                dve.wait_ge(fk_ready, n + 1)
                for g in range(4):
                    ps = four(filled("prep", n, ("vT", g)))
                    ins = dve.tensor_tensor(vt[:, units(g), :], ps,
                                            fk[:, units(g)].unsqueeze(2).broadcast_to([P, 4, P]), ALU.mult)
                    ins.then_inc(vt_ready, 1)

            def mean_square(m, par, h):
                x = 2 * par + h
                dve.wait_ge(sqo_ready, m * 4 + (x + 1))
                dve.tensor_reduce(sso[:, x, :], sq[:, x, :].rearrange("p (a b) -> p a b", a=4),
                                  AX.X, ALU.add).then_inc(sqo_read, 1)
                dve.wait_ge(sqo_read, m * 4 + (x + 1))
                dve.scalar_tensor_tensor(out=rms[:, x, :], in0=sso[:, x, :], scalar=1.0 / DH,
                                         in1=qe[:, 8 * h + par:8 * h + 8:2],
                                         op0=ALU.mult, op1=ALU.add).then_inc(rms_ready, 1)

            def gated(m, par, h):
                x = 2 * par + h
                ps = four(filled("solve", m, (("o_even", "o_odd")[par], h)))
                dve.wait_ge(fac_ready, m * 2 + (par + 1))
                for j in range(4):
                    ins = dve.scalar_tensor_tensor(out=og[:, x, j, :], in0=ps[:, j, :],
                                                   scalar=fac[:, x, j:j + 1],
                                                   in1=zs[:, 8 * h + 2 * j + par, :],
                                                   op0=ALU.mult, op1=ALU.mult)
                ins.then_inc(og_ready, 1)

            def solve(m):
                for lv in range(2):
                    for g in range(4):
                        ps = four(filled("solve", m, ("YX", lv, g)))
                        for p0, p1, c0, c1 in x_blocks(lv):
                            ins = dve.tensor_copy(X[p0:p1, units(g), c0:c1], ps[p0:p1, :, c0:c1])
                        ins.then_inc(xj_ready, 1)
                for h in range(2):
                    ps = four(filled("solve", m, ("kS", h)))
                    for j in range(4):
                        u = 8 * h + 2 * j + 1
                        ins = dve.scalar_tensor_tensor(out=vt[:, u, :], in0=ps[:, j, :],
                                                       scalar=negc[:, u:u + 1], in1=vt[:, u, :],
                                                       op0=ALU.mult, op1=ALU.add)
                    ins.then_inc(r_ready, 1)
                dve.wait_ge(z_ready, m * 4 + 4)
                dve.wait_ge(kd_ready, m * 5 + 5)
                for par, name in enumerate(("out_even", "out_odd")):
                    if par == 0:
                        for p in range(2):
                            for h in range(2):
                                mean_square(m, p, h)
                            for h in range(2):
                                gated(m, p, h)
                    for t in range(2):
                        ps = filled("solve", m, (name, t))[:].rearrange("p (a b) -> p a b", a=2)
                        acc = attn_out[:, 4 * t + par:4 * t + 4:2, :]
                        wait(dve, acc_done, m * 4)
                        ins = dve.tensor_tensor(acc, ps, acc, ALU.add)
                        ins.then_inc(acc_done, 1)

            def inverse_root(u0, u1, norm):
                dve.tensor_scalar(rstd[:, u0:u1], mv[:, u0:u1, 1], LN_EPS, None, ALU.add).then_inc(var_ready, 1)
                dve.wait_ge(rstd_ready, norm)

            def layer_stats(step, base, src, tiles, norm):
                for u in range(tiles):
                    ins = dve.bn_stats(stats[:, u, :], src(u))
                ins.then_inc(step, 1)
                dve.wait_ge(step, base + 1)
                for u in range(tiles):
                    ins = dve.bn_aggr(mv[:, u, :], stats[:, u, :])
                ins.then_inc(step, 1)
                dve.wait_ge(step, base + 2)
                inverse_root(0, tiles, norm)

            dve.wait_ge(x_loaded, 16)
            layer_stats(ln_step, 0, lambda u: x_sb[:, u, :], NU, 1)
            for u in range(NU):
                dve.tensor_scalar(xn_v[:, u, :], x_sb[:, u, :], mv[:, u, 0:1], rstd[:, u:u + 1],
                                  ALU.subtract, ALU.mult).then_inc(xn_ready, 1)
            dve.wait_ge(ba_filled, 4)
            dve.wait_ge(rows_act, 4)
            for t in range(2):
                dve.tensor_scalar(sp_r[:, 512 * t:512 * t + 512], work[2 + t][0:NH, :], dtb[:, 0:1], 0.0,
                                  ALU.add, ALU.max).then_inc(rows_dve, 1)
            dve.wait_ge(rows_act, 7)
            dve.wait_ge(rows_dve, 2)
            dve.tensor_tensor(sp_r, sp_r, t1_r, ALU.add).then_inc(rows_dve, 1)
            dve.wait_ge(rows_dve, 3)
            dve.tensor_scalar(g_r, sp_r, expA[:, 0:1], -1.0, ALU.mult, ALU.mult).then_inc(rows_dve, 1)
            dve.wait_ge(rows_dve, 4)
            dve.wait_ge(consts_ready, 7)
            for u in range(NU):
                dve.tensor_tensor_scan(gc_r[:, u * P:(u + 1) * P], ones[0:NH, :], g_r[:, u * P:(u + 1) * P],
                                       0.0, ALU.mult, ALU.add).then_inc(rows_dve, 1)
            dve.wait_ge(rows_dve, 12)
            gc3 = gc_r.rearrange("p (u t) -> p u t", t=P)
            dve.tensor_tensor(dif_r.rearrange("p (u t) -> p u t", t=P),
                              gc3[:, :, P - 1:P].broadcast_to([NH, NU, P]), gc3,
                              ALU.subtract).then_inc(rows_dve, 1)
            dve.tensor_scalar(ngc_r, gc_r, -1.0, None, ALU.mult).then_inc(rows_dve, 1)
            for p in range(6):
                taps(0, p)
            dve.wait_ge(colsT_filled, 1)
            dve.tensor_copy(cols_all[:].rearrange("p h q u -> p q u h"),
                            work[0][:, 0:3 * NU * NH].rearrange("p (q u h) -> p q u h", q=3, u=NU)
                            ).then_inc(colsT_ready, 1)
            dve.wait_ge(gc_stored, 16)
            prepare(0)
            with dve.Fori(1, NP) as n:
                taps(n, 0)
                taps(n, 1)
                substitute(n - 1)
                for p in range(2, 6):
                    taps(n, p)
                solve(n - 1)
                prepare(n)
            substitute(NP - 1)
            solve(NP - 1)

            dve.wait_ge(total_filled, 1)
            dve.tensor_scalar(scale[:], proj[0][:, 0:3], 1.0 / (D * E), Q_EPS, ALU.mult,
                              ALU.add).then_inc(quant_step, 1)
            dve.wait_ge(quant_step, 1)
            dve.tensor_scalar(half[:], scale[:], 0.5, None, ALU.mult).then_inc(quant_step, 1)
            dve.tensor_scalar(nhalf[:], scale[:], -0.5, None, ALU.mult).then_inc(quant_step, 1)
            dve.wait_ge(quant_step, 3)
            for i in range(3):
                low = M[:].rearrange("p u t -> p (u t)") if i % 2 else X[:].rearrange("p u t -> p (u t)")
                dve.tensor_scalar(low, raw[:, i, :], nhalf[:, i:i + 1], None, ALU.is_lt).then_inc(quant_step, 1)
                dve.wait_ge(quant_step, 4 + i)
                dve.scalar_tensor_tensor(out=raw[:, i, :], in0=raw[:, i, :], scalar=half[:, i:i + 1], in1=low,
                                         op0=ALU.is_gt, op1=ALU.subtract).then_inc(digits_ready, 1)
                dve.wait_ge(digits_ready, i + 1)
            dve.wait_ge(acc_done, 4 * NP)
            layer_stats(x1_step, 0, lambda u: attn_out[:, u, :], NU, 2)
            for u in range(NU):
                ins = dve.tensor_scalar(attn_out[:, u, :], attn_out[:, u, :], mv[:, u, 0:1], rstd[:, u:u + 1],
                                        ALU.subtract, ALU.mult)
            ins.then_inc(x1_step, 1)
            dve.wait_ge(x1_step, 3)
            dve.tensor_tensor(x_sb[:], x_sb[:], attn_out[:], ALU.add).then_inc(x1_step, 1)
            dve.wait_ge(x1_step, 4)
            layer_stats(x1_step, 4, lambda u: x_sb[:, u, :], NU, 3)
            for u in range(NU):
                dve.tensor_scalar(xn_v[:, u, :], x_sb[:, u, :], mv[:, u, 0:1], rstd[:, u:u + 1],
                                  ALU.subtract, ALU.mult).then_inc(xn2_ready, 1)
            dve.tensor_tensor(half[:, 0:1], scale[:, 1:2], scale[:, 2:3], ALU.mult).then_inc(fin_step, 1)
            for i in range(2 * ET):
                dve.wait_ge(silu_up, i + 1)
                if i == 0:
                    dve.wait_ge(xn2T_filled, 4)
                if i >= 2:
                    dve.wait_ge(down_filled, i - 1)
                dve.tensor_tensor(og[:, i % 2], four(proj[2 * (i % 2) + 1]),
                                  conv[:, i % 2, :].rearrange("p (a b) -> p a b", a=4),
                                  ALU.mult).then_inc(hid_ready, 1)
            y2 = attn_out
            for t in range(2):
                dve.wait_ge(down_filled, ET * (t + 1))
                dve.wait_ge(fin_step, 1 + 3 * t)
                for b in range(2):
                    ins = dve.tensor_scalar(y2[:, 4 * t + 2 * b:4 * t + 2 * b + 2, :],
                                            work[2 * t + b][:].rearrange("p (a b) -> p a b", a=2),
                                            half[:, 0:1], None, ALU.mult)
                ins.then_inc(fin_step, 1)
                dve.wait_ge(fin_step, 2 + 3 * t)
                for j in range(4):
                    ins = dve.bn_stats(stats[:, 4 * t + j, :], y2[:, 4 * t + j, :])
                ins.then_inc(fin_step, 1)
                dve.wait_ge(fin_step, 3 + 3 * t)
                for j in range(4):
                    ins = dve.bn_aggr(mv[:, 4 * t + j, :], stats[:, 4 * t + j, :])
                ins.then_inc(fin_step, 1)
                dve.wait_ge(fin_step, 4 + 3 * t)
                inverse_root(4 * t, 4 * t + 4, 4 + t)
                for j in range(4):
                    u = 4 * t + j
                    dve.tensor_scalar(y2[:, u, :], y2[:, u, :], mv[:, u, 0:1], rstd[:, u:u + 1],
                                      ALU.subtract, ALU.mult).then_inc(x1_step, 1)
                for j in range(4):
                    u = 4 * t + j
                    dve.wait_ge(x1_step, 6 + u + 1)
                    dve.tensor_tensor(x_sb[:, u, :], x_sb[:, u, :], y2[:, u, :], ALU.add).then_inc(fin_ready, 1)


_INS = ["L0_attn_hidden_states", "L0_attn_W_qkvz", "L0_attn_W_ba", "L0_attn_conv_weight", "L0_attn_dt_bias",
        "L0_attn_A_log", "L0_attn_norm_weight", "L0_attn_W_out", "L0_ffn_W_up", "L0_ffn_W_gate", "L0_ffn_W_down"]


def kernel(**inputs):
    import numpy as np
    import concourse.bacc as bacc
    from concourse import mybir as mb
    from concourse.bass_utils import run_bass_kernel_spmd

    nc = bacc.Bacc("TRN2", target_bir_lowering=False, num_devices=1)
    arrays, args = {}, []
    for name in _INS:
        a = np.ascontiguousarray(inputs[name])
        arrays[f"in_{name}"] = a
        args.append(nc.dram_tensor(f"in_{name}", a.shape, mb.dt.from_np(a.dtype), kind="ExternalInput").ap())
    shape = inputs[_INS[0]].shape
    out = nc.dram_tensor("out_0", shape, mb.dt.float32, kind="ExternalOutput").ap()
    sandwich(nc, *args, out)
    got = run_bass_kernel_spmd(nc, [arrays], core_ids=[0])
    return got.results[0]["out_0"]
```

```python
from contextlib import ExitStack

import concourse.bass as bass
from concourse import mybir

F32 = mybir.dt.float32
F32R = mybir.dt.float32r
ALU = mybir.AluOpType
ACT = mybir.ActivationFunctionType
AX = mybir.AxisListType

P = 128
T, D = 1024, 256
KT = D // P
NH, DH = 16, 128
NU = T // P
SEG = 256
NP = NH // 2
NB16 = P // 16
E = 1024
ET = E // P
LN_EPS, L2_EPS, RMS_EPS, Q_EPS = 1e-5, 1e-6, 1e-6, 1e-8

K_, Q_, V_ = 0, 1, 2
W_COL = {K_: DH, Q_: 0, V_: 2 * DH}
CONV_S = {K_: 1, Q_: 0, V_: 2}

PREP = {}
for g in range(4):
    PREP["kT", g] = 2 * g
    PREP["qT", g] = 2 * g + 1
    PREP["gram", g, 0] = 8 + 2 * g
    PREP["gram", g, 1] = 9 + 2 * g
    PREP["vT", g] = 16 + g
SOLVE = {}
for g in range(4):
    SOLVE["z", g] = g
    for lv in range(2):
        SOLVE["LM", lv, g] = 4 + 12 * lv + g
        SOLVE["MY", lv, g] = 8 + 12 * lv + 2 * g
        SOLVE["YX", lv, g] = 9 + 12 * lv + 2 * g
    SOLVE["LM", 2, g] = 28 + g
    SOLVE["MY", 2, g] = 32 + g
for h in range(2):
    for at, name in ((36, "y_even"), (38, "state"), (40, "kS"), (42, "o_even"), (44, "y_odd"),
                     (46, "oT_even"), (48, "o_odd"), (50, "out_even"), (52, "oT_odd"), (54, "out_odd")):
        SOLVE[name, h] = at + h
MIXED = [("proj", 0), ("z", 0), ("proj", 1), ("z", 1), ("silu", 0), ("proj", 2), ("z", 2), ("silu", 1), ("z", 3),
         ("proj", 3), ("silu", 2)]
for lv in range(3):
    MIXED += [("LM", lv, g) for g in range(4)]
    if lv == 0:
        MIXED += [("silu", 3)]
    for g in range(4):
        MIXED += [("MY", lv, g)] + ([("YX", lv, g)] if lv < 2 else [])
        if lv < 2 and g % 2:
            MIXED += [("abs", 2 * lv + g // 2)]
N_PREP, N_SOLVE = len(PREP), len(SOLVE)
N_TURNS = N_PREP + N_SOLVE
assert N_PREP % 4 == 0 and N_SOLVE % 4 == 0


def turn_of(phase, key):
    return (PREP if phase == "prep" else SOLVE)[key]


def bank_of(phase, key):
    return turn_of(phase, key) % 4


def filled_at(phase, n, key):
    return n * N_TURNS + ((0 if phase == "prep" else N_PREP) + turn_of(phase, key) + 1)


def before(phase, n, key):
    t = turn_of(phase, key) - 4
    if t < 0 and phase == "prep":
        phase, n, t = "solve", n - 1, t + N_SOLVE
        if isinstance(n, int) and n < 0:
            return None
    elif t < 0:
        phase, t = "prep", t + N_PREP
    table = PREP if phase == "prep" else SOLVE
    return phase, n, next(k for k, v in table.items() if v == t)


def tap_at(n, turn, tap):
    return n * 36 + (6 * (turn // 2) + 2 * tap + turn % 2 + 1)


def wait(eng, sem, value):
    if isinstance(value, int) and value <= 0:
        return
    eng.wait_ge(sem, value)


def m_blocks(lv):
    s = 16 << lv
    return [(a, a + s, a + s, a + 2 * s) for a in range(0, P, 2 * s)]


def x_blocks(lv):
    s = 16 << lv
    if s == 16:
        return [(a, a + 32, a, a + 16) for a in range(0, P, 32)]
    return [(a + s, a + 2 * s, a, a + s) for a in range(0, P, 2 * s)]


N_INV = 31
N_PREP_STEP = 2 * 2


def sandwich(nc, x, W_qkvz, W_ba, conv_w, dt_bias, A_log, norm_w, W_out, W_up, W_gate, W_down, out):
    x_t = x.rearrange("b s d -> (b s) d").rearrange("(u p) d -> p u d", p=P)
    out_t = out.rearrange("b s d -> (b s) d").rearrange("(u p) d -> p u d", p=P)
    wq_d = W_qkvz.rearrange("(k p) (n h c) -> n p k h c", p=P, n=NP, h=2)
    wout_d = W_out.rearrange("(n h p) d -> n p h d", n=NP, h=2)
    conv_d = conv_w.rearrange("(s n h p) t -> n p s h t", s=3, n=NP, h=2)
    gc_d = nc.dram_tensor("gc_rows", (NH, T), F32, kind="Internal").ap()
    blk_out_d = nc.dram_tensor("l_blocks", (2 * NU, NB16, 16, 16), F32, kind="Internal").ap()
    blk_in_d = nc.dram_tensor("x_blocks", (2, 2 * NU, NB16, 16, 16), F32, kind="Internal").ap()

    with ExitStack() as ctx:
        place = {}

        def sb(name, shape, dtype=F32):
            place[name] = -(-nc.sbuf_base // 32) * 32
            return ctx.enter_context(nc.sbuf_tensor(name, shape, dtype))

        def over(name, under, shape, dtype):
            return nc.alloc_sbuf_tensor_at(name, shape, dtype, offset=place[under])

        def sem(name):
            return ctx.enter_context(nc.semaphore(name))

        x_sb = sb("x_sb", [P, NU, D])
        xT_hi = sb("xT_hi", [P, KT, T], F32R)
        xT_lo = over("xT_lo", "x_sb", [P, KT, T], F32R)
        attn_out = sb("attn_out", [P, NU, D])
        ident = sb("ident", [P, P])
        strict = sb("strict", [P, P])
        upper = sb("upper", [P, P])
        ones = sb("ones", [P, P])
        w_qkv = sb("w_qkv", [P, KT, 2, 3 * DH])
        w_z = sb("w_z", [P, KT, 2, DH])
        wq_hi = sb("wq_hi", [P, KT, 2, 3 * DH], F32R)
        wq_lo = over("wq_lo", "w_qkv", [P, KT, 2, 3 * DH], F32R)
        wz_hi = sb("wz_hi", [P, KT, 2, DH], F32R)
        wz_lo = over("wz_lo", "w_z", [P, KT, 2, DH], F32R)
        w_conv = sb("w_conv", [P, 3, 2, 4])
        w_o = sb("w_o", [P, 2, D])
        nw = sb("nw", [P, 1])
        wba = sb("wba", [P, KT, 2 * NH])
        alog = sb("alog", [NH, 1])
        dtb = sb("dtb", [NH, 1])
        conv = sb("conv", [P, 4, 512])
        chan = sb("chan", [P, 2, 3, T])
        decays = sb("decays", [P, 3, 2 * T])
        gcb = decays[:, 0, :].rearrange("p (h t) -> p h t", h=2)
        Wd = decays[:, 1, :].rearrange("p (u t) -> p u t", t=P)
        Wi = decays[:, 2, :].rearrange("p (u t) -> p u t", t=P)
        cols_all = sb("cols_all", [P, NH, 3, NU])
        cols = sb("cols", [P, 2, 3, NU])
        eg = gcb.rearrange("p h (u t) -> p h u t", t=P)[:, :, 1::2, :]
        sq = sb("sq", [P, 4, 512])
        ss = sb("ss", [P, 16])
        sst = sb("sst", [P, 16])
        rt = sb("rt", [P, 16])
        rs = sb("rs", [P, 16])
        negc = sb("negc", [P, 16])
        fk = sb("fk", [P, 16])
        ssq = sb("ssq", [P, 16])
        qe = sb("qe", [P, 16])
        zs = sb("zs", [P, 16, P])
        kd = sb("kd", [P, 2, 4, P])
        kp = sb("kp", [P, 2, 4, P])
        qp = sb("qp", [P, 2, 4, P])
        vt = sb("vt", [P, 16, P])
        Lneg = sb("Lneg", [P, 16, P])
        attnT = sb("attnT", [P, 16, P])
        lb_prod = sb("lb_prod", [P, 2, 16, 16])
        lb = lb_prod[:, 0]
        prod = lb_prod[:, 1].rearrange("p r c -> p (r c)")
        xm = sb("xm", [P, 2, 16, 16])
        xc = lb_prod
        diag16 = sb("diag16", [P, NB16, 16])
        M = sb("M", [P, 16, P])
        X = sb("X", [P, 16, P])
        Y = sb("Y", [P, 16, P])
        ye = sb("ye", [P, 2, 4, P])
        yo = sb("yo", [P, 2, 4, P])
        S = sb("S", [P, 2, 4, P])
        og = sb("og", [P, 4, 4, P])
        oT = [t[:, h].rearrange("p a b -> p (a b)") for t in (ye, yo) for h in range(2)]
        sso = sb("sso", [P, 4, 4])
        rms = sb("rms", [P, 4, 4])
        fac = sb("fac", [P, 4, 4])
        stats = sb("stats", [P, NU, 6])
        mv = sb("mv", [P, NU, 2])
        rstd = sb("rstd", [P, NU])
        lnk = sb("lnk", [P, 16])
        lno = sb("lno", [P, 4, 4])
        lnv = sb("lnv", [P, NU])
        raw = decays
        asum = sb("asum", [P, 3])
        scale = sb("scale", [P, 3])
        half = sb("half", [P, 3])
        nhalf = sb("nhalf", [P, 3])
        xn = og
        xn_v = og[:].rearrange("p a b c -> p (a b c)").rearrange("p (u d) -> p u d", d=D)
        xnT = M[:].rearrange("p a b -> p (a b)").rearrange("p (k t) -> p k t", k=KT)
        wT = over("wT", "chan", [P, 3, 2 * E], F32R)
        x2T_lo = over("x2T_lo", "X", [P, KT, T], F32R)
        hid_hi = over("hid_hi", "og", [P, 4, 512], F32R)
        hid_lo = over("hid_lo", "sq", [P, 4, 512], F32R)
        beta_r = Wd[0:NH, 0:8, :].rearrange("p a b -> p (a b)")
        t1_r = Wd[0:NH, 8:16, :].rearrange("p a b -> p (a b)")
        sp_r = Wi[0:NH, 0:8, :].rearrange("p a b -> p (a b)")
        g_r = Wi[0:NH, 8:16, :].rearrange("p a b -> p (a b)")
        gc_r = vt[0:NH, 0:8, :].rearrange("p a b -> p (a b)")
        ngc_r = vt[0:NH, 8:16, :].rearrange("p a b -> p (a b)")
        egl_r = zs[0:NH, 0:8, :].rearrange("p a b -> p (a b)")
        dif_r = zs[0:NH, 8:16, :].rearrange("p a b -> p (a b)")
        expA = sb("expA", [NH, 1])

        proj = [ctx.enter_context(nc.psum_tensor(f"proj{i}", [P, 512], F32)) for i in range(4)]
        work = [ctx.enter_context(nc.psum_tensor(f"work{i}", [P, 512], F32)) for i in range(4)]

        x_loaded, small_loaded, ffn_loaded = sem("x_loaded"), sem("small_loaded"), sem("ffn_loaded")
        wqkv_loaded, conv_loaded, wz_loaded, wo_loaded = (sem("wqkv_loaded"), sem("conv_loaded"),
                                                          sem("wz_loaded"), sem("wo_loaded"))
        gcb_loaded, cols_loaded = sem("gcb_loaded"), sem("cols_loaded")
        gc_stored, l_stored, l_loaded = sem("gc_stored"), sem("l_stored"), sem("l_loaded")
        x_stored, m_stored, out_stored = sem("x_stored"), sem("m_stored"), sem("out_stored")
        xc_loaded, mc_loaded, x_spread, m_spread = (sem("xc_loaded"), sem("mc_loaded"), sem("x_spread"),
                                                    sem("m_spread"))
        consts_step, consts_ready = sem("consts_step"), sem("consts_ready")
        ln_step, xn_ready, xnT_filled, xnT_ready = (sem("ln_step"), sem("xn_ready"), sem("xnT_filled"),
                                                    sem("xnT_ready"))
        xT_hi_ready, xT_split, wq_hi_ready, wq_split, wz_hi_ready, wz_split = (
            sem("xT_hi_ready"), sem("xT_split"), sem("wq_hi_ready"), sem("wq_split"), sem("wz_hi_ready"),
            sem("wz_split"))
        ba_filled, rows_act, rows_dve, rows_ready = (sem("ba_filled"), sem("rows_act"), sem("rows_dve"),
                                                     sem("rows_ready"))
        colsT_filled, colsT_ready = sem("colsT_filled"), sem("colsT_ready")
        proj_filled, tap3_done, taps_done, silu_done = (sem("proj_filled"), sem("tap3_done"),
                                                        sem("taps_done"), sem("silu_done"))
        work_filled = sem("work_filled")
        z_ready, eg_ready, abs_done, w_ready, sq_ready, sq_read = (
            sem("z_ready"), sem("eg_ready"), sem("abs_done"), sem("w_ready"), sem("sq_ready"), sem("sq_read"))
        prep_step, negc_ready, kd_ready, masked, scaled, kq_ready = (
            sem("prep_step"), sem("negc_ready"), sem("kd_ready"), sem("masked"), sem("scaled"), sem("kq_ready"))
        l_ready, vt_ready, inv_step = sem("l_ready"), sem("vt_ready"), sem("inv_step")
        y_ready, m_ready, xj_ready = sem("y_ready"), sem("m_ready"), sem("xj_ready")
        ye_ready, s_ready, r_ready, yo_ready = sem("ye_ready"), sem("s_ready"), sem("r_ready"), sem("yo_ready")
        sqo_ready, sqo_read, rms_ready, og_ready, oT_ready, acc_done = (
            sem("sqo_ready"), sem("sqo_read"), sem("rms_ready"), sem("og_ready"), sem("oT_ready"),
            sem("acc_done"))
        fk_ready, qe_ready = sem("fk_ready"), sem("qe_ready")
        lnk_done, rs_ready, lno_done, fac_ready = (sem("lnk_done"), sem("rs_ready"), sem("lno_done"),
                                                   sem("fac_ready"))
        var_ready, lnv_done, rstd_ready = sem("var_ready"), sem("lnv_done"), sem("rstd_ready")
        asum_ready, total_filled, quant_step, digits_ready = (
            sem("asum_ready"), sem("total_filled"), sem("quant_step"), sem("digits_ready"))
        wT_filled, wT_ready = sem("wT_filled"), sem("wT_ready")
        x1_step, xn2_ready, xn2T_filled, xn2T_ready = (sem("x1_step"), sem("xn2_ready"),
                                                       sem("xn2T_filled"), sem("xn2T_ready"))
        x2_hi_ready, hid_hi_ready, hid_made = sem("x2_hi_ready"), sem("hid_hi_ready"), sem("hid_made")
        up_filled, silu_up, hid_ready, down_filled = (sem("up_filled"), sem("silu_up"), sem("hid_ready"),
                                                      sem("down_filled"))
        fin_step, fin_ready = sem("fin_step"), sem("fin_ready")

        def four(ap):
            return ap[:].rearrange("p (a b) -> p a b", a=4)

        def units(g):
            return slice(4 * g, 4 * g + 4)

        def odd_units(t, h):
            return t[:, 8 * h + 1:8 * h + 8:2, :]

        block = ctx.enter_context(nc.Block())

        @block.sync
        def _(sp):
            sp.dma_start(x_sb[:], x_t).then_inc(x_loaded, 16)
            sp.dma_start(wba[:], W_ba.rearrange("(k p) c -> p k c", p=P)).then_inc(small_loaded, 16)
            sp.dma_start(alog[:], A_log.rearrange("(h a) -> h a", a=1)).then_inc(small_loaded, 16)
            sp.dma_start(dtb[:], dt_bias.rearrange("(h a) -> h a", a=1)).then_inc(small_loaded, 16)
            sp.dma_start(nw[:], norm_w.rearrange("(h a) -> h a", a=1)).then_inc(small_loaded, 16)

            def pick(view, n):
                if isinstance(n, int):
                    return view[n]
                v = view[bass.ds(n, 1)]
                names = " ".join("abcdef"[:len(view.shape) - 1])
                return v.rearrange(f"n {names} -> (n a) {names[2:]}")

            def constant_wait():
                sp.wait_ge(x_loaded, 16)

            def load_qkv(n):
                constant_wait()
                wait(sp, proj_filled, n * 12)
                for k in range(KT):
                    sp.dma_start(w_qkv[:, k], pick(wq_d[:, :, k, :, 0:3 * DH], n)).then_inc(wqkv_loaded, 16)
                constant_wait()
                wait(sp, taps_done, n * 36)
                for s in range(3):
                    sp.dma_start(w_conv[:, s], pick(conv_d[:, :, s], n)).then_inc(conv_loaded, 16)

            def load_z(n):
                constant_wait()
                wait(sp, z_ready, n * 4)
                for k in range(KT):
                    sp.dma_start(w_z[:, k], pick(wq_d[:, :, k, :, 3 * DH:4 * DH], n)).then_inc(wz_loaded, 16)

            def load_gates(n):
                constant_wait()
                wait(sp, kq_ready, n * 2)
                if isinstance(n, int):
                    rows = gc_d[2 * n:2 * n + 2, :]
                    pair = cols_all[:, 2 * n:2 * n + 2]
                else:
                    rows = gc_d[bass.ds(n * 2, 2), :]
                    pair = cols_all[:, bass.ds(n * 2, 2)]
                sp.dma_start(gcb, rows.partition_broadcast(P)).then_inc(gcb_loaded, 16)
                constant_wait()
                wait(sp, vt_ready, n * 4)
                sp.dma_start(cols[:], pair).then_inc(cols_loaded, 16)

            def blocks_out(m, n):
                sp.wait_ge(l_ready, n * 8)
                for b in range(NB16):
                    sp.dma_start(blk_out_d[:, b].rearrange("u r c -> r u c"),
                                 Lneg[16 * b:16 * b + 16, :, 16 * b:16 * b + 16]).then_inc(l_stored, 16)
                sp.wait_ge(l_stored, n * (16 * NB16))
                sp.dma_start(lb, blk_out_d.rearrange("u b r c -> (u b) r c")).then_inc(l_loaded, 16)

            def blocks_in(m, n):
                sp.wait_ge(inv_step, n * N_INV)
                for i, stored in ((1, m_stored), (0, x_stored)):
                    sp.dma_start(blk_in_d[i].rearrange("u b r c -> (u b) (r c)"),
                                 xm[:, i].rearrange("p r c -> p (r c)")).then_inc(stored, 16)
                for i, stored, loaded in ((1, m_stored, mc_loaded), (0, x_stored, xc_loaded)):
                    sp.wait_ge(stored, n * 16)
                    sp.dma_start(xc[:, i], blk_in_d[i].rearrange("u b r c -> (b r) u c")).then_inc(loaded, 16)

            def load_wo(m, n):
                sp.dma_start(w_o[:], pick(wout_d, m)).then_inc(wo_loaded, 16)

            load_qkv(0)
            sp.wait_ge(rows_dve, 12)
            sp.dma_start(gc_d, gc_r).then_inc(gc_stored, 16)
            sp.wait_ge(gc_stored, 16)
            sp.wait_ge(colsT_ready, 1)
            load_gates(0)
            load_z(0)
            load_qkv(1)

            def body(n, more):
                blocks_out(n - 1, n)
                load_gates(n)
                blocks_in(n - 1, n)
                load_wo(n - 1, n)
                load_z(n)
                if more:
                    load_qkv(n + 1)

            with sp.Fori(1, NP - 1) as n:
                body(n, True)
            body(NP - 1, False)
            blocks_out(NP - 1, NP)
            blocks_in(NP - 1, NP)
            load_wo(NP - 1, NP)
            sp.wait_ge(kq_ready, 2 * NP)
            for i, w in enumerate((W_up, W_gate)):
                sp.dma_start(raw[:, i].rearrange("p (t d) -> p t d", d=D),
                             w.rearrange("(t p) d -> p t d", p=P)).then_inc(ffn_loaded, 16)
            sp.dma_start(raw[:, 2].rearrange("p (a e) -> p a e", e=E),
                         W_down.rearrange("(a p) e -> p a e", p=P)).then_inc(ffn_loaded, 16)
            sp.wait_ge(z_ready, 4 * NP)
            sp.dma_start(x_sb[:], x_t).then_inc(x_loaded, 16)
            for u in range(NU):
                sp.wait_ge(fin_ready, u + 1)
                sp.dma_start(out_t[:, u, :], x_sb[:, u, :]).then_inc(out_stored, 16)
            sp.wait_ge(out_stored, 16 * NU)

        @block.gpsimd
        def _(pool):
            def select(t, ap, base, pattern, mult, op, fill):
                pool.affine_select(out=ap, in_=ap, compare_op=op, fill=fill, base=base, pattern=pattern,
                                   channel_multiplier=mult).then_inc(consts_ready, 1)

            pool.memset(ident[:], 0.0).then_inc(consts_step, 1)
            pool.memset(ones[:], 1.0).then_inc(consts_ready, 1)
            pool.memset(strict[:], 1.0).then_inc(consts_step, 1)
            pool.memset(upper[:], 1.0).then_inc(consts_step, 1)
            pool.memset(Y[:], 0.0).then_inc(consts_step, 1)
            pool.memset(diag16[:], 1.0).then_inc(consts_step, 1)
            pool.memset(xm[:], 0.0).then_inc(consts_step, 1)
            pool.memset(attn_out[:], 0.0).then_inc(consts_ready, 1)
            pool.wait_ge(consts_step, 6)
            select(ident, ident[:], 0, [[-1, P]], 1, ALU.not_equal, 1.0)
            select(strict, strict[:], 0, [[-1, P]], 1, ALU.is_gt, 0.0)
            select(upper, upper[:], 0, [[1, P]], -1, ALU.is_ge, 0.0)
            select(Y, Y[:], 0, [[0, 16], [-1, P]], 1, ALU.not_equal, 1.0)
            select(xm, xm[:], 0, [[0, 2], [-1, 16], [1, 16]], 0, ALU.not_equal, 1.0)

            select(diag16, diag16[:], 0, [[-16, NB16], [0, 16]], 1, ALU.is_ge, 0.0)
            pool.wait_ge(consts_ready, 8)
            select(diag16, diag16[:], 15, [[16, NB16], [0, 16]], -1, ALU.is_ge, 0.0)

            def spread(m):
                pool.wait_ge(xc_loaded, m * 16 + 16)
                for g in range(4):
                    pool.tensor_tensor(X[:, units(g), :].rearrange("p u (b c) -> p u b c", c=16),
                                       xc[:, 0, units(g), :].unsqueeze(2).broadcast_to([P, 4, NB16, 16]),
                                       diag16[:].unsqueeze(1).broadcast_to([P, 4, NB16, 16]),
                                       ALU.mult).then_inc(x_spread, 1)

            def one_of(w):
                return ones[:, 0:1].unsqueeze(2).broadcast_to([P, 2, w.shape[-1]])

            def split_qkv(n):
                for k in range(KT):
                    pool.wait_ge(wqkv_loaded, n * (16 * KT) + 16 * KT)
                    pool.tensor_tensor(wq_hi[:, k], w_qkv[:, k], one_of(w_qkv),
                                       ALU.mult).then_inc(wq_hi_ready, 1)
                    pool.wait_ge(wq_hi_ready, n * KT + (k + 1))
                    pool.tensor_tensor(wq_lo[:, k], w_qkv[:, k], wq_hi[:, k].bitcast(F32),
                                       ALU.subtract).then_inc(wq_split, 1)

            def split_z(n):
                for k in range(KT):
                    pool.wait_ge(wz_loaded, n * (16 * KT) + 16 * KT)
                    pool.tensor_tensor(wz_hi[:, k], w_z[:, k], one_of(w_z),
                                       ALU.mult).then_inc(wz_hi_ready, 1)
                    pool.wait_ge(wz_hi_ready, n * KT + (k + 1))
                    pool.tensor_tensor(wz_lo[:, k], w_z[:, k], wz_hi[:, k].bitcast(F32),
                                       ALU.subtract).then_inc(wz_split, 1)

            def masks(n):
                wait(pool, l_ready, n * 8)
                for g in range(4):
                    pool.wait_ge(w_ready, n * 4 + (g + 1))
                    w4 = Wd[:, units(g), :]
                    pool.tensor_tensor(Wi[:, units(g), :], w4, upper[:].unsqueeze(1).broadcast_to([P, 4, P]),
                                       ALU.mult).then_inc(masked, 1)
                    pool.wait_ge(masked, n * 8 + (2 * g + 1))
                    pool.tensor_tensor(w4, w4, strict[:].unsqueeze(1).broadcast_to([P, 4, P]),
                                       ALU.mult).then_inc(masked, 1)

            def prepare(n):
                for g in range(4):
                    w4 = Wd[:, units(g), :]
                    pool.wait_ge(negc_ready, n * 2 + (g // 2 + 1))
                    pool.wait_ge(masked, n * 8 + (2 * g + 2))
                    pool.tensor_tensor(w4, w4, negc[:, units(g)].unsqueeze(2).broadcast_to([P, 4, P]),
                                       ALU.mult).then_inc(scaled, 1)
                wait(pool, work_filled, filled_at("solve", n - 1, ("o_odd", 1)))
                for h in range(2):
                    pool.wait_ge(eg_ready, n * 2 + (h + 1))
                    pool.wait_ge(silu_done, n * 12 + (4 + 6 * h))
                    for s, t in ((K_, kp), (Q_, qp)):
                        src = chan[:, h, s, :].rearrange("p (u t) -> p u t", t=P)[:, 1::2, :]
                        ins = pool.tensor_tensor(t[:, h], src, eg[:, h], ALU.mult)
                    ins.then_inc(kq_ready, 1)

            pool.wait_ge(consts_ready, 9)
            def body(n, more):
                spread(n - 1)
                masks(n)
                split_z(n)
                if more:
                    split_qkv(n + 1)
                prepare(n)

            split_qkv(0)
            masks(0)
            split_z(0)
            split_qkv(1)
            prepare(0)
            with pool.Fori(1, NP - 1) as n:
                body(n, True)
            body(NP - 1, False)
            spread(NP - 1)

        @block.tensor
        def _(pe):
            read_by = {}
            for g in range(4):
                read_by["z", g] = [(z_ready, 4, g + 1)]
                read_by["kT", g] = [(kd_ready, 4, g + 1)]
                read_by["qT", g] = [(sq_ready, 8, 2 * g + 2)]
                read_by["vT", g] = [(vt_ready, 4, g + 1)]
                for t in range(2):
                    read_by["gram", g, t] = [(l_ready, 8, 2 * g + t + 1)]
                for lv in range(3):
                    read_by["LM", lv, g] = [(y_ready, 12, 4 * lv + g + 1)]
                    read_by["MY", lv, g] = [(m_ready, 12, 4 * lv + g + 1)]
                    read_by["YX", lv, g] = [(xj_ready, 8, 4 * lv + g + 1)]
            for h in range(2):
                read_by["y_even", h] = [(ye_ready, 2, h + 1)]
                read_by["state", h] = [(s_ready, 2, h + 1)]
                read_by["kS", h] = [(r_ready, 2, h + 1)]
                read_by["y_odd", h] = [(yo_ready, 2, h + 1)]
                for par, name in enumerate(("even", "odd")):
                    read_by["o_" + name, h] = [(sqo_ready, 4, 2 * par + h + 1), (og_ready, 4, 2 * par + h + 1)]
                    read_by["oT_" + name, h] = [(oT_ready, 4, 2 * par + h + 1)]
                    read_by["out_" + name, h] = [(acc_done, 4, 2 * par + h + 1)]

            def bank(phase, n, key, met=None):
                earlier = before(phase, n, key)
                if earlier is not None:
                    for done, per, count in read_by[earlier[2]]:
                        if done is not met:
                            pe.wait_ge(done, earlier[1] * per + count)
                return work[bank_of(phase, key)]

            def split_product(ps, terms):
                for i, (a, b) in enumerate(terms):
                    ins = pe.matmul(ps, a, b, start=(i == 0), stop=(i == len(terms) - 1))
                return ins

            def project(n, p):
                if p == 0:
                    pe.wait_ge(wq_split, n * KT + KT)
                h, s = p // 3, p % 3
                for t in range(2):
                    turn = 2 * p + t
                    if turn >= 4:
                        pe.wait_ge(taps_done, tap_at(n, turn - 4, 2))
                    elif not (isinstance(n, int) and n == 0):
                        pe.wait_ge(taps_done, tap_at(n, turn + 8, 2) - 36)
                    c = W_COL[s]
                    ins = split_product(proj[turn % 4][:],
                                        [(w[:, k, h, c:c + DH], x[:, k, 512 * t:512 * t + 512])
                                         for k in range(KT)
                                         for w, x in ((wq_lo, xT_hi), (wq_hi, xT_lo), (wq_hi, xT_hi))])
                    ins.then_inc(proj_filled, 1)

            def z_product(m, g):
                if g == 0:
                    pe.wait_ge(wz_split, m * KT + KT)
                ps = bank("solve", m, ("z", g))
                for j in range(2):
                    u = 2 * g + j
                    ins = split_product(ps[:, j * 2 * DH:(j + 1) * 2 * DH],
                                        [(x[:, k, u * P:(u + 1) * P], w[:, k].rearrange("p h c -> p (h c)"))
                                         for k in range(KT)
                                         for x, w in ((xT_lo, wz_hi), (xT_hi, wz_lo), (xT_hi, wz_hi))])
                ins.then_inc(work_filled, 1)

            def prepare(n):
                def turned(name, s, g):
                    ps = bank("prep", n, (name, g))
                    for j in range(4):
                        u = 4 * (g % 2) + j
                        ins = pe.transpose(ps[:, j * P:(j + 1) * P], chan[:, g // 2, s, u * P:(u + 1) * P],
                                           ident[:])
                    ins.then_inc(work_filled, 1)

                for g in range(4):
                    pe.wait_ge(silu_done, n * 12 + (4 + 6 * (g // 2)))
                    turned("kT", K_, g)
                    turned("qT", Q_, g)
                for g in range(4):
                    for t in range(2):
                        ps = bank("prep", n, ("gram", g, t))
                        for j in range(2):
                            u = 4 * (g % 2) + 2 * t + j
                            ins = pe.matmul(ps[:, j * 2 * P:(j + 1) * 2 * P],
                                            chan[:, g // 2, K_, u * P:(u + 1) * P],
                                            chan[:, g // 2, K_:V_, u * P:(u + 1) * P], start=True, stop=True)
                        ins.then_inc(work_filled, 1)
                for g in range(4):
                    pe.wait_ge(silu_done, n * 12 + (6 + 6 * (g // 2)))
                    turned("vT", V_, g)

            def product(n, key, terms, met=None):
                ps = bank("solve", n, key, met)
                for j in range(4):
                    ts = terms(j)
                    for i, (a, b) in enumerate(ts):
                        ins = pe.matmul(ps[:, j * P:(j + 1) * P], a, b, start=(i == 0), stop=(i == len(ts) - 1))
                ins.then_inc(work_filled, 1)

            def join(m, key):
                name, lv, g = key
                if name == "LM":
                    if lv:
                        pe.wait_ge(m_ready, m * 12 + (4 * (lv - 1) + g + 1))
                    else:
                        pe.wait_ge(m_spread, m * 4 + (g + 1))
                    product(m, key, lambda j: [(Lneg[:, 4 * g + j, :], M[:, 4 * g + j, :])])
                elif name == "MY":
                    pe.wait_ge(y_ready, m * 12 + (4 * lv + g + 1))
                    if lv:
                        pe.wait_ge(xj_ready, m * 8 + (4 * (lv - 1) + g + 1))
                    else:
                        pe.wait_ge(x_spread, m * 4 + (g + 1))
                    product(m, key, lambda j: [(X[:, 4 * g + j, :], Y[:, 4 * g + j, :])])
                else:
                    product(m, key, lambda j: [(Y[:, 4 * g + j, :], X[:, 4 * g + j, :])])

            def mixed(n, m):
                for step in MIXED:
                    if step[0] == "proj":
                        if n is not None:
                            project(n, step[1])
                    elif step[0] in ("silu", "abs") or m is None:
                        pass
                    elif step[0] == "z":
                        z_product(m, step[1])
                    else:
                        join(m, step)

            def ffn_total():
                pe.wait_ge(asum_ready, 3)
                pe.wait_ge(taps_done, 36 * NP)
                pe.matmul(proj[0][:, 0:3], ones[:], asum[:], start=True, stop=True).then_inc(total_filled, 1)

            def digits_turned():
                for i in range(3):
                    pe.wait_ge(digits_ready, i + 1)
                    for q in range(4):
                        turn = 4 * i + q
                        if turn >= 4:
                            pe.wait_ge(wT_ready, turn - 3)
                        for j in range(4):
                            if i < 2:
                                src = raw[:, i, (4 * (q % 2) + j) * D + (q // 2) * P:][:, 0:P]
                            else:
                                src = raw[:, i, (j % 2) * E + (2 * q + j // 2) * P:][:, 0:P]
                            ins = pe.transpose(proj[q][:, j * P:(j + 1) * P], src, ident[:])
                        ins.then_inc(wT_filled, 1)

            def solve(m, n):
                def turned(name, par):
                    for h in range(2):
                        pe.wait_ge(og_ready, m * 4 + (2 * par + h + 1))
                        ps = bank("solve", m, (name, h))
                        for j in range(4):
                            ins = pe.transpose(ps[:, j * P:(j + 1) * P], og[:, 2 * par + h, j, :], ident[:])
                        ins.then_inc(work_filled, 1)

                def output(name, par):
                    pe.wait_ge(oT_ready, m * 4 + (2 * par + 2))
                    for t in range(2):
                        ps = bank("solve", m, (name, t), oT_ready)
                        for j in range(2):
                            for h in range(2):
                                at = (2 * t + j) * P
                                ins = pe.matmul(ps[:, j * D:(j + 1) * D], oT[2 * par + h][:, at:at + P],
                                                w_o[:, h, :], start=(h == 0), stop=(h == 1))
                        ins.then_inc(work_filled, 1)

                for h in range(2):
                    pe.wait_ge(m_ready, m * 12 + (10 + 2 * h))
                    product(m, ("y_even", h), lambda j: [(M[:, 8 * h + 2 * j, :], vt[:, 8 * h + 2 * j, :])],
                            m_ready)
                if n is not None:
                    project(n, 4)
                else:
                    ffn_total()
                for h in range(2):
                    pe.wait_ge(ye_ready, m * 2 + (h + 1))
                    product(m, ("state", h), lambda j: [(kd[:, h, j, :], ye[:, h, j, :])])
                for h in range(2):
                    pe.wait_ge(kq_ready, m * 2 + (h + 1))
                    pe.wait_ge(s_ready, m * 2 + (h + 1))
                    product(m, ("kS", h), lambda j: [(kp[:, h, j, :], S[:, h, j, :])])
                for h in range(2):
                    product(m, ("o_even", h), lambda j: [(attnT[:, 8 * h + 2 * j, :], ye[:, h, j, :])])
                for h in range(2):
                    pe.wait_ge(r_ready, m * 2 + (h + 1))
                    product(m, ("y_odd", h), lambda j: [(M[:, 8 * h + 2 * j + 1, :], vt[:, 8 * h + 2 * j + 1, :])])
                turned("oT_even", 0)
                for h in range(2):
                    pe.wait_ge(yo_ready, m * 2 + (h + 1))
                    product(m, ("o_odd", h), lambda j: [(qp[:, h, j, :], S[:, h, j, :]),
                                                        (attnT[:, 8 * h + 2 * j + 1, :], yo[:, h, j, :])])
                if n is not None:
                    project(n, 5)
                else:
                    digits_turned()
                pe.wait_ge(wo_loaded, m * 16 + 16)
                output("out_even", 0)
                turned("oT_odd", 1)
                output("out_odd", 1)

            pe.wait_ge(consts_ready, 9)
            pe.wait_ge(xn_ready, NU)
            for k in range(KT):
                for t in range(2):
                    for j in range(4):
                        u = 4 * t + j
                        ins = pe.transpose(proj[2 * k + t][:, j * P:(j + 1) * P], xn_v[:, u, k * P:(k + 1) * P],
                                           ident[:])
                    ins.then_inc(xnT_filled, 1)
            pe.wait_ge(small_loaded, 64)
            pe.wait_ge(xnT_ready, 4)
            for i in range(2):
                for t in range(2):
                    for k in range(KT):
                        ins = pe.matmul(work[2 * i + t][0:NH, :], wba[:, k, i::2],
                                        xnT[:, k, 512 * t:512 * t + 512], start=(k == 0), stop=(k == KT - 1))
                    ins.then_inc(ba_filled, 1)
            pe.wait_ge(xT_split, 4)
            mixed(0, None)
            for p in (4, 5):
                project(0, p)
            pe.wait_ge(rows_dve, 14)
            pe.wait_ge(rows_ready, 1)
            for i, rows in enumerate((ngc_r, beta_r, egl_r)):
                for u in range(NU):
                    at = (i * NU + u) * NH
                    ins = pe.transpose(work[0][:, at:at + NH], rows[:, u * P:(u + 1) * P], ident[0:NH, 0:NH])
            ins.then_inc(colsT_filled, 1)
            pe.wait_ge(colsT_ready, 1)
            prepare(0)
            with pe.Fori(1, NP) as n:
                mixed(n, n - 1)
                solve(n - 1, n)
                prepare(n)
            mixed(None, NP - 1)
            solve(NP - 1, None)

            pe.wait_ge(xn2_ready, NU)
            pe.wait_ge(wT_ready, 12)
            for k in range(KT):
                for t in range(2):
                    for j in range(4):
                        u = 4 * t + j
                        ins = pe.transpose(proj[2 * k + t][:, j * P:(j + 1) * P], xn_v[:, u, k * P:(k + 1) * P],
                                           ident[:])
                    ins.then_inc(xn2T_filled, 1)
            pe.wait_ge(xn2T_ready, 4)
            pe.wait_ge(x2_hi_ready, 4)

            def down(i):
                t, e = i // ET, i % ET
                pe.wait_ge(hid_ready, i + 1)
                pe.wait_ge(hid_hi_ready, i + 1)
                for j in range(4):
                    for part in (hid_lo, hid_hi):
                        ins = pe.matmul(work[2 * t + j // 2][:, (j % 2) * D:(j % 2 + 1) * D],
                                        part[:, i % 4, j * P:(j + 1) * P], wT[:, 2, e * D:(e + 1) * D],
                                        start=(e == 0 and j % 2 == 0 and part is hid_lo),
                                        stop=(e == ET - 1 and part is hid_hi), skip_group_check=True)
                ins.then_inc(down_filled, 1)

            for i in range(2 * ET):
                t, e = i // ET, i % ET
                if i >= 2:
                    pe.wait_ge(hid_made, i - 1)
                for w in range(2):
                    ins = split_product(proj[2 * (i % 2) + w][:],
                                        [(wT[:, w, k * E + e * P:k * E + (e + 1) * P],
                                          x[:, k, 512 * t:512 * t + 512])
                                         for k in range(KT) for x in (x2T_lo, xT_hi)])
                ins.then_inc(up_filled, 1)
                if i >= 2:
                    down(i - 2)
            for i in (2 * ET - 2, 2 * ET - 1):
                down(i)

        @block.scalar
        def _(act):
            def filled(phase, n, key):
                act.wait_ge(work_filled, filled_at(phase, n, key))
                return four(work[bank_of(phase, key)])

            def project(n, p):
                if p == 0:
                    act.wait_ge(conv_loaded, n * 48 + 48)
                for turn in (2 * p, 2 * p + 1):
                    act.wait_ge(proj_filled, n * 12 + (turn + 1))
                    wait(act, silu_done, n * 12 + (turn - 3))
                    act.activation(conv[:, turn % 4, :], proj[turn % 4][:], ACT.Copy,
                                   scale=w_conv[:, CONV_S[p % 3], p // 3, 3:4]).then_inc(tap3_done, 1)

            def silu(n, p):
                if p == 0:
                    wait(act, kq_ready, n * 2)
                for i in range(2):
                    turn = 2 * p + i
                    act.wait_ge(taps_done, tap_at(n, turn, 2))
                    act.activation(chan[:, p // 3, p % 3, 512 * i:512 * i + 512], conv[:, turn % 4, :],
                                   ACT.Silu).then_inc(silu_done, 1)

            def z_silu(m, g):
                ps = filled("solve", m, ("z", g))
                act.activation(zs[:].rearrange("p (h u) c -> p h u c", h=2)[:, :, 2 * g:2 * g + 2, :],
                               ps.rearrange("p (u h) c -> p h u c", h=2), ACT.Silu).then_inc(z_ready, 1)

            def distance(n, g):
                if g == 0:
                    act.wait_ge(gcb_loaded, n * 16 + 16)
                    act.wait_ge(cols_loaded, n * 16 + 16)
                    wait(act, l_ready, n * 8)
                for j in range(4):
                    u = 4 * (g % 2) + j
                    ins = act.activation(Wd[:, 4 * g + j, :], gcb[:, g // 2, u * P:(u + 1) * P], ACT.Abs,
                                         bias=cols[:, g // 2, 0, u:u + 1])
                ins.then_inc(abs_done, 1)

            def decay(n):
                wait(act, kq_ready, n * 2)
                for g in range(4):
                    act.wait_ge(abs_done, n * 4 + (g + 1))
                    act.activation(Wd[:, units(g), :], Wd[:, units(g), :], ACT.Exp,
                                   scale=-1.0).then_inc(w_ready, 1)
                for h in range(2):
                    src = gcb[:, h, :].rearrange("p (u t) -> p u t", t=P)[:, 1::2, :]
                    act.activation(eg[:, h], src, ACT.Exp).then_inc(eg_ready, 1)

            def prepare(n):
                for g in range(4):
                    for i, name in enumerate(("kT", "qT")):
                        ps = filled("prep", n, (name, g))
                        turn = 2 * g + i
                        if turn >= 4:
                            act.wait_ge(sq_read, n * 8 + (turn - 3))
                        act.activation(sq[:, turn % 4, :].rearrange("p (a b) -> p a b", a=4), ps,
                                       ACT.Square).then_inc(sq_ready, 1)
                        if name == "kT":
                            for j in (0, 2):
                                u = 4 * (g % 2) + j
                                ins = act.activation(kd[:, g // 2, u // 2, :], ps[:, j, :], ACT.Copy,
                                                     scale=cols[:, g // 2, 2, u:u + 1])
                            ins.then_inc(kd_ready, 1)
                act.preload_act_table_set("natural_log_exp_and_others")
                act.wait_ge(prep_step, n * N_PREP_STEP + N_PREP_STEP)
                act.activation(lnk[:], sst[:], ACT.Ln).then_inc(lnk_done, 1)
                act.wait_ge(lnk_done, n + 1)
                act.activation(rs[:], lnk[:], ACT.Exp, scale=-0.5).then_inc(rs_ready, 1)

            def join(m, key):
                name, lv, g = key
                if name == "YX":
                    return
                dst, done = (Y, y_ready) if name == "LM" else (M, m_ready)
                ps = filled("solve", m, key)
                for p0, p1, c0, c1 in m_blocks(lv):
                    ins = act.activation(dst[p0:p1, units(g), c0:c1], ps[p0:p1, :, c0:c1], ACT.Copy)
                ins.then_inc(done, 1)

            def mixed(n, m):
                for step in MIXED:
                    if step[0] in ("proj", "silu", "abs"):
                        if n is None:
                            continue
                        if step[0] == "proj":
                            project(n, step[1])
                        elif step[0] == "silu":
                            silu(n, step[1])
                        elif m is not None:
                            distance(n, step[1])
                    elif m is None:
                        continue
                    elif step[0] == "z":
                        z_silu(m, step[1])
                    else:
                        join(m, step)

            def weight_sums():
                act.wait_ge(silu_done, 12 * NP)
                for i in range(3):
                    act.wait_ge(ffn_loaded, 48)
                    act.activation(conv[:].rearrange("p a b -> p (a b)"), raw[:, i, :], ACT.Abs,
                                   accum_out=asum[:, i:i + 1]).then_inc(asum_ready, 1)
                    act.wait_ge(asum_ready, i + 1)

            def digits_turned():
                for turn in range(12):
                    act.wait_ge(wT_filled, turn + 1)
                    i, q = turn // 4, turn % 4
                    act.activation(wT[:, i, 512 * q:512 * q + 512], proj[q][:], ACT.Copy).then_inc(wT_ready, 1)

            def solve(m, n):
                def evict(key, dst, done):
                    ps = filled("solve", m, key)
                    ins = act.activation(dst, ps, ACT.Copy)
                    ins.then_inc(done, 1)

                def square(par, h):
                    name = ("o_even", "o_odd")[par]
                    x = 2 * par + h
                    ps = filled("solve", m, (name, h))
                    if par == 0 and h == 0:
                        act.wait_ge(sq_read, m * 8 + 8)
                    ins = act.activation(sq[:, x, :].rearrange("p (a b) -> p a b", a=4), ps, ACT.Square)
                    ins.then_inc(sqo_ready, 1)

                def factor(par):
                    act.wait_ge(rms_ready, m * 4 + (2 * par + 2))
                    act.activation(lno[:, 2 * par:2 * par + 2, :], rms[:, 2 * par:2 * par + 2, :],
                                   ACT.Ln).then_inc(lno_done, 1)
                    act.wait_ge(lno_done, m * 2 + (par + 1))
                    act.activation(fac[:, 2 * par:2 * par + 2, :], lno[:, 2 * par:2 * par + 2, :], ACT.Exp,
                                   scale=-0.5).then_inc(fac_ready, 1)

                def turned(par):
                    for h in range(2):
                        x = 2 * par + h
                        ps = filled("solve", m, (("oT_even", "oT_odd")[par], h))
                        act.activation(oT[x].rearrange("p (a b) -> p a b", a=4), ps, ACT.Copy,
                                       scale=nw[:, 0:1]).then_inc(oT_ready, 1)

                act.preload_act_table_set("natural_log_exp_and_others")
                for h in range(2):
                    evict(("y_even", h), ye[:, h], ye_ready)
                if n is not None:
                    project(n, 4)
                else:
                    weight_sums()
                for h in range(2):
                    evict(("state", h), S[:, h], s_ready)
                if n is not None:
                    decay(n)
                for h in range(2):
                    square(0, h)
                factor(0)
                for h in range(2):
                    evict(("y_odd", h), yo[:, h], yo_ready)
                turned(0)
                for h in range(2):
                    square(1, h)
                if n is not None:
                    project(n, 5)
                factor(1)
                if n is None:
                    digits_turned()
                if n is not None:
                    silu(n, 4)
                turned(1)
                if n is not None:
                    silu(n, 5)

            def inverse_root(u0, u1, norm):
                act.wait_ge(var_ready, norm)
                act.activation(lnv[:, u0:u1], rstd[:, u0:u1], ACT.Ln).then_inc(lnv_done, 1)
                act.wait_ge(lnv_done, norm)
                act.activation(rstd[:, u0:u1], lnv[:, u0:u1], ACT.Exp, scale=-0.5).then_inc(rstd_ready, 1)

            act.preload_act_table_set("natural_log_exp_and_others")
            inverse_root(0, NU, 1)
            for i in range(4):
                act.wait_ge(xnT_filled, i + 1)
                act.activation(xnT[:, i // 2, 512 * (i % 2):512 * (i % 2) + 512], proj[i][:],
                               ACT.Copy).then_inc(xnT_ready, 1)
            act.wait_ge(ba_filled, 4)
            for t in range(2):
                act.activation(beta_r[:, 512 * t:512 * t + 512], work[t][0:NH, :],
                               ACT.Sigmoid).then_inc(rows_act, 1)
            for t in range(2):
                act.activation(t1_r[:, 512 * t:512 * t + 512], work[2 + t][0:NH, :], ACT.Abs,
                               bias=dtb[:, 0:1]).then_inc(rows_act, 1)
            act.preload_act_table_set("natural_log_exp_and_others")
            act.activation(expA[:], alog[:], ACT.Exp).then_inc(rows_act, 1)
            act.wait_ge(rows_act, 4)
            act.activation(t1_r, t1_r, ACT.Exp, scale=-1.0).then_inc(rows_act, 1)
            act.wait_ge(rows_act, 6)
            act.activation(t1_r, t1_r, ACT.Ln, bias=1.0).then_inc(rows_act, 1)
            act.wait_ge(rows_dve, 13)
            act.activation(egl_r, dif_r, ACT.Exp).then_inc(rows_ready, 1)
            mixed(0, None)
            for p in (4, 5):
                project(0, p)
                silu(0, p)
            act.wait_ge(colsT_ready, 1)
            for g in range(4):
                distance(0, g)
            act.preload_act_table_set("natural_log_exp_and_others")
            decay(0)
            prepare(0)
            with act.Fori(1, NP) as n:
                mixed(n, n - 1)
                solve(n - 1, n)
                prepare(n)
            mixed(None, NP - 1)
            solve(NP - 1, None)

            inverse_root(0, NU, 2)
            inverse_root(0, NU, 3)
            for i in range(4):
                act.wait_ge(xn2T_filled, i + 1)
                act.activation(xT_hi[:, i // 2, 512 * (i % 2):512 * (i % 2) + 512], proj[i][:],
                               ACT.Copy).then_inc(x2_hi_ready, 1)

            def hidden_high(i):
                act.wait_ge(hid_made, i + 1)
                if i >= 4:
                    act.wait_ge(down_filled, i - 3)
                act.activation(hid_hi[:, i % 4], conv[:, i % 4, :], ACT.Copy).then_inc(hid_hi_ready, 1)

            for i in range(2 * ET):
                act.wait_ge(up_filled, i + 1)
                if i >= 4:
                    act.wait_ge(hid_ready, i - 3)
                act.activation(conv[:, i % 4, :], proj[2 * (i % 2)][:], ACT.Silu,
                               scale=scale[:, 0:1]).then_inc(silu_up, 1)
                if i >= 1:
                    hidden_high(i - 1)
            hidden_high(2 * ET - 1)
            act.preload_act_table_set("natural_log_exp_and_others")
            inverse_root(0, 4, 4)
            inverse_root(4, 8, 5)

        @block.vector
        def _(dve):
            def filled(phase, n, key):
                dve.wait_ge(work_filled, filled_at(phase, n, key))
                return work[bank_of(phase, key)]

            def taps(n, pair, between=iter(())):
                h, s = pair // 3, pair % 3
                for tap in range(3):
                    for i in range(2):
                        turn = 2 * pair + i
                        d = tap + 1
                        if tap == 0:
                            dve.wait_ge(tap3_done, n * 12 + (turn + 1))
                        else:
                            dve.wait_ge(taps_done, tap_at(n, turn, tap - 1))
                        acc = conv[:, turn % 4, :].rearrange("p (b t) -> p b t", t=SEG)[:, :, d:]
                        src = proj[turn % 4][:].rearrange("p (b t) -> p b t", t=SEG)[:, :, 0:SEG - d]
                        dve.scalar_tensor_tensor(out=acc, in0=src,
                                                 scalar=w_conv[:, CONV_S[s], h, 2 - tap:3 - tap],
                                                 in1=acc, op0=ALU.mult, op1=ALU.add).then_inc(taps_done, 1)
                        for _ in range(6):
                            next(between, None)

            def substitute(m):
                for i in range(1, 16):
                    pv = prod[:, 0:i * i].rearrange("p (c j) -> p c j", j=i)
                    if i == 1:
                        dve.wait_ge(l_loaded, m * 16 + 16)
                    else:
                        dve.wait_ge(inv_step, m * N_INV + (2 * i - 2))
                    dve.tensor_tensor(pv, lb[:, i, 0:i].unsqueeze(1).broadcast_to([P, i, i]),
                                      xm[:, 0, 0:i, 0:i].rearrange("p j c -> p c j"),
                                      ALU.mult).then_inc(inv_step, 1)
                    yield
                    dve.wait_ge(inv_step, m * N_INV + (2 * i - 1))
                    dve.tensor_reduce(xm[:, 0, i, 0:i], pv, AX.X, ALU.add).then_inc(inv_step, 1)
                    yield
                dve.wait_ge(inv_step, m * N_INV + (N_INV - 1))
                dve.tensor_copy(xm[:, 1], xm[:, 0].rearrange("p r c -> p c r")).then_inc(inv_step, 1)
                yield

            def prepare(n):
                dve.wait_ge(cols_loaded, n * 16 + 16)
                for g in range(4):
                    for i, t in enumerate((ss, ssq)):
                        turn = 2 * g + i
                        dve.wait_ge(sq_ready, n * 8 + (turn + 1))
                        dve.tensor_reduce(t[:, units(g)], sq[:, turn % 4, :].rearrange("p (a b) -> p a b", a=4),
                                          AX.X, ALU.add).then_inc(sq_read, 1)
                    if g % 2:
                        h = g // 2
                        us = slice(8 * h, 8 * h + 8)
                        dve.wait_ge(sq_read, n * 8 + (2 * g + 1))
                        dve.tensor_scalar(sst[:, us], ss[:, us], L2_EPS, None, ALU.add).then_inc(prep_step, 1)
                        dve.wait_ge(prep_step, n * N_PREP_STEP + (2 * h + 1))
                        dve.reciprocal(rt[:, us], sst[:, us]).then_inc(prep_step, 1)
                        dve.wait_ge(prep_step, n * N_PREP_STEP + (2 * h + 2))
                        dve.scalar_tensor_tensor(out=negc[:, us], in0=rt[:, us], scalar=-1.0,
                                                 in1=cols[:, h, 1, :],
                                                 op0=ALU.mult, op1=ALU.mult).then_inc(negc_ready, 1)
                dve.wait_ge(sq_read, n * 8 + 8)
                dve.tensor_scalar(qe[:], ssq[:], L2_EPS, DH * RMS_EPS, ALU.add, ALU.mult).then_inc(qe_ready, 1)
                for g in range(4):
                    dve.wait_ge(scaled, n * 4 + (g + 1))
                    for t in range(2):
                        ps = filled("prep", n, ("gram", g, t))[:].rearrange("p (a b) -> p a b", a=2)
                        us = slice(4 * g + 2 * t, 4 * g + 2 * t + 2)
                        dve.tensor_tensor(Lneg[:, us, :], ps[:, :, 0:P], Wd[:, us, :], ALU.mult)
                        ins = dve.tensor_tensor(attnT[:, us, :], ps[:, :, P:2 * P], Wi[:, us, :], ALU.mult)
                        ins.then_inc(l_ready, 1)
                dve.wait_ge(rs_ready, n + 1)
                dve.tensor_tensor(fk[:].rearrange("p (h u) -> p h u", h=2),
                                  rs[:].rearrange("p (h u) -> p h u", h=2), cols[:, :, 1, :],
                                  ALU.mult).then_inc(fk_ready, 1)
                dve.wait_ge(fk_ready, n + 1)
                for g in range(4):
                    ps = four(filled("prep", n, ("vT", g)))
                    ins = dve.tensor_tensor(vt[:, units(g), :], ps,
                                            fk[:, units(g)].unsqueeze(2).broadcast_to([P, 4, P]), ALU.mult)
                    ins.then_inc(vt_ready, 1)

            def mean_square(m, par, h):
                x = 2 * par + h
                dve.wait_ge(sqo_ready, m * 4 + (x + 1))
                dve.tensor_reduce(sso[:, x, :], sq[:, x, :].rearrange("p (a b) -> p a b", a=4),
                                  AX.X, ALU.add).then_inc(sqo_read, 1)
                dve.wait_ge(sqo_read, m * 4 + (x + 1))
                dve.scalar_tensor_tensor(out=rms[:, x, :], in0=sso[:, x, :], scalar=1.0 / DH,
                                         in1=qe[:, 8 * h + par:8 * h + 8:2],
                                         op0=ALU.mult, op1=ALU.add).then_inc(rms_ready, 1)

            def gated(m, par, h):
                x = 2 * par + h
                ps = four(filled("solve", m, (("o_even", "o_odd")[par], h)))
                dve.wait_ge(fac_ready, m * 2 + (par + 1))
                for j in range(4):
                    ins = dve.scalar_tensor_tensor(out=og[:, x, j, :], in0=ps[:, j, :],
                                                   scalar=fac[:, x, j:j + 1],
                                                   in1=zs[:, 8 * h + 2 * j + par, :],
                                                   op0=ALU.mult, op1=ALU.mult)
                ins.then_inc(og_ready, 1)

            def mixed(n, m):
                between = iter(()) if m is None else substitute(m)
                for step in MIXED:
                    if step[0] == "proj":
                        if n is not None:
                            taps(n, step[1], iter(()) if step[1] < 1 else between)
                    elif step == ("LM", 0, 0) and m is not None:
                        for _ in between:
                            pass
                        dve.wait_ge(mc_loaded, m * 16 + 16)
                        dve.wait_ge(consts_ready, 9)
                        for g in range(4):
                            dve.tensor_tensor(M[:, units(g), :].rearrange("p u (b c) -> p u b c", c=16),
                                              xc[:, 1, units(g), :].unsqueeze(2).broadcast_to([P, 4, NB16, 16]),
                                              diag16[:].unsqueeze(1).broadcast_to([P, 4, NB16, 16]),
                                              ALU.mult).then_inc(m_spread, 1)
                    elif step[0] == "YX" and m is not None:
                        lv, g = step[1:]
                        ps = four(filled("solve", m, step))
                        for p0, p1, c0, c1 in x_blocks(lv):
                            ins = dve.tensor_copy(X[p0:p1, units(g), c0:c1], ps[p0:p1, :, c0:c1])
                        ins.then_inc(xj_ready, 1)

            def digits():
                dve.wait_ge(total_filled, 1)
                dve.tensor_scalar(scale[:], proj[0][:, 0:3], 1.0 / (D * E), Q_EPS, ALU.mult,
                                  ALU.add).then_inc(quant_step, 1)
                dve.wait_ge(quant_step, 1)
                dve.tensor_scalar(half[:], scale[:], 0.5, None, ALU.mult).then_inc(quant_step, 1)
                dve.tensor_scalar(nhalf[:], scale[:], -0.5, None, ALU.mult).then_inc(quant_step, 1)
                dve.wait_ge(quant_step, 3)
                for i in range(3):
                    low = Y[:].rearrange("p u t -> p (u t)") if i % 2 else X[:].rearrange("p u t -> p (u t)")
                    dve.tensor_scalar(low, raw[:, i, :], nhalf[:, i:i + 1], None, ALU.is_lt).then_inc(quant_step, 1)
                    dve.wait_ge(quant_step, 4 + i)
                    dve.scalar_tensor_tensor(out=raw[:, i, :], in0=raw[:, i, :], scalar=half[:, i:i + 1], in1=low,
                                             op0=ALU.is_gt, op1=ALU.subtract).then_inc(digits_ready, 1)
                    dve.wait_ge(digits_ready, i + 1)

            def solve(m, n):
                if n is not None:
                    taps(n, 4)
                else:
                    digits()
                for h in range(2):
                    ps = four(filled("solve", m, ("kS", h)))
                    for j in range(4):
                        u = 8 * h + 2 * j + 1
                        ins = dve.scalar_tensor_tensor(out=vt[:, u, :], in0=ps[:, j, :],
                                                       scalar=negc[:, u:u + 1], in1=vt[:, u, :],
                                                       op0=ALU.mult, op1=ALU.add)
                    ins.then_inc(r_ready, 1)
                dve.wait_ge(z_ready, m * 4 + 4)
                dve.wait_ge(qe_ready, m + 1)
                for par, name in enumerate(("out_even", "out_odd")):
                    if par == 0:
                        for p in range(2):
                            for h in range(2):
                                mean_square(m, p, h)
                            for h in range(2):
                                gated(m, p, h)
                        if n is not None:
                            taps(n, 5)
                    for t in range(2):
                        ps = filled("solve", m, (name, t))[:].rearrange("p (a b) -> p a b", a=2)
                        acc = attn_out[:, 4 * t + par:4 * t + 4:2, :]
                        ins = dve.tensor_tensor(acc, ps, acc, ALU.add)
                        ins.then_inc(acc_done, 1)

            def inverse_root(u0, u1, norm):
                dve.tensor_scalar(rstd[:, u0:u1], mv[:, u0:u1, 1], LN_EPS, None, ALU.add).then_inc(var_ready, 1)
                dve.wait_ge(rstd_ready, norm)

            def layer_stats(step, base, src, tiles, norm):
                for u in range(tiles):
                    ins = dve.bn_stats(stats[:, u, :], src(u))
                ins.then_inc(step, 1)
                dve.wait_ge(step, base + 1)
                for u in range(tiles):
                    ins = dve.bn_aggr(mv[:, u, :], stats[:, u, :])
                ins.then_inc(step, 1)
                dve.wait_ge(step, base + 2)
                inverse_root(0, tiles, norm)

            dve.wait_ge(x_loaded, 16)
            layer_stats(ln_step, 0, lambda u: x_sb[:, u, :], NU, 1)
            for u in range(NU):
                dve.tensor_scalar(xn_v[:, u, :], x_sb[:, u, :], mv[:, u, 0:1], rstd[:, u:u + 1],
                                  ALU.subtract, ALU.mult).then_inc(xn_ready, 1)
            for i in range(4):
                part = slice(512 * (i % 2), 512 * (i % 2) + 512)
                dve.wait_ge(xnT_ready, i + 1)
                dve.tensor_copy(xT_hi[:, i // 2, part], xnT[:, i // 2, part]).then_inc(xT_hi_ready, 1)
            dve.wait_ge(xn_ready, NU)
            for i in range(4):
                part = slice(512 * (i % 2), 512 * (i % 2) + 512)
                dve.wait_ge(xT_hi_ready, i + 1)
                dve.tensor_tensor(xT_lo[:, i // 2, part], xnT[:, i // 2, part],
                                  xT_hi[:, i // 2, part].bitcast(F32), ALU.subtract).then_inc(xT_split, 1)
            dve.wait_ge(ba_filled, 4)
            dve.wait_ge(rows_act, 4)
            for t in range(2):
                dve.tensor_scalar(sp_r[:, 512 * t:512 * t + 512], work[2 + t][0:NH, :], dtb[:, 0:1], 0.0,
                                  ALU.add, ALU.max).then_inc(rows_dve, 1)
            dve.wait_ge(rows_act, 7)
            dve.wait_ge(rows_dve, 2)
            dve.tensor_tensor(sp_r, sp_r, t1_r, ALU.add).then_inc(rows_dve, 1)
            dve.wait_ge(rows_dve, 3)
            dve.tensor_scalar(g_r, sp_r, expA[:, 0:1], -1.0, ALU.mult, ALU.mult).then_inc(rows_dve, 1)
            dve.wait_ge(rows_dve, 4)
            dve.wait_ge(consts_ready, 9)
            for u in range(NU):
                dve.tensor_tensor_scan(gc_r[:, u * P:(u + 1) * P], ones[0:NH, :], g_r[:, u * P:(u + 1) * P],
                                       0.0, ALU.mult, ALU.add).then_inc(rows_dve, 1)
            dve.wait_ge(rows_dve, 12)
            gc3 = gc_r.rearrange("p (u t) -> p u t", t=P)
            dve.tensor_tensor(dif_r.rearrange("p (u t) -> p u t", t=P),
                              gc3[:, :, P - 1:P].broadcast_to([NH, NU, P]), gc3,
                              ALU.subtract).then_inc(rows_dve, 1)
            dve.tensor_scalar(ngc_r, gc_r, -1.0, None, ALU.mult).then_inc(rows_dve, 1)
            mixed(0, None)
            for p in (4, 5):
                taps(0, p)
            dve.wait_ge(colsT_filled, 1)
            dve.tensor_copy(cols_all[:].rearrange("p h q u -> p q u h"),
                            work[0][:, 0:3 * NU * NH].rearrange("p (q u h) -> p q u h", q=3, u=NU)
                            ).then_inc(colsT_ready, 1)
            dve.wait_ge(gc_stored, 16)
            prepare(0)
            with dve.Fori(1, NP) as n:
                mixed(n, n - 1)
                solve(n - 1, n)
                prepare(n)
            mixed(None, NP - 1)
            solve(NP - 1, None)

            dve.wait_ge(acc_done, 4 * NP)
            layer_stats(x1_step, 0, lambda u: attn_out[:, u, :], NU, 2)
            for u in range(NU):
                ins = dve.tensor_scalar(attn_out[:, u, :], attn_out[:, u, :], mv[:, u, 0:1], rstd[:, u:u + 1],
                                        ALU.subtract, ALU.mult)
            ins.then_inc(x1_step, 1)
            dve.wait_ge(x1_step, 3)
            dve.wait_ge(x_loaded, 32)
            dve.tensor_tensor(x_sb[:], x_sb[:], attn_out[:], ALU.add).then_inc(x1_step, 1)
            dve.wait_ge(x1_step, 4)
            layer_stats(x1_step, 4, lambda u: x_sb[:, u, :], NU, 3)
            for u in range(NU):
                dve.tensor_scalar(xn_v[:, u, :], x_sb[:, u, :], mv[:, u, 0:1], rstd[:, u:u + 1],
                                  ALU.subtract, ALU.mult).then_inc(xn2_ready, 1)
            dve.tensor_tensor(half[:, 0:1], scale[:, 1:2], scale[:, 2:3], ALU.mult).then_inc(fin_step, 1)
            for i in range(4):
                part = slice(512 * (i % 2), 512 * (i % 2) + 512)
                dve.wait_ge(x2_hi_ready, i + 1)
                dve.tensor_tensor(x2T_lo[:, i // 2, part], proj[i][:], xT_hi[:, i // 2, part].bitcast(F32),
                                  ALU.subtract).then_inc(xn2T_ready, 1)

            def hidden_low(i):
                dve.wait_ge(hid_hi_ready, i + 1)
                dve.tensor_tensor(hid_lo[:, i % 4], conv[:, i % 4, :], hid_hi[:, i % 4].bitcast(F32),
                                  ALU.subtract).then_inc(hid_ready, 1)

            for i in range(2 * ET):
                dve.wait_ge(silu_up, i + 1)
                dve.tensor_tensor(conv[:, i % 4, :], proj[2 * (i % 2) + 1][:], conv[:, i % 4, :],
                                  ALU.mult).then_inc(hid_made, 1)
                if i >= 1:
                    hidden_low(i - 1)
            hidden_low(2 * ET - 1)
            y2 = attn_out
            for t in range(2):
                dve.wait_ge(down_filled, ET * (t + 1))
                dve.wait_ge(fin_step, 1 + 3 * t)
                for b in range(2):
                    ins = dve.tensor_scalar(y2[:, 4 * t + 2 * b:4 * t + 2 * b + 2, :],
                                            work[2 * t + b][:].rearrange("p (a b) -> p a b", a=2),
                                            half[:, 0:1], None, ALU.mult)
                ins.then_inc(fin_step, 1)
                dve.wait_ge(fin_step, 2 + 3 * t)
                for j in range(4):
                    ins = dve.bn_stats(stats[:, 4 * t + j, :], y2[:, 4 * t + j, :])
                ins.then_inc(fin_step, 1)
                dve.wait_ge(fin_step, 3 + 3 * t)
                for j in range(4):
                    ins = dve.bn_aggr(mv[:, 4 * t + j, :], stats[:, 4 * t + j, :])
                ins.then_inc(fin_step, 1)
                dve.wait_ge(fin_step, 4 + 3 * t)
                inverse_root(4 * t, 4 * t + 4, 4 + t)
                for j in range(4):
                    u = 4 * t + j
                    dve.tensor_scalar(y2[:, u, :], y2[:, u, :], mv[:, u, 0:1], rstd[:, u:u + 1],
                                      ALU.subtract, ALU.mult).then_inc(x1_step, 1)
                for j in range(4):
                    u = 4 * t + j
                    dve.wait_ge(x1_step, 6 + u + 1)
                    dve.tensor_tensor(x_sb[:, u, :], x_sb[:, u, :], y2[:, u, :], ALU.add).then_inc(fin_ready, 1)


_INS = ["L0_attn_hidden_states", "L0_attn_W_qkvz", "L0_attn_W_ba", "L0_attn_conv_weight", "L0_attn_dt_bias",
        "L0_attn_A_log", "L0_attn_norm_weight", "L0_attn_W_out", "L0_ffn_W_up", "L0_ffn_W_gate", "L0_ffn_W_down"]


def kernel(**inputs):
    import numpy as np
    import concourse.bacc as bacc
    from concourse import mybir as mb
    from concourse.bass_utils import run_bass_kernel_spmd

    nc = bacc.Bacc("TRN2", target_bir_lowering=False, num_devices=1)
    arrays, args = {}, []
    for name in _INS:
        a = np.ascontiguousarray(inputs[name])
        arrays[f"in_{name}"] = a
        args.append(nc.dram_tensor(f"in_{name}", a.shape, mb.dt.from_np(a.dtype), kind="ExternalInput").ap())
    shape = inputs[_INS[0]].shape
    out = nc.dram_tensor("out_0", shape, mb.dt.float32, kind="ExternalOutput").ap()
    sandwich(nc, *args, out)
    got = run_bass_kernel_spmd(nc, [arrays], core_ids=[0])
    return got.results[0]["out_0"]
```

```python
from contextlib import ExitStack

import concourse.bass as bass
from concourse import mybir

F32 = mybir.dt.float32
F32R = mybir.dt.float32r
ALU = mybir.AluOpType
ACT = mybir.ActivationFunctionType
AX = mybir.AxisListType

P = 128
T, D = 1024, 256
KT = D // P
NH, DH = 16, 128
NU = T // P
SEG = 256
NP = NH // 2
NB16 = P // 16
E = 1024
ET = E // P
LN_EPS, L2_EPS, RMS_EPS, Q_EPS = 1e-5, 1e-6, 1e-6, 1e-8

K_, Q_, V_ = 0, 1, 2
W_COL = {K_: DH, Q_: 0, V_: 2 * DH}
CONV_S = {K_: 1, Q_: 0, V_: 2}

STREAMS = [(0, K_), (1, K_), (0, Q_), (1, Q_), (0, V_), (1, V_)]

MIXED = []
for lv in range(3):
    MIXED += [("LM", lv, g) for g in range(4)]
    MIXED += [("proj", 2 * lv)]
    MIXED += [("silu", 2 * lv - 1)] if lv == 1 else [("decay",)] if lv == 2 else []
    for g in range(4):
        MIXED += [("MY", lv, g)] + ([("YX", lv, g)] if lv < 2 else [])
        if lv < 2 and g % 2:
            MIXED += [("abs", 2 * lv + g // 2)]
    MIXED += [("silu", 3)] if lv == 2 else []
    MIXED += [("silu", 2 * lv)] + ([("proj", 2 * lv + 1)] if lv < 2 else [])

TURNS = [("solve", step) for step in MIXED if step[0] in ("LM", "MY", "YX")]
for name, at in (("y_even", None), ("state", None), ("kT", 0), ("kS", None), ("kT", 2), ("o_even", None),
                 ("y_odd", None), ("oT_even", None), ("o_odd", None), ("out_even", None), ("oT_odd", None),
                 ("out_odd", None)):
    TURNS += [("solve", (name, h)) if at is None else ("prep", (name, at + h)) for h in range(2)]
for name in ("kq", "qT", "vT", "z"):
    TURNS += [("prep", (name, g)) for g in range(4)]
N_TURNS = len(TURNS)
OF = {phase: [turn for turn in TURNS if turn[0] == phase] for phase in ("solve", "prep")}
assert N_TURNS % 4 == 0


def bank_of(phase, key):
    return TURNS.index((phase, key)) % 4


def filled_at(phase, n, key):
    body = n + 1 if phase == "solve" else n
    turn = (phase, key)
    if isinstance(body, int) and body <= 0:
        return OF["prep"].index(turn) + 1 if phase == "prep" else 0
    before_it = len(OF["prep"]) - N_TURNS
    if isinstance(body, int) and body == NP:
        return NP * N_TURNS + (before_it + OF["solve"].index(turn) + 1)
    return body * N_TURNS + (before_it + TURNS.index(turn) + 1)


def before(phase, n, key):
    body = n + 1 if phase == "solve" else n
    at = TURNS.index((phase, key)) - 4
    while True:
        if at < 0:
            at, body = at + N_TURNS, body - 1
            if isinstance(body, int) and body < 0:
                return None
        kind, k = TURNS[at]
        if isinstance(body, int) and ((body == 0 and kind == "solve") or (body == NP and kind == "prep")):
            at -= 4
            continue
        return kind, (body - 1 if kind == "solve" else body), k


def tap_at(n, turn, tap):
    return n * 36 + (6 * (turn // 2) + 2 * tap + turn % 2 + 1)


def wait(eng, sem, value):
    if isinstance(value, int) and value <= 0:
        return
    eng.wait_ge(sem, value)


def m_blocks(lv):
    s = 16 << lv
    return [(a, a + s, a + s, a + 2 * s) for a in range(0, P, 2 * s)]


def x_blocks(lv):
    s = 16 << lv
    if s == 16:
        return [(a, a + 32, a, a + 16) for a in range(0, P, 32)]
    return [(a + s, a + 2 * s, a, a + s) for a in range(0, P, 2 * s)]


N_INV = 31
N_PREP_STEP = 2 * 2


def sandwich(nc, x, W_qkvz, W_ba, conv_w, dt_bias, A_log, norm_w, W_out, W_up, W_gate, W_down, out):
    x_t = x.rearrange("b s d -> (b s) d").rearrange("(u p) d -> p u d", p=P)
    out_t = out.rearrange("b s d -> (b s) d").rearrange("(u p) d -> p u d", p=P)
    wq_d = W_qkvz.rearrange("(k p) (n h c) -> n p k h c", p=P, n=NP, h=2)
    wout_d = W_out.rearrange("(n h p) d -> n p h d", n=NP, h=2)
    conv_d = conv_w.rearrange("(s n h p) t -> n p s h t", s=3, n=NP, h=2)
    gc_d = nc.dram_tensor("gc_rows", (NH, T), F32, kind="Internal").ap()
    blk_out_d = nc.dram_tensor("l_blocks", (2 * NU, NB16, 16, 16), F32, kind="Internal").ap()
    blk_in_d = nc.dram_tensor("x_blocks", (2, 2 * NU, NB16, 16, 16), F32, kind="Internal").ap()

    with ExitStack() as ctx:
        place = {}

        def sb(name, shape, dtype=F32):
            place[name] = -(-nc.sbuf_base // 32) * 32
            return ctx.enter_context(nc.sbuf_tensor(name, shape, dtype))

        def over(name, under, shape, dtype):
            return nc.alloc_sbuf_tensor_at(name, shape, dtype, offset=place[under])

        def sem(name):
            return ctx.enter_context(nc.semaphore(name))

        x_sb = sb("x_sb", [P, NU, D])
        xT_hi = sb("xT_hi", [P, KT, T], F32R)
        xT_lo = over("xT_lo", "x_sb", [P, KT, T], F32R)
        attn_out = sb("attn_out", [P, NU, D])
        ident = sb("ident", [P, P])
        strict = sb("strict", [P, P])
        upper = sb("upper", [P, P])
        ones = sb("ones", [P, P])
        w_qkv = sb("w_qkv", [P, KT, 2, 3 * DH])
        w_z = sb("w_z", [P, KT, 2, DH])
        wq_hi = sb("wq_hi", [P, KT, 2, 3 * DH], F32R)
        wq_lo = over("wq_lo", "w_qkv", [P, KT, 2, 3 * DH], F32R)
        wz_hi = sb("wz_hi", [P, KT, 2, DH], F32R)
        wz_lo = over("wz_lo", "w_z", [P, KT, 2, DH], F32R)
        w_conv = sb("w_conv", [P, 3, 2, 4])
        w_o = sb("w_o", [P, 2, D])
        nw = sb("nw", [P, 1])
        wba = sb("wba", [P, KT, 2 * NH])
        alog = sb("alog", [NH, 1])
        dtb = sb("dtb", [NH, 1])
        conv = sb("conv", [P, 4, 512])
        chan = sb("chan", [P, 2, 3, T])
        decays = sb("decays", [P, 3, 2 * T])
        gcb = decays[:, 0, :].rearrange("p (h t) -> p h t", h=2)
        Wd = decays[:, 1, :].rearrange("p (u t) -> p u t", t=P)
        Wi = decays[:, 2, :].rearrange("p (u t) -> p u t", t=P)
        cols_all = sb("cols_all", [P, NH, 3, NU])
        cols = sb("cols", [P, 2, 3, NU])
        eg = gcb.rearrange("p h (u t) -> p h u t", t=P)[:, :, 1::2, :]
        sq = sb("sq", [P, 4, 512])
        ss = sb("ss", [P, 16])
        sst = sb("sst", [P, 16])
        rt = sb("rt", [P, 16])
        rs = sb("rs", [P, 16])
        negc = sb("negc", [P, 16])
        fk = sb("fk", [P, 16])
        ssq = sb("ssq", [P, 16])
        qe = sb("qe", [P, 16])
        zs = sb("zs", [P, 16, P])
        kd = sb("kd", [P, 2, 4, P])
        kp = sb("kp", [P, 2, 4, P])
        qp = sb("qp", [P, 2, 4, P])
        vt = sb("vt", [P, 16, P])
        Lneg = sb("Lneg", [P, 16, P])
        attnT = sb("attnT", [P, 16, P])
        lb_prod = sb("lb_prod", [P, 2, 16, 16])
        lb = lb_prod[:, 0]
        prod = lb_prod[:, 1].rearrange("p r c -> p (r c)")
        xm = sb("xm", [P, 2, 16, 16])
        xc = lb_prod
        diag16 = sb("diag16", [P, NB16, 16])
        M = sb("M", [P, 16, P])
        X = sb("X", [P, 16, P])
        Y = sb("Y", [P, 16, P])
        ye = sb("ye", [P, 2, 4, P])
        yo = sb("yo", [P, 2, 4, P])
        S = sb("S", [P, 2, 4, P])
        og = sb("og", [P, 4, 4, P])
        oT = [t[:, h].rearrange("p a b -> p (a b)") for t in (ye, yo) for h in range(2)]
        sso = sb("sso", [P, 4, 4])
        rms = sb("rms", [P, 4, 4])
        fac = sb("fac", [P, 4, 4])
        stats = sb("stats", [P, NU, 6])
        mv = sb("mv", [P, NU, 2])
        rstd = sb("rstd", [P, NU])
        lnk = sb("lnk", [P, 16])
        lno = sb("lno", [P, 4, 4])
        lnv = sb("lnv", [P, NU])
        raw = decays
        asum = sb("asum", [P, 3])
        scale = sb("scale", [P, 3])
        half = sb("half", [P, 3])
        nhalf = sb("nhalf", [P, 3])
        xn_v = og[:].rearrange("p a b c -> p (a b c)").rearrange("p (u d) -> p u d", d=D)
        xnT = M[:].rearrange("p a b -> p (a b)").rearrange("p (k t) -> p k t", k=KT)
        wT = over("wT", "chan", [P, 3, 2 * E], F32R)
        x2T_lo = over("x2T_lo", "X", [P, KT, T], F32R)
        hid_hi = over("hid_hi", "og", [P, 4, 512], F32R)
        hid_lo = over("hid_lo", "sq", [P, 4, 512], F32R)
        beta_r = Wd[0:NH, 0:8, :].rearrange("p a b -> p (a b)")
        t1_r = Wd[0:NH, 8:16, :].rearrange("p a b -> p (a b)")
        sp_r = Wi[0:NH, 0:8, :].rearrange("p a b -> p (a b)")
        g_r = Wi[0:NH, 8:16, :].rearrange("p a b -> p (a b)")
        gc_r = vt[0:NH, 0:8, :].rearrange("p a b -> p (a b)")
        ngc_r = vt[0:NH, 8:16, :].rearrange("p a b -> p (a b)")
        egl_r = zs[0:NH, 0:8, :].rearrange("p a b -> p (a b)")
        dif_r = zs[0:NH, 8:16, :].rearrange("p a b -> p (a b)")
        expA = sb("expA", [NH, 1])

        proj = [ctx.enter_context(nc.psum_tensor(f"proj{i}", [P, 512], F32)) for i in range(4)]
        work = [ctx.enter_context(nc.psum_tensor(f"work{i}", [P, 512], F32)) for i in range(4)]

        x_loaded, small_loaded, ffn_loaded = sem("x_loaded"), sem("small_loaded"), sem("ffn_loaded")
        wqkv_loaded, conv_loaded, wz_loaded, wo_loaded = (sem("wqkv_loaded"), sem("conv_loaded"),
                                                          sem("wz_loaded"), sem("wo_loaded"))
        gcb_loaded, cols_loaded = sem("gcb_loaded"), sem("cols_loaded")
        gc_stored, l_stored, l_loaded = sem("gc_stored"), sem("l_stored"), sem("l_loaded")
        x_stored, m_stored, out_stored = sem("x_stored"), sem("m_stored"), sem("out_stored")
        xc_loaded, mc_loaded, x_spread, m_spread = (sem("xc_loaded"), sem("mc_loaded"), sem("x_spread"),
                                                    sem("m_spread"))
        consts_step, consts_ready = sem("consts_step"), sem("consts_ready")
        ln_step, xn_ready, xnT_filled, xnT_ready = (sem("ln_step"), sem("xn_ready"), sem("xnT_filled"),
                                                    sem("xnT_ready"))
        xT_hi_ready, xT_split, wq_hi_ready, wq_split, wz_hi_ready, wz_split = (
            sem("xT_hi_ready"), sem("xT_split"), sem("wq_hi_ready"), sem("wq_split"), sem("wz_hi_ready"),
            sem("wz_split"))
        ba_filled, rows_act, rows_dve, rows_ready = (sem("ba_filled"), sem("rows_act"), sem("rows_dve"),
                                                     sem("rows_ready"))
        colsT_filled, colsT_ready = sem("colsT_filled"), sem("colsT_ready")
        proj_filled, tap3_done, taps_done, silu_done = (sem("proj_filled"), sem("tap3_done"),
                                                        sem("taps_done"), sem("silu_done"))
        work_filled = sem("work_filled")
        z_ready, eg_ready, abs_done, w_ready = (
            sem("z_ready"), sem("eg_ready"), sem("abs_done"), sem("w_ready"))
        prep_step, negc_ready, kd_ready, masked, kq_ready, gram_filled, a_ready = (
            sem("prep_step"), sem("negc_ready"), sem("kd_ready"), sem("masked"), sem("kq_ready"),
            sem("gram_filled"), sem("a_ready"))
        k_summed, q_summed = sem("k_summed"), sem("q_summed")
        l_ready, vt_ready, inv_step = sem("l_ready"), sem("vt_ready"), sem("inv_step")
        y_ready, m_ready, xj_ready = sem("y_ready"), sem("m_ready"), sem("xj_ready")
        ye_ready, s_ready, r_ready, yo_ready = sem("ye_ready"), sem("s_ready"), sem("r_ready"), sem("yo_ready")
        sqo_ready, sqo_read, rms_ready, og_ready, oT_ready, acc_done = (
            sem("sqo_ready"), sem("sqo_read"), sem("rms_ready"), sem("og_ready"), sem("oT_ready"),
            sem("acc_done"))
        fk_ready, qe_ready = sem("fk_ready"), sem("qe_ready")
        lnk_done, rs_ready, lno_done, fac_ready = (sem("lnk_done"), sem("rs_ready"), sem("lno_done"),
                                                   sem("fac_ready"))
        var_ready, lnv_done, rstd_ready = sem("var_ready"), sem("lnv_done"), sem("rstd_ready")
        asum_ready, total_filled, quant_step, digits_ready = (
            sem("asum_ready"), sem("total_filled"), sem("quant_step"), sem("digits_ready"))
        wT_filled, wT_ready = sem("wT_filled"), sem("wT_ready")
        x1_step, xn2_ready, xn2T_filled, xn2T_ready = (sem("x1_step"), sem("xn2_ready"),
                                                       sem("xn2T_filled"), sem("xn2T_ready"))
        x2_hi_ready, hid_hi_ready, hid_made = sem("x2_hi_ready"), sem("hid_hi_ready"), sem("hid_made")
        up_filled, silu_up, hid_ready, down_filled = (sem("up_filled"), sem("silu_up"), sem("hid_ready"),
                                                      sem("down_filled"))
        fin_step, fin_ready = sem("fin_step"), sem("fin_ready")

        def four(ap):
            return ap[:].rearrange("p (a b) -> p a b", a=4)

        def units(g):
            return slice(4 * g, 4 * g + 4)

        block = ctx.enter_context(nc.Block())

        @block.sync
        def _(sp):
            sp.dma_start(x_sb[:], x_t).then_inc(x_loaded, 16)
            sp.dma_start(wba[:], W_ba.rearrange("(k p) c -> p k c", p=P)).then_inc(small_loaded, 16)
            sp.dma_start(alog[:], A_log.rearrange("(h a) -> h a", a=1)).then_inc(small_loaded, 16)
            sp.dma_start(dtb[:], dt_bias.rearrange("(h a) -> h a", a=1)).then_inc(small_loaded, 16)
            sp.dma_start(nw[:], norm_w.rearrange("(h a) -> h a", a=1)).then_inc(small_loaded, 16)

            def pick(view, n):
                if isinstance(n, int):
                    return view[n]
                v = view[bass.ds(n, 1)]
                names = " ".join("abcdef"[:len(view.shape) - 1])
                return v.rearrange(f"n {names} -> (n a) {names[2:]}")

            def constant_wait():
                sp.wait_ge(x_loaded, 16)

            def load_qkv(n):
                constant_wait()
                wait(sp, proj_filled, n * 12)
                for k in range(KT):
                    sp.dma_start(w_qkv[:, k], pick(wq_d[:, :, k, :, 0:3 * DH], n)).then_inc(wqkv_loaded, 16)
                constant_wait()
                wait(sp, taps_done, n * 36)
                for s in range(3):
                    sp.dma_start(w_conv[:, s], pick(conv_d[:, :, s], n)).then_inc(conv_loaded, 16)

            def load_z(n):
                constant_wait()
                wait(sp, z_ready, n * 4)
                for k in range(KT):
                    sp.dma_start(w_z[:, k], pick(wq_d[:, :, k, :, 3 * DH:4 * DH], n)).then_inc(wz_loaded, 16)

            def load_gates(n):
                constant_wait()
                wait(sp, kq_ready, n * 2)
                if isinstance(n, int):
                    rows = gc_d[2 * n:2 * n + 2, :]
                    pair = cols_all[:, 2 * n:2 * n + 2]
                else:
                    rows = gc_d[bass.ds(n * 2, 2), :]
                    pair = cols_all[:, bass.ds(n * 2, 2)]
                sp.dma_start(gcb, rows.partition_broadcast(P)).then_inc(gcb_loaded, 16)
                constant_wait()
                wait(sp, vt_ready, n * 4)
                sp.dma_start(cols[:], pair).then_inc(cols_loaded, 16)

            def blocks(n):
                sp.wait_ge(l_ready, n * 4 + 4)
                for b in range(NB16):
                    sp.dma_start(blk_out_d[:, b].rearrange("u r c -> r u c"),
                                 Lneg[16 * b:16 * b + 16, :, 16 * b:16 * b + 16]).then_inc(l_stored, 16)
                sp.wait_ge(l_stored, n * (16 * NB16) + 16 * NB16)
                sp.dma_start(lb, blk_out_d.rearrange("u b r c -> (u b) r c")).then_inc(l_loaded, 16)
                sp.wait_ge(inv_step, n * N_INV + N_INV)
                for i, stored in ((1, m_stored), (0, x_stored)):
                    sp.dma_start(blk_in_d[i].rearrange("u b r c -> (u b) (r c)"),
                                 xm[:, i].rearrange("p r c -> p (r c)")).then_inc(stored, 16)
                for i, stored, loaded in ((1, m_stored, mc_loaded), (0, x_stored, xc_loaded)):
                    sp.wait_ge(stored, n * 16 + 16)
                    sp.dma_start(xc[:, i], blk_in_d[i].rearrange("u b r c -> (b r) u c")).then_inc(loaded, 16)

            def load_wo(m):
                sp.dma_start(w_o[:], pick(wout_d, m)).then_inc(wo_loaded, 16)

            load_qkv(0)
            sp.wait_ge(rows_dve, 12)
            sp.dma_start(gc_d, gc_r).then_inc(gc_stored, 16)
            sp.wait_ge(gc_stored, 16)
            sp.wait_ge(colsT_ready, 1)
            load_gates(0)
            load_z(0)
            load_qkv(1)
            blocks(0)

            def body(n, more):
                load_gates(n)
                load_wo(n - 1)
                load_z(n)
                if more:
                    load_qkv(n + 1)
                blocks(n)

            with sp.Fori(1, NP - 1) as n:
                body(n, True)
            body(NP - 1, False)
            sp.wait_ge(vt_ready, 4 * NP)
            load_wo(NP - 1)
            sp.wait_ge(kq_ready, 2 * NP)
            sp.wait_ge(a_ready, 4 * NP)
            for i, w in enumerate((W_up, W_gate)):
                sp.dma_start(raw[:, i].rearrange("p (t d) -> p t d", d=D),
                             w.rearrange("(t p) d -> p t d", p=P)).then_inc(ffn_loaded, 16)
            sp.dma_start(raw[:, 2].rearrange("p (a e) -> p a e", e=E),
                         W_down.rearrange("(a p) e -> p a e", p=P)).then_inc(ffn_loaded, 16)
            sp.wait_ge(z_ready, 4 * NP)
            sp.dma_start(x_sb[:], x_t).then_inc(x_loaded, 16)
            for u in range(NU):
                sp.wait_ge(fin_ready, u + 1)
                sp.dma_start(out_t[:, u, :], x_sb[:, u, :]).then_inc(out_stored, 16)
            sp.wait_ge(out_stored, 16 * NU)

        @block.gpsimd
        def _(pool):
            def select(t, ap, base, pattern, mult, op, fill):
                pool.affine_select(out=ap, in_=ap, compare_op=op, fill=fill, base=base, pattern=pattern,
                                   channel_multiplier=mult).then_inc(consts_ready, 1)

            pool.memset(ident[:], 0.0).then_inc(consts_step, 1)
            pool.memset(ones[:], 1.0).then_inc(consts_ready, 1)
            pool.memset(strict[:], 1.0).then_inc(consts_step, 1)
            pool.memset(upper[:], 1.0).then_inc(consts_step, 1)
            pool.memset(Y[:], 0.0).then_inc(consts_step, 1)
            pool.memset(diag16[:], 1.0).then_inc(consts_step, 1)
            pool.memset(xm[:], 0.0).then_inc(consts_step, 1)
            pool.memset(attn_out[:], 0.0).then_inc(consts_ready, 1)
            pool.wait_ge(consts_step, 6)
            select(ident, ident[:], 0, [[-1, P]], 1, ALU.not_equal, 1.0)
            select(strict, strict[:], 0, [[-1, P]], 1, ALU.is_gt, 0.0)
            select(upper, upper[:], 0, [[1, P]], -1, ALU.is_ge, 0.0)
            select(Y, Y[:], 0, [[0, 16], [-1, P]], 1, ALU.not_equal, 1.0)
            select(xm, xm[:], 0, [[0, 2], [-1, 16], [1, 16]], 0, ALU.not_equal, 1.0)

            select(diag16, diag16[:], 0, [[-16, NB16], [0, 16]], 1, ALU.is_ge, 0.0)
            pool.wait_ge(consts_ready, 8)
            select(diag16, diag16[:], 15, [[16, NB16], [0, 16]], -1, ALU.is_ge, 0.0)

            def spread(m):
                pool.wait_ge(xc_loaded, m * 16 + 16)
                for g in range(4):
                    pool.tensor_tensor(X[:, units(g), :].rearrange("p u (b c) -> p u b c", c=16),
                                       xc[:, 0, units(g), :].unsqueeze(2).broadcast_to([P, 4, NB16, 16]),
                                       diag16[:].unsqueeze(1).broadcast_to([P, 4, NB16, 16]),
                                       ALU.mult).then_inc(x_spread, 1)

            def one_of(w):
                return ones[:, 0:1].unsqueeze(2).broadcast_to([P, 2, w.shape[-1]])

            def split_qkv(n):
                for k in range(KT):
                    pool.wait_ge(wqkv_loaded, n * (16 * KT) + 16 * KT)
                    pool.tensor_tensor(wq_hi[:, k], w_qkv[:, k], one_of(w_qkv),
                                       ALU.mult).then_inc(wq_hi_ready, 1)
                    pool.wait_ge(wq_hi_ready, n * KT + (k + 1))
                    pool.tensor_tensor(wq_lo[:, k], w_qkv[:, k], wq_hi[:, k].bitcast(F32),
                                       ALU.subtract).then_inc(wq_split, 1)

            def split_z(n):
                for k in range(KT):
                    pool.wait_ge(wz_loaded, n * (16 * KT) + 16 * KT)
                    pool.tensor_tensor(wz_hi[:, k], w_z[:, k], one_of(w_z),
                                       ALU.mult).then_inc(wz_hi_ready, 1)
                    pool.wait_ge(wz_hi_ready, n * KT + (k + 1))
                    pool.tensor_tensor(wz_lo[:, k], w_z[:, k], wz_hi[:, k].bitcast(F32),
                                       ALU.subtract).then_inc(wz_split, 1)

            def masks(n):
                wait(pool, a_ready, n * 4)
                for g in range(4):
                    pool.wait_ge(w_ready, n * 4 + (g + 1))
                    w4 = Wd[:, units(g), :]
                    pool.tensor_tensor(Wi[:, units(g), :], w4, upper[:].unsqueeze(1).broadcast_to([P, 4, P]),
                                       ALU.mult).then_inc(masked, 1)
                    pool.wait_ge(masked, n * 8 + (2 * g + 1))
                    pool.tensor_tensor(w4, w4, strict[:].unsqueeze(1).broadcast_to([P, 4, P]),
                                       ALU.mult).then_inc(masked, 1)

            def prepare(n):
                wait(pool, work_filled, filled_at("solve", n - 1, ("o_odd", 1)))
                for h in range(2):
                    pool.wait_ge(eg_ready, n * 2 + (h + 1))
                    pool.wait_ge(silu_done, n * 12 + (6 + 2 * h))
                    for s, t in ((K_, kp), (Q_, qp)):
                        src = chan[:, h, s, :].rearrange("p (u t) -> p u t", t=P)[:, 1::2, :]
                        ins = pool.tensor_tensor(t[:, h], src, eg[:, h], ALU.mult)
                    ins.then_inc(kq_ready, 1)

            pool.wait_ge(consts_ready, 9)
            def body(n, more):
                masks(n)
                split_z(n)
                if more:
                    split_qkv(n + 1)
                prepare(n)
                spread(n)

            split_qkv(0)
            masks(0)
            split_z(0)
            split_qkv(1)
            prepare(0)
            spread(0)
            with pool.Fori(1, NP - 1) as n:
                body(n, True)
            body(NP - 1, False)

        @block.tensor
        def _(pe):
            read_by = {}
            for g in range(4):
                read_by["z", g] = [(z_ready, 4, g + 1)]
                read_by["kT", g] = [(kd_ready, 4, g + 1)]
                read_by["qT", g] = [(q_summed, 4, g + 1)]
                read_by["kq", g] = [(a_ready, 4, g + 1)]
                read_by["vT", g] = [(vt_ready, 4, g + 1)]
                for lv in range(3):
                    read_by["LM", lv, g] = [(y_ready, 12, 4 * lv + g + 1)]
                    read_by["MY", lv, g] = [(m_ready, 12, 4 * lv + g + 1)]
                    read_by["YX", lv, g] = [(xj_ready, 8, 4 * lv + g + 1)]
            for h in range(2):
                read_by["y_even", h] = [(ye_ready, 2, h + 1)]
                read_by["state", h] = [(s_ready, 2, h + 1)]
                read_by["kS", h] = [(r_ready, 2, h + 1)]
                read_by["y_odd", h] = [(yo_ready, 2, h + 1)]
                for par, name in enumerate(("even", "odd")):
                    read_by["o_" + name, h] = [(sqo_ready, 4, 2 * par + h + 1), (og_ready, 4, 2 * par + h + 1)]
                    read_by["oT_" + name, h] = [(oT_ready, 4, 2 * par + h + 1)]
                    read_by["out_" + name, h] = [(acc_done, 4, 2 * par + h + 1)]

            def bank(phase, n, key, met=None):
                earlier = before(phase, n, key)
                if earlier is not None:
                    for done, per, count in read_by[earlier[2]]:
                        if done is not met:
                            pe.wait_ge(done, earlier[1] * per + count)
                return work[bank_of(phase, key)]

            def split_product(ps, terms):
                for i, (a, b) in enumerate(terms):
                    ins = pe.matmul(ps, a, b, start=(i == 0), stop=(i == len(terms) - 1))
                return ins

            def project(n, p):
                if p == 0:
                    pe.wait_ge(wq_split, n * KT + KT)
                h, s = STREAMS[p]
                for t in range(2):
                    turn = 2 * p + t
                    if turn >= 4:
                        pe.wait_ge(taps_done, tap_at(n, turn - 4, 2))
                    elif not (isinstance(n, int) and n == 0):
                        pe.wait_ge(l_ready, n * 4 + (turn + 1) - 4)
                    c = W_COL[s]
                    ins = split_product(proj[turn % 4][:],
                                        [(w[:, k, h, c:c + DH], x[:, k, 512 * t:512 * t + 512])
                                         for k in range(KT)
                                         for w, x in ((wq_lo, xT_hi), (wq_hi, xT_lo), (wq_hi, xT_hi))])
                    ins.then_inc(proj_filled, 1)

            def z_product(m, g):
                if g == 0:
                    pe.wait_ge(wz_split, m * KT + KT)
                ps = bank("prep", m, ("z", g))
                for j in range(2):
                    u = 2 * g + j
                    ins = split_product(ps[:, j * 2 * DH:(j + 1) * 2 * DH],
                                        [(x[:, k, u * P:(u + 1) * P], w[:, k].rearrange("p h c -> p (h c)"))
                                         for k in range(KT)
                                         for x, w in ((xT_lo, wz_hi), (xT_hi, wz_lo), (xT_hi, wz_hi))])
                ins.then_inc(work_filled, 1)

            def gram(ps, s, g):
                for j in range(4):
                    u = 4 * (g % 2) + j
                    ins = pe.matmul(ps[:, j * P:(j + 1) * P], chan[:, g // 2, K_, u * P:(u + 1) * P],
                                    chan[:, g // 2, s, u * P:(u + 1) * P], start=True, stop=True)
                return ins

            def to_tokens(n, name, s, g):
                ps = bank("prep", n, (name, g))
                for j in range(4):
                    u = 4 * (g % 2) + j
                    ins = pe.transpose(ps[:, j * P:(j + 1) * P], chan[:, g // 2, s, u * P:(u + 1) * P],
                                       ident[:])
                ins.then_inc(work_filled, 1)

            def k_turned(n, h):
                pe.wait_ge(silu_done, n * 12 + (2 + 2 * h))
                for g in (2 * h, 2 * h + 1):
                    to_tokens(n, "kT", K_, g)

            def k_gram(n):
                for g in range(4):
                    pe.wait_ge(taps_done, tap_at(n, 8 + g, 2))
                    gram(proj[g], K_, g).then_inc(gram_filled, 1)

            def rest(n):
                for g in range(4):
                    pe.wait_ge(silu_done, n * 12 + (6 + 2 * (g // 2)))
                    gram(bank("prep", n, ("kq", g)), Q_, g).then_inc(work_filled, 1)
                for g in range(4):
                    to_tokens(n, "qT", Q_, g)
                for g in range(4):
                    pe.wait_ge(silu_done, n * 12 + (10 + 2 * (g // 2)))
                    to_tokens(n, "vT", V_, g)
                for g in range(4):
                    z_product(n, g)

            def product(n, key, terms, met=None):
                ps = bank("solve", n, key, met)
                for j in range(4):
                    ts = terms(j)
                    for i, (a, b) in enumerate(ts):
                        ins = pe.matmul(ps[:, j * P:(j + 1) * P], a, b, start=(i == 0), stop=(i == len(ts) - 1))
                ins.then_inc(work_filled, 1)

            def join(m, key):
                name, lv, g = key
                if name == "LM":
                    if lv:
                        pe.wait_ge(m_ready, m * 12 + (4 * (lv - 1) + g + 1))
                    else:
                        pe.wait_ge(m_spread, m * 4 + (g + 1))
                    product(m, key, lambda j: [(Lneg[:, 4 * g + j, :], M[:, 4 * g + j, :])])
                elif name == "MY":
                    pe.wait_ge(y_ready, m * 12 + (4 * lv + g + 1))
                    if lv:
                        pe.wait_ge(xj_ready, m * 8 + (4 * (lv - 1) + g + 1))
                    else:
                        pe.wait_ge(x_spread, m * 4 + (g + 1))
                    product(m, key, lambda j: [(X[:, 4 * g + j, :], Y[:, 4 * g + j, :])])
                else:
                    product(m, key, lambda j: [(Y[:, 4 * g + j, :], X[:, 4 * g + j, :])])

            def mixed(n, m):
                for step in MIXED:
                    if step[0] == "proj":
                        if n is not None:
                            project(n, step[1])
                    elif step[0] in ("silu", "abs", "decay") or m is None:
                        pass
                    else:
                        join(m, step)

            def ffn_total():
                pe.wait_ge(asum_ready, 3)
                pe.wait_ge(l_ready, 4 * NP)
                pe.matmul(proj[0][:, 0:3], ones[:], asum[:], start=True, stop=True).then_inc(total_filled, 1)

            def digits_turned():
                for i in range(3):
                    pe.wait_ge(digits_ready, i + 1)
                    for q in range(4):
                        turn = 4 * i + q
                        if turn >= 4:
                            pe.wait_ge(wT_ready, turn - 3)
                        for j in range(4):
                            if i < 2:
                                src = raw[:, i, (4 * (q % 2) + j) * D + (q // 2) * P:][:, 0:P]
                            else:
                                src = raw[:, i, (j % 2) * E + (2 * q + j // 2) * P:][:, 0:P]
                            ins = pe.transpose(proj[q][:, j * P:(j + 1) * P], src, ident[:])
                        ins.then_inc(wT_filled, 1)

            def solve(m, n):
                def turned(name, par):
                    for h in range(2):
                        pe.wait_ge(og_ready, m * 4 + (2 * par + h + 1))
                        ps = bank("solve", m, (name, h))
                        for j in range(4):
                            ins = pe.transpose(ps[:, j * P:(j + 1) * P], og[:, 2 * par + h, j, :], ident[:])
                        ins.then_inc(work_filled, 1)

                def output(name, par):
                    pe.wait_ge(oT_ready, m * 4 + (2 * par + 2))
                    for t in range(2):
                        ps = bank("solve", m, (name, t), oT_ready)
                        for j in range(2):
                            for h in range(2):
                                at = (2 * t + j) * P
                                ins = pe.matmul(ps[:, j * D:(j + 1) * D], oT[2 * par + h][:, at:at + P],
                                                w_o[:, h, :], start=(h == 0), stop=(h == 1))
                        ins.then_inc(work_filled, 1)

                for h in range(2):
                    pe.wait_ge(m_ready, m * 12 + (10 + 2 * h))
                    product(m, ("y_even", h), lambda j: [(M[:, 8 * h + 2 * j, :], vt[:, 8 * h + 2 * j, :])],
                            m_ready)
                if n is not None:
                    project(n, 5)
                else:
                    ffn_total()
                for h in range(2):
                    pe.wait_ge(ye_ready, m * 2 + (h + 1))
                    product(m, ("state", h), lambda j: [(kd[:, h, j, :], ye[:, h, j, :])])
                if n is not None:
                    k_turned(n, 0)
                for h in range(2):
                    pe.wait_ge(kq_ready, m * 2 + (h + 1))
                    pe.wait_ge(s_ready, m * 2 + (h + 1))
                    product(m, ("kS", h), lambda j: [(kp[:, h, j, :], S[:, h, j, :])])
                if n is not None:
                    k_turned(n, 1)
                for h in range(2):
                    product(m, ("o_even", h), lambda j: [(attnT[:, 8 * h + 2 * j, :], ye[:, h, j, :])])
                for h in range(2):
                    pe.wait_ge(r_ready, m * 2 + (h + 1))
                    product(m, ("y_odd", h), lambda j: [(M[:, 8 * h + 2 * j + 1, :], vt[:, 8 * h + 2 * j + 1, :])])
                if n is not None:
                    k_gram(n)
                turned("oT_even", 0)
                for h in range(2):
                    pe.wait_ge(yo_ready, m * 2 + (h + 1))
                    product(m, ("o_odd", h), lambda j: [(qp[:, h, j, :], S[:, h, j, :]),
                                                        (attnT[:, 8 * h + 2 * j + 1, :], yo[:, h, j, :])])
                if n is None:
                    digits_turned()
                pe.wait_ge(wo_loaded, m * 16 + 16)
                output("out_even", 0)
                turned("oT_odd", 1)
                output("out_odd", 1)

            pe.wait_ge(consts_ready, 9)
            pe.wait_ge(xn_ready, NU)
            for k in range(KT):
                for t in range(2):
                    for j in range(4):
                        u = 4 * t + j
                        ins = pe.transpose(proj[2 * k + t][:, j * P:(j + 1) * P], xn_v[:, u, k * P:(k + 1) * P],
                                           ident[:])
                    ins.then_inc(xnT_filled, 1)
            pe.wait_ge(small_loaded, 64)
            pe.wait_ge(xnT_ready, 4)
            for i in range(2):
                for t in range(2):
                    for k in range(KT):
                        ins = pe.matmul(work[2 * i + t][0:NH, :], wba[:, k, i::2],
                                        xnT[:, k, 512 * t:512 * t + 512], start=(k == 0), stop=(k == KT - 1))
                    ins.then_inc(ba_filled, 1)
            pe.wait_ge(xT_split, 4)
            for p in (0, 1):
                project(0, p)
            pe.wait_ge(rows_dve, 14)
            pe.wait_ge(rows_ready, 1)
            for i, rows in enumerate((ngc_r, beta_r, egl_r)):
                for u in range(NU):
                    at = (i * NU + u) * NH
                    ins = pe.transpose(work[0][:, at:at + NH], rows[:, u * P:(u + 1) * P], ident[0:NH, 0:NH])
            ins.then_inc(colsT_filled, 1)
            for p in range(2, 6):
                project(0, p)
            pe.wait_ge(colsT_ready, 1)
            k_turned(0, 0)
            k_turned(0, 1)
            k_gram(0)
            rest(0)
            with pe.Fori(1, NP) as n:
                mixed(n, n - 1)
                solve(n - 1, n)
                rest(n)
            mixed(None, NP - 1)
            solve(NP - 1, None)

            pe.wait_ge(xn2_ready, NU)
            pe.wait_ge(wT_ready, 12)
            for k in range(KT):
                for t in range(2):
                    for j in range(4):
                        u = 4 * t + j
                        ins = pe.transpose(proj[2 * k + t][:, j * P:(j + 1) * P],
                                           attn_out[:, u, k * P:(k + 1) * P], ident[:])
                    ins.then_inc(xn2T_filled, 1)
            pe.wait_ge(xn2T_ready, 4)
            pe.wait_ge(x2_hi_ready, 4)

            def down(i):
                t, e = i // ET, i % ET
                pe.wait_ge(hid_ready, i + 1)
                pe.wait_ge(hid_hi_ready, i + 1)
                for j in range(4):
                    for part in (hid_lo, hid_hi):
                        ins = pe.matmul(work[2 * t + j // 2][:, (j % 2) * D:(j % 2 + 1) * D],
                                        part[:, i % 4, j * P:(j + 1) * P], wT[:, 2, e * D:(e + 1) * D],
                                        start=(e == 0 and j % 2 == 0 and part is hid_lo),
                                        stop=(e == ET - 1 and part is hid_hi), skip_group_check=True)
                ins.then_inc(down_filled, 1)

            for i in range(2 * ET):
                t, e = i // ET, i % ET
                if i >= 2:
                    pe.wait_ge(hid_made, i - 1)
                for w in range(2):
                    ins = split_product(proj[2 * (i % 2) + w][:],
                                        [(wT[:, w, k * E + e * P:k * E + (e + 1) * P],
                                          x[:, k, 512 * t:512 * t + 512])
                                         for k in range(KT) for x in (x2T_lo, xT_hi)])
                ins.then_inc(up_filled, 1)
                if i >= 2:
                    down(i - 2)
            for i in (2 * ET - 2, 2 * ET - 1):
                down(i)

        @block.scalar
        def _(act):
            def filled(phase, n, key):
                act.wait_ge(work_filled, filled_at(phase, n, key))
                return four(work[bank_of(phase, key)])

            def project(n, p):
                if p == 0:
                    act.wait_ge(conv_loaded, n * 48 + 48)
                for turn in (2 * p, 2 * p + 1):
                    act.wait_ge(proj_filled, n * 12 + (turn + 1))
                    wait(act, silu_done, n * 12 + (turn - 3))
                    act.activation(conv[:, turn % 4, :], proj[turn % 4][:], ACT.Copy,
                                   scale=w_conv[:, CONV_S[STREAMS[p][1]], STREAMS[p][0], 3:4]).then_inc(tap3_done, 1)

            def silu(n, p):
                if p == 0:
                    wait(act, kq_ready, n * 2)
                for i in range(2):
                    turn = 2 * p + i
                    act.wait_ge(taps_done, tap_at(n, turn, 2))
                    h, s = STREAMS[p]
                    act.activation(chan[:, h, s, 512 * i:512 * i + 512], conv[:, turn % 4, :],
                                   ACT.Silu).then_inc(silu_done, 1)

            def z_silu(m, g):
                ps = filled("prep", m, ("z", g))
                act.activation(zs[:].rearrange("p (h u) c -> p h u c", h=2)[:, :, 2 * g:2 * g + 2, :],
                               ps.rearrange("p (u h) c -> p h u c", h=2), ACT.Silu).then_inc(z_ready, 1)

            def distance(n, g):
                if g == 0:
                    act.wait_ge(gcb_loaded, n * 16 + 16)
                    act.wait_ge(cols_loaded, n * 16 + 16)
                    wait(act, l_ready, n * 4)
                for j in range(4):
                    u = 4 * (g % 2) + j
                    ins = act.activation(Wd[:, 4 * g + j, :], gcb[:, g // 2, u * P:(u + 1) * P], ACT.Abs,
                                         bias=cols[:, g // 2, 0, u:u + 1])
                ins.then_inc(abs_done, 1)

            def decay(n):
                for g in range(4):
                    act.wait_ge(abs_done, n * 4 + (g + 1))
                    act.activation(Wd[:, units(g), :], Wd[:, units(g), :], ACT.Exp,
                                   scale=-1.0).then_inc(w_ready, 1)

            def exp_gc(n):
                act.wait_ge(abs_done, n * 4 + 4)
                for h in range(2):
                    act.activation(eg[:, h], eg[:, h], ACT.Exp).then_inc(eg_ready, 1)

            def squares(sums, ps, g, done):
                for j in range(4):
                    ins = act.activation(sq[:, g, j * P:(j + 1) * P], ps[:, j, :], ACT.Square,
                                         accum_out=sums[:, 4 * g + j:4 * g + j + 1])
                ins.then_inc(done, 1)

            def k_squares(n, g):
                wait(act, q_summed, n * 4)
                squares(ss, filled("prep", n, ("kT", g)), g, k_summed)

            def k_decayed(n, g):
                ps = filled("prep", n, ("kT", g))
                for j in (0, 2):
                    u = 4 * (g % 2) + j
                    ins = act.activation(kd[:, g // 2, u // 2, :], ps[:, j, :], ACT.Copy,
                                         scale=cols[:, g // 2, 2, u:u + 1])
                ins.then_inc(kd_ready, 1)

            def inverse_norm(n):
                act.wait_ge(prep_step, n * N_PREP_STEP + N_PREP_STEP)
                act.activation(lnk[:], sst[:], ACT.Ln).then_inc(lnk_done, 1)
                act.wait_ge(lnk_done, n + 1)
                act.activation(rs[:], lnk[:], ACT.Exp, scale=-0.5).then_inc(rs_ready, 1)

            def rest(n):
                silu(n, 5)
                act.wait_ge(k_summed, n * 4 + 4)
                wait(act, sqo_read, n * 4)
                for g in range(4):
                    squares(ssq, filled("prep", n, ("qT", g)), g, q_summed)
                act.wait_ge(fk_ready, n + 1)
                for g in range(4):
                    ps = filled("prep", n, ("vT", g))
                    for j in range(4):
                        u = 4 * g + j
                        ins = act.activation(vt[:, u, :], ps[:, j, :], ACT.Copy, scale=fk[:, u:u + 1])
                    ins.then_inc(vt_ready, 1)
                for g in range(4):
                    z_silu(n, g)

            def join(m, key):
                name, lv, g = key
                if name == "YX":
                    return
                dst, done = (Y, y_ready) if name == "LM" else (M, m_ready)
                ps = filled("solve", m, key)
                for p0, p1, c0, c1 in m_blocks(lv):
                    ins = act.activation(dst[p0:p1, units(g), c0:c1], ps[p0:p1, :, c0:c1], ACT.Copy)
                ins.then_inc(done, 1)

            def weight_sum(i):
                act.wait_ge(silu_done, 12 * NP)
                act.wait_ge(ffn_loaded, 48)
                act.activation(conv[:].rearrange("p a b -> p (a b)"), raw[:, i, :], ACT.Abs,
                               accum_out=asum[:, i:i + 1]).then_inc(asum_ready, 1)
                act.wait_ge(asum_ready, i + 1)

            def mixed(n, m):
                for step in MIXED:
                    if step[0] in ("proj", "silu", "abs", "decay"):
                        if n is None:
                            if step in (("proj", 2), ("proj", 3), ("proj", 4)):
                                weight_sum(step[1] - 2)
                            continue
                        if step[0] == "proj":
                            project(n, step[1])
                        elif step[0] == "silu":
                            silu(n, step[1])
                        elif m is None:
                            pass
                        elif step[0] == "abs":
                            distance(n, step[1])
                        else:
                            act.preload_act_table_set("natural_log_exp_and_others")
                            decay(n)
                    elif m is None:
                        continue
                    else:
                        join(m, step)

            def digits_turned():
                for turn in range(12):
                    act.wait_ge(wT_filled, turn + 1)
                    i, q = turn // 4, turn % 4
                    act.activation(wT[:, i, 512 * q:512 * q + 512], proj[q][:], ACT.Copy).then_inc(wT_ready, 1)

            def solve(m, n):
                def evict(key, dst, done):
                    ps = filled("solve", m, key)
                    ins = act.activation(dst, ps, ACT.Copy)
                    ins.then_inc(done, 1)

                def square(par, h):
                    name = ("o_even", "o_odd")[par]
                    x = 2 * par + h
                    ps = filled("solve", m, (name, h))
                    ins = act.activation(sq[:, x, :].rearrange("p (a b) -> p a b", a=4), ps, ACT.Square)
                    ins.then_inc(sqo_ready, 1)

                def factor(par):
                    act.wait_ge(rms_ready, m * 4 + (2 * par + 2))
                    act.activation(lno[:, 2 * par:2 * par + 2, :], rms[:, 2 * par:2 * par + 2, :],
                                   ACT.Ln).then_inc(lno_done, 1)
                    act.wait_ge(lno_done, m * 2 + (par + 1))
                    act.activation(fac[:, 2 * par:2 * par + 2, :], lno[:, 2 * par:2 * par + 2, :], ACT.Exp,
                                   scale=-0.5).then_inc(fac_ready, 1)

                def turned(par):
                    for h in range(2):
                        x = 2 * par + h
                        ps = filled("solve", m, (("oT_even", "oT_odd")[par], h))
                        act.activation(oT[x].rearrange("p (a b) -> p a b", a=4), ps, ACT.Copy,
                                       scale=nw[:, 0:1]).then_inc(oT_ready, 1)

                for h in range(2):
                    evict(("y_even", h), ye[:, h], ye_ready)
                if n is not None:
                    project(n, 5)
                for h in range(2):
                    evict(("state", h), S[:, h], s_ready)
                act.preload_act_table_set("natural_log_exp_and_others")
                if n is not None:
                    for g in range(4):
                        k_squares(n, g)
                        k_decayed(n, g)
                    exp_gc(n)
                if n is not None:
                    act.wait_ge(k_summed, n * 4 + 4)
                for h in range(2):
                    square(0, h)
                factor(0)
                for h in range(2):
                    evict(("y_odd", h), yo[:, h], yo_ready)
                turned(0)
                for h in range(2):
                    square(1, h)
                if n is not None:
                    inverse_norm(n)
                factor(1)
                if n is None:
                    digits_turned()
                turned(1)

            def inverse_root(us, norm):
                act.wait_ge(var_ready, norm)
                act.activation(lnv[:, us], rstd[:, us], ACT.Ln).then_inc(lnv_done, 1)
                act.wait_ge(lnv_done, norm)
                act.activation(rstd[:, us], lnv[:, us], ACT.Exp, scale=-0.5).then_inc(rstd_ready, 1)

            act.preload_act_table_set("natural_log_exp_and_others")
            inverse_root(slice(0, NU), 1)
            for i in range(4):
                act.wait_ge(xnT_filled, i + 1)
                act.activation(xnT[:, i // 2, 512 * (i % 2):512 * (i % 2) + 512], proj[i][:],
                               ACT.Copy).then_inc(xnT_ready, 1)
            act.wait_ge(ba_filled, 4)
            for t in range(2):
                act.activation(beta_r[:, 512 * t:512 * t + 512], work[t][0:NH, :],
                               ACT.Sigmoid).then_inc(rows_act, 1)
            for t in range(2):
                act.activation(t1_r[:, 512 * t:512 * t + 512], work[2 + t][0:NH, :], ACT.Abs,
                               bias=dtb[:, 0:1]).then_inc(rows_act, 1)
            act.preload_act_table_set("natural_log_exp_and_others")
            act.activation(expA[:], alog[:], ACT.Exp).then_inc(rows_act, 1)
            act.wait_ge(rows_act, 4)
            act.activation(t1_r, t1_r, ACT.Exp, scale=-1.0).then_inc(rows_act, 1)
            act.wait_ge(rows_act, 6)
            act.activation(t1_r, t1_r, ACT.Ln, bias=1.0).then_inc(rows_act, 1)
            act.wait_ge(rows_dve, 13)
            act.activation(egl_r, dif_r, ACT.Exp).then_inc(rows_ready, 1)
            for p in range(6):
                project(0, p)
                if p:
                    silu(0, p - 1)
                if p == 3:
                    act.wait_ge(colsT_ready, 1)
                    for g in range(4):
                        distance(0, g)
                if p == 4:
                    act.preload_act_table_set("natural_log_exp_and_others")
                    decay(0)
            for g in range(4):
                k_squares(0, g)
                k_decayed(0, g)
            exp_gc(0)
            inverse_norm(0)
            rest(0)
            with act.Fori(1, NP) as n:
                mixed(n, n - 1)
                solve(n - 1, n)
                rest(n)
            mixed(None, NP - 1)
            solve(NP - 1, None)

            for norm in (2, 3, 4, 5):
                inverse_root(slice((norm - 2) // 2, NU, 2), norm)
            for i in range(4):
                act.wait_ge(xn2T_filled, i + 1)
                act.activation(xT_hi[:, i // 2, 512 * (i % 2):512 * (i % 2) + 512], proj[i][:],
                               ACT.Copy).then_inc(x2_hi_ready, 1)

            def hidden_high(i):
                act.wait_ge(hid_made, i + 1)
                if i >= 4:
                    act.wait_ge(down_filled, i - 3)
                act.activation(hid_hi[:, i % 4], conv[:, i % 4, :], ACT.Copy).then_inc(hid_hi_ready, 1)

            for i in range(2 * ET):
                act.wait_ge(up_filled, i + 1)
                if i >= 4:
                    act.wait_ge(hid_ready, i - 3)
                act.activation(conv[:, i % 4, :], proj[2 * (i % 2)][:], ACT.Silu,
                               scale=scale[:, 0:1]).then_inc(silu_up, 1)
                if i >= 1:
                    hidden_high(i - 1)
            hidden_high(2 * ET - 1)
            act.preload_act_table_set("natural_log_exp_and_others")
            inverse_root(slice(0, 4), 6)
            inverse_root(slice(4, 8), 7)

        @block.vector
        def _(dve):
            def filled(phase, n, key):
                dve.wait_ge(work_filled, filled_at(phase, n, key))
                return work[bank_of(phase, key)]

            def taps(n, pair):
                h, s = STREAMS[pair]
                for tap in range(3):
                    for i in range(2):
                        turn = 2 * pair + i
                        d = tap + 1
                        if tap == 0:
                            dve.wait_ge(tap3_done, n * 12 + (turn + 1))
                        else:
                            dve.wait_ge(taps_done, tap_at(n, turn, tap - 1))
                        acc = conv[:, turn % 4, :].rearrange("p (b t) -> p b t", t=SEG)[:, :, d:]
                        src = proj[turn % 4][:].rearrange("p (b t) -> p b t", t=SEG)[:, :, 0:SEG - d]
                        dve.scalar_tensor_tensor(out=acc, in0=src,
                                                 scalar=w_conv[:, CONV_S[s], h, 2 - tap:3 - tap],
                                                 in1=acc, op0=ALU.mult, op1=ALU.add).then_inc(taps_done, 1)

            def substitute(m):
                for i in range(1, 16):
                    pv = prod[:, 0:i * i].rearrange("p (c j) -> p c j", j=i)
                    if i == 1:
                        dve.wait_ge(l_loaded, m * 16 + 16)
                    else:
                        dve.wait_ge(inv_step, m * N_INV + (2 * i - 2))
                    dve.tensor_tensor(pv, lb[:, i, 0:i].unsqueeze(1).broadcast_to([P, i, i]),
                                      xm[:, 0, 0:i, 0:i].rearrange("p j c -> p c j"),
                                      ALU.mult).then_inc(inv_step, 1)
                    yield
                    dve.wait_ge(inv_step, m * N_INV + (2 * i - 1))
                    dve.tensor_reduce(xm[:, 0, i, 0:i], pv, AX.X, ALU.add).then_inc(inv_step, 1)
                    yield
                dve.wait_ge(inv_step, m * N_INV + (N_INV - 1))
                dve.tensor_copy(xm[:, 1], xm[:, 0].rearrange("p r c -> p c r")).then_inc(inv_step, 1)

            def early(n):
                dve.wait_ge(cols_loaded, n * 16 + 16)
                for h in range(2):
                    us = slice(8 * h, 8 * h + 8)
                    dve.wait_ge(k_summed, n * 4 + (2 * h + 2))
                    dve.tensor_scalar(sst[:, us], ss[:, us], L2_EPS, None, ALU.add).then_inc(prep_step, 1)
                    dve.wait_ge(prep_step, n * N_PREP_STEP + (2 * h + 1))
                    dve.reciprocal(rt[:, us], sst[:, us]).then_inc(prep_step, 1)
                    dve.wait_ge(prep_step, n * N_PREP_STEP + (2 * h + 2))
                    dve.scalar_tensor_tensor(out=negc[:, us], in0=rt[:, us], scalar=-1.0,
                                             in1=cols[:, h, 1, :],
                                             op0=ALU.mult, op1=ALU.mult).then_inc(negc_ready, 1)
                for g in range(4):
                    dve.wait_ge(masked, n * 8 + (2 * g + 2))
                    dve.wait_ge(negc_ready, n * 2 + (g // 2 + 1))
                    dve.wait_ge(gram_filled, n * 4 + (g + 1))
                    for j in range(4):
                        u = 4 * g + j
                        ins = dve.scalar_tensor_tensor(out=Lneg[:, u, :], in0=proj[g][:, j * P:(j + 1) * P],
                                                       scalar=negc[:, u:u + 1], in1=Wd[:, u, :],
                                                       op0=ALU.mult, op1=ALU.mult)
                    ins.then_inc(l_ready, 1)

            def rest(n):
                dve.wait_ge(rs_ready, n + 1)
                dve.tensor_tensor(fk[:].rearrange("p (h u) -> p h u", h=2),
                                  rs[:].rearrange("p (h u) -> p h u", h=2), cols[:, :, 1, :],
                                  ALU.mult).then_inc(fk_ready, 1)
                steps = substitute(n)
                for g in range(4):
                    ps = four(filled("prep", n, ("kq", g)))
                    dve.tensor_tensor(attnT[:, units(g), :], ps, Wi[:, units(g), :], ALU.mult).then_inc(a_ready, 1)
                    for _ in range(5):
                        next(steps, None)
                for _ in steps:
                    pass
                dve.wait_ge(q_summed, n * 4 + 4)
                dve.tensor_scalar(qe[:], ssq[:], L2_EPS, DH * RMS_EPS, ALU.add, ALU.mult).then_inc(qe_ready, 1)
                dve.wait_ge(mc_loaded, n * 16 + 16)
                for g in range(4):
                    dve.tensor_tensor(M[:, units(g), :].rearrange("p u (b c) -> p u b c", c=16),
                                      xc[:, 1, units(g), :].unsqueeze(2).broadcast_to([P, 4, NB16, 16]),
                                      diag16[:].unsqueeze(1).broadcast_to([P, 4, NB16, 16]),
                                      ALU.mult).then_inc(m_spread, 1)

            def inverse_root(us, norm):
                us = slice(us[0], us[-1] + 1, us[1] - us[0])
                dve.tensor_scalar(rstd[:, us], mv[:, us, 1], LN_EPS, None, ALU.add).then_inc(var_ready, 1)
                dve.wait_ge(rstd_ready, norm)

            def layer_stats(step, base, us, src, norm):
                for u in us:
                    ins = dve.bn_stats(stats[:, u, :], src[:, u, :])
                ins.then_inc(step, 1)
                dve.wait_ge(step, base + 1)
                for u in us:
                    ins = dve.bn_aggr(mv[:, u, :], stats[:, u, :])
                ins.then_inc(step, 1)
                dve.wait_ge(step, base + 2)
                inverse_root(us, norm)

            def fin_units(par):
                us, first = range(par, NU, 2), 6 * par
                dve.wait_ge(acc_done, 4 * NP - 2 + 2 * par)
                layer_stats(x1_step, first, us, attn_out, 2 + 2 * par)
                for u in us:
                    ins = dve.tensor_scalar(attn_out[:, u, :], attn_out[:, u, :], mv[:, u, 0:1],
                                            rstd[:, u:u + 1], ALU.subtract, ALU.mult)
                ins.then_inc(x1_step, 1)
                dve.wait_ge(x1_step, first + 3)
                dve.wait_ge(x_loaded, 32)
                dve.tensor_tensor(x_sb[:, par::2], x_sb[:, par::2], attn_out[:, par::2],
                                  ALU.add).then_inc(x1_step, 1)
                dve.wait_ge(x1_step, first + 4)
                layer_stats(x1_step, first + 4, us, x_sb, 3 + 2 * par)
                for u in us:
                    dve.tensor_scalar(attn_out[:, u, :], x_sb[:, u, :], mv[:, u, 0:1], rstd[:, u:u + 1],
                                      ALU.subtract, ALU.mult).then_inc(xn2_ready, 1)

            def mean_square(m, par, h):
                x = 2 * par + h
                dve.wait_ge(sqo_ready, m * 4 + (x + 1))
                dve.tensor_reduce(sso[:, x, :], sq[:, x, :].rearrange("p (a b) -> p a b", a=4),
                                  AX.X, ALU.add).then_inc(sqo_read, 1)
                dve.wait_ge(sqo_read, m * 4 + (x + 1))
                dve.scalar_tensor_tensor(out=rms[:, x, :], in0=sso[:, x, :], scalar=1.0 / DH,
                                         in1=qe[:, 8 * h + par:8 * h + 8:2],
                                         op0=ALU.mult, op1=ALU.add).then_inc(rms_ready, 1)

            def gated(m, par, h):
                x = 2 * par + h
                ps = four(filled("solve", m, (("o_even", "o_odd")[par], h)))
                dve.wait_ge(fac_ready, m * 2 + (par + 1))
                for j in range(4):
                    ins = dve.scalar_tensor_tensor(out=og[:, x, j, :], in0=ps[:, j, :],
                                                   scalar=fac[:, x, j:j + 1],
                                                   in1=zs[:, 8 * h + 2 * j + par, :],
                                                   op0=ALU.mult, op1=ALU.mult)
                ins.then_inc(og_ready, 1)

            def mixed(n, m):
                for step in MIXED:
                    if step[0] == "proj":
                        if n is not None:
                            taps(n, step[1])
                    elif step[0] == "YX" and m is not None:
                        lv, g = step[1:]
                        ps = four(filled("solve", m, step))
                        for p0, p1, c0, c1 in x_blocks(lv):
                            ins = dve.tensor_copy(X[p0:p1, units(g), c0:c1], ps[p0:p1, :, c0:c1])
                        ins.then_inc(xj_ready, 1)

            def quant_scales():
                dve.wait_ge(total_filled, 1)
                dve.tensor_scalar(scale[:], proj[0][:, 0:3], 1.0 / (D * E), Q_EPS, ALU.mult,
                                  ALU.add).then_inc(quant_step, 1)
                dve.wait_ge(quant_step, 1)
                dve.tensor_scalar(half[:], scale[:], 0.5, None, ALU.mult).then_inc(quant_step, 1)
                dve.tensor_scalar(nhalf[:], scale[:], -0.5, None, ALU.mult).then_inc(quant_step, 1)
                dve.wait_ge(quant_step, 3)

            def digits(i):
                low = (Y if i % 2 else X)[:].rearrange("p u t -> p (u t)")
                dve.tensor_scalar(low, raw[:, i, :], nhalf[:, i:i + 1], None, ALU.is_lt).then_inc(quant_step, 1)
                dve.wait_ge(quant_step, 4 + i)
                dve.scalar_tensor_tensor(out=raw[:, i, :], in0=raw[:, i, :], scalar=half[:, i:i + 1], in1=low,
                                         op0=ALU.is_gt, op1=ALU.subtract).then_inc(digits_ready, 1)
                dve.wait_ge(digits_ready, i + 1)

            def solve(m, n):
                if n is not None:
                    taps(n, 5)
                else:
                    quant_scales()
                    digits(0)
                for h in range(2):
                    ps = four(filled("solve", m, ("kS", h)))
                    for j in range(4):
                        u = 8 * h + 2 * j + 1
                        ins = dve.scalar_tensor_tensor(out=vt[:, u, :], in0=ps[:, j, :],
                                                       scalar=negc[:, u:u + 1], in1=vt[:, u, :],
                                                       op0=ALU.mult, op1=ALU.add)
                    ins.then_inc(r_ready, 1)
                dve.wait_ge(z_ready, m * 4 + 4)
                dve.wait_ge(qe_ready, m + 1)
                for par in range(2):
                    for h in range(2):
                        mean_square(m, par, h)
                    for h in range(2):
                        gated(m, par, h)
                    if par == 0:
                        if n is not None:
                            early(n)
                        else:
                            digits(1)
                            digits(2)
                for par, name in enumerate(("out_even", "out_odd")):
                    for t in range(2):
                        ps = filled("solve", m, (name, t))[:].rearrange("p (a b) -> p a b", a=2)
                        acc = attn_out[:, 4 * t + par:4 * t + 4:2, :]
                        ins = dve.tensor_tensor(acc, ps, acc, ALU.add)
                        ins.then_inc(acc_done, 1)
                    if par == 0 and n is None:
                        fin_units(0)

            def columns():
                dve.wait_ge(colsT_filled, 1)
                dve.tensor_copy(cols_all[:].rearrange("p h q u -> p q u h"),
                                work[0][:, 0:3 * NU * NH].rearrange("p (q u h) -> p q u h", q=3, u=NU)
                                ).then_inc(colsT_ready, 1)

            dve.wait_ge(x_loaded, 16)
            layer_stats(ln_step, 0, range(NU), x_sb, 1)
            for u in range(NU):
                dve.tensor_scalar(xn_v[:, u, :], x_sb[:, u, :], mv[:, u, 0:1], rstd[:, u:u + 1],
                                  ALU.subtract, ALU.mult).then_inc(xn_ready, 1)
            for i in range(4):
                part = slice(512 * (i % 2), 512 * (i % 2) + 512)
                dve.wait_ge(xnT_ready, i + 1)
                dve.tensor_copy(xT_hi[:, i // 2, part], xnT[:, i // 2, part]).then_inc(xT_hi_ready, 1)
            dve.wait_ge(xn_ready, NU)
            for i in range(4):
                part = slice(512 * (i % 2), 512 * (i % 2) + 512)
                dve.wait_ge(xT_hi_ready, i + 1)
                dve.tensor_tensor(xT_lo[:, i // 2, part], xnT[:, i // 2, part],
                                  xT_hi[:, i // 2, part].bitcast(F32), ALU.subtract).then_inc(xT_split, 1)
            dve.wait_ge(ba_filled, 4)
            dve.wait_ge(rows_act, 4)
            for t in range(2):
                dve.tensor_scalar(sp_r[:, 512 * t:512 * t + 512], work[2 + t][0:NH, :], dtb[:, 0:1], 0.0,
                                  ALU.add, ALU.max).then_inc(rows_dve, 1)
            dve.wait_ge(rows_act, 7)
            dve.wait_ge(rows_dve, 2)
            dve.tensor_tensor(sp_r, sp_r, t1_r, ALU.add).then_inc(rows_dve, 1)
            dve.wait_ge(rows_dve, 3)
            dve.tensor_scalar(g_r, sp_r, expA[:, 0:1], -1.0, ALU.mult, ALU.mult).then_inc(rows_dve, 1)
            dve.wait_ge(rows_dve, 4)
            dve.wait_ge(consts_ready, 9)
            for u in range(NU):
                dve.tensor_tensor_scan(gc_r[:, u * P:(u + 1) * P], ones[0:NH, :], g_r[:, u * P:(u + 1) * P],
                                       0.0, ALU.mult, ALU.add).then_inc(rows_dve, 1)
            dve.wait_ge(rows_dve, 12)
            gc3 = gc_r.rearrange("p (u t) -> p u t", t=P)
            dve.tensor_tensor(dif_r.rearrange("p (u t) -> p u t", t=P),
                              gc3[:, :, P - 1:P].broadcast_to([NH, NU, P]), gc3,
                              ALU.subtract).then_inc(rows_dve, 1)
            dve.tensor_scalar(ngc_r, gc_r, -1.0, None, ALU.mult).then_inc(rows_dve, 1)
            for p in range(6):
                taps(0, p)
                if p == 1:
                    columns()
            dve.wait_ge(gc_stored, 16)
            early(0)
            rest(0)
            with dve.Fori(1, NP) as n:
                mixed(n, n - 1)
                solve(n - 1, n)
                rest(n)
            mixed(None, NP - 1)
            solve(NP - 1, None)

            fin_units(1)
            dve.tensor_tensor(half[:, 0:1], scale[:, 1:2], scale[:, 2:3], ALU.mult).then_inc(fin_step, 1)
            for i in range(4):
                part = slice(512 * (i % 2), 512 * (i % 2) + 512)
                dve.wait_ge(x2_hi_ready, i + 1)
                dve.tensor_tensor(x2T_lo[:, i // 2, part], proj[i][:], xT_hi[:, i // 2, part].bitcast(F32),
                                  ALU.subtract).then_inc(xn2T_ready, 1)

            def hidden_low(i):
                dve.wait_ge(hid_hi_ready, i + 1)
                dve.tensor_tensor(hid_lo[:, i % 4], conv[:, i % 4, :], hid_hi[:, i % 4].bitcast(F32),
                                  ALU.subtract).then_inc(hid_ready, 1)

            for i in range(2 * ET):
                dve.wait_ge(silu_up, i + 1)
                dve.tensor_tensor(conv[:, i % 4, :], proj[2 * (i % 2) + 1][:], conv[:, i % 4, :],
                                  ALU.mult).then_inc(hid_made, 1)
                if i >= 1:
                    hidden_low(i - 1)
            hidden_low(2 * ET - 1)
            y2 = attn_out
            for t in range(2):
                dve.wait_ge(down_filled, ET * (t + 1))
                dve.wait_ge(fin_step, 1 + 3 * t)
                for b in range(2):
                    ins = dve.tensor_scalar(y2[:, 4 * t + 2 * b:4 * t + 2 * b + 2, :],
                                            work[2 * t + b][:].rearrange("p (a b) -> p a b", a=2),
                                            half[:, 0:1], None, ALU.mult)
                ins.then_inc(fin_step, 1)
                dve.wait_ge(fin_step, 2 + 3 * t)
                for j in range(4):
                    ins = dve.bn_stats(stats[:, 4 * t + j, :], y2[:, 4 * t + j, :])
                ins.then_inc(fin_step, 1)
                dve.wait_ge(fin_step, 3 + 3 * t)
                for j in range(4):
                    ins = dve.bn_aggr(mv[:, 4 * t + j, :], stats[:, 4 * t + j, :])
                ins.then_inc(fin_step, 1)
                dve.wait_ge(fin_step, 4 + 3 * t)
                inverse_root(range(4 * t, 4 * t + 4), 6 + t)
                for j in range(4):
                    u = 4 * t + j
                    dve.tensor_scalar(y2[:, u, :], y2[:, u, :], mv[:, u, 0:1], rstd[:, u:u + 1],
                                      ALU.subtract, ALU.mult).then_inc(x1_step, 1)
                for j in range(4):
                    u = 4 * t + j
                    dve.wait_ge(x1_step, 12 + u + 1)
                    dve.tensor_tensor(x_sb[:, u, :], x_sb[:, u, :], y2[:, u, :], ALU.add).then_inc(fin_ready, 1)


_INS = ["L0_attn_hidden_states", "L0_attn_W_qkvz", "L0_attn_W_ba", "L0_attn_conv_weight", "L0_attn_dt_bias",
        "L0_attn_A_log", "L0_attn_norm_weight", "L0_attn_W_out", "L0_ffn_W_up", "L0_ffn_W_gate", "L0_ffn_W_down"]


def kernel(**inputs):
    import numpy as np
    import concourse.bacc as bacc
    from concourse import mybir as mb
    from concourse.bass_utils import run_bass_kernel_spmd

    nc = bacc.Bacc("TRN2", target_bir_lowering=False, num_devices=1)
    arrays, args = {}, []
    for name in _INS:
        a = np.ascontiguousarray(inputs[name])
        arrays[f"in_{name}"] = a
        args.append(nc.dram_tensor(f"in_{name}", a.shape, mb.dt.from_np(a.dtype), kind="ExternalInput").ap())
    shape = inputs[_INS[0]].shape
    out = nc.dram_tensor("out_0", shape, mb.dt.float32, kind="ExternalOutput").ap()
    sandwich(nc, *args, out)
    got = run_bass_kernel_spmd(nc, [arrays], core_ids=[0])
    return got.results[0]["out_0"]
```
